# Optimizing a Trainium2 kernel written in Bass

```python
import numpy as np
import jax
import jax.numpy as jnp

def _softmax(x, axis=-1):
    return jax.nn.softmax(x, axis=axis)

def _gelu(x):
    return jax.nn.gelu(x, approximate=True)

def _silu(x):
    return jax.nn.silu(x)

def _sigmoid(x):
    return jax.nn.sigmoid(x)

def _layernorm(x, axis=-1, eps=1e-05):
    m = jnp.mean(x, axis=axis, keepdims=True)
    v = jnp.var(x, axis=axis, keepdims=True)
    return (x - m) / jnp.sqrt(v + eps)

def _scatter_add(tgt, idx, src, axis=0):
    return tgt.at[idx].add(src)

def _segment_sum(src, seg, n):
    return jax.ops.segment_sum(src, seg, n)
kernel_name = 'mk_lm_tower_d2_tok_ids512_r4_30dbb5'

def setup_inputs(seed: int=0):
    np.random.seed(seed)
    _w = jnp.asarray

    def _rec_inputs():
        import jax
        import jax.numpy as jnp
        _rk = jax.random.key(seed)
        x = jax.random.randint(jax.random.fold_in(_rk, 1), (8, 500), 0, 15000, jnp.int32)
        fside_BS_value = -0.00455523 + 1.00028 * jax.random.normal(jax.random.fold_in(_rk, 21), (8, 500), jnp.float32)
        return (x, fside_BS_value)
    x, fside_BS_value = _rec_inputs()

    def _L0_tok_setup():
        import jax, jax.numpy as jnp
        import numpy as np
        D_TOKEN = 128
        IN_FEATURE = 500
        VOCAB = 15000
        BATCH = 32
        EPS = 1e-05

        def layer_norm(x, gamma, beta):
            mu = jnp.mean(x, axis=-1, keepdims=True)
            var = jnp.mean(jnp.square(x - mu), axis=-1, keepdims=True)
            return (x - mu) * jax.lax.rsqrt(var + EPS) * gamma + beta
        key = jax.random.key(seed)
        ks = jax.random.split(key, 8)
        inv_sqrt_d = 1.0 / np.sqrt(D_TOKEN)
        gene = jax.random.randint(ks[0], (BATCH, IN_FEATURE), 0, VOCAB, dtype=jnp.int64 if jax.config.read('jax_enable_x64') else jnp.int32)
        value = jax.random.normal(ks[1], (BATCH, IN_FEATURE), dtype=jnp.float32)
        emb_table = jax.random.normal(ks[2], (VOCAB, D_TOKEN), dtype=jnp.float32)
        w_val = jax.random.normal(ks[3], (IN_FEATURE, D_TOKEN), dtype=jnp.float32) * inv_sqrt_d
        b_val = jax.random.normal(ks[4], (IN_FEATURE, D_TOKEN), dtype=jnp.float32) * inv_sqrt_d
        gamma_g = jnp.ones((D_TOKEN,), jnp.float32)
        beta_g = jnp.zeros((D_TOKEN,), jnp.float32)
        gamma_v = jnp.ones((D_TOKEN,), jnp.float32)
        beta_v = jnp.zeros((D_TOKEN,), jnp.float32)
        return {'gene': gene, 'value': value, 'emb_table': emb_table, 'w_val': w_val, 'b_val': b_val, 'gamma_g': gamma_g, 'beta_g': beta_g, 'gamma_v': gamma_v, 'beta_v': beta_v}
    _L0_tok_all = _L0_tok_setup()
    _L0_tok_in = {k: v for k, v in _L0_tok_all.items() if k in ('emb_table', 'w_val', 'b_val', 'gamma_g', 'beta_g', 'gamma_v', 'beta_v')}
    del _L0_tok_all

    def _L0_attn_setup():
        import jax, jax.numpy as jnp
        import numpy as np
        import math
        D_MODEL = 128
        D_STATE = 64
        CHUNK = 4
        NC = D_MODEL // CHUNK
        B_SZ, L_SEQ = (8, 1024)

        def _layernorm(x, g, b, eps=1e-05):
            mu = jnp.mean(x, axis=-1, keepdims=True)
            var = jnp.mean((x - mu) ** 2, axis=-1, keepdims=True)
            return (x - mu) * jax.lax.rsqrt(var + eps) * g + b
        key = jax.random.key(seed)
        ks = jax.random.split(key, 10)
        x = jax.random.normal(ks[0], (B_SZ, L_SEQ, D_MODEL), dtype=jnp.float32)
        ln_gamma = jnp.ones((D_MODEL,), jnp.float32)
        ln_beta = jnp.zeros((D_MODEL,), jnp.float32)
        Win = jax.random.normal(ks[1], (D_MODEL, D_MODEL), jnp.float32) / math.sqrt(D_MODEL)
        bin_ = jnp.zeros((D_MODEL,), jnp.float32)
        Wout = jax.random.normal(ks[2], (D_MODEL, D_MODEL), jnp.float32) / math.sqrt(D_MODEL)
        bout = jnp.zeros((D_MODEL,), jnp.float32)
        Lambda_re = -0.5 * jnp.ones((NC, D_STATE), jnp.float32)
        Lambda_im = jnp.broadcast_to(jnp.arange(D_STATE, dtype=jnp.float32) * 2.0 * math.pi / D_STATE, (NC, D_STATE))
        Bmat = jax.random.normal(ks[3], (NC, D_STATE), jnp.float32)
        C_re = jax.random.normal(ks[4], (NC, D_STATE), jnp.float32)
        C_im = jax.random.normal(ks[5], (NC, D_STATE), jnp.float32)
        Dvec = jax.random.normal(ks[6], (NC,), jnp.float32)
        return {'x': x, 'ln_gamma': ln_gamma, 'ln_beta': ln_beta, 'Win': Win, 'bin_': bin_, 'Wout': Wout, 'bout': bout, 'Lambda_re': Lambda_re, 'Lambda_im': Lambda_im, 'Bmat': Bmat, 'C_re': C_re, 'C_im': C_im, 'Dvec': Dvec}
    _L0_attn_all = _L0_attn_setup()
    _L0_attn_in = {k: v for k, v in _L0_attn_all.items() if k in ('ln_gamma', 'ln_beta', 'Win', 'bin_', 'Wout', 'bout', 'Lambda_re', 'Lambda_im', 'Bmat', 'C_re', 'C_im', 'Dvec')}
    del _L0_attn_all

    def _L0_ffn_setup():
        import jax, jax.numpy as jnp
        import numpy as np
        B, T, D, F, E, K = (8, 256, 128, 512, 8, 2)

        def _moe_forward(x, Wr, br, W1, b1, W2, b2):
            Bx, Tx, Dx = x.shape
            xf = x.reshape(-1, Dx)
            logits = xf @ Wr + br
            probs = jax.nn.softmax(logits, axis=-1)
            vals, idx = jax.lax.top_k(probs, K)
            cw = (jax.nn.one_hot(idx, E, dtype=x.dtype) * vals[..., None]).sum(axis=1)

            def body(acc, params):
                W1e, b1e, W2e, b2e, cwe = params
                h = jax.nn.relu(xf @ W1e + b1e)
                y = h @ W2e + b2e
                return (acc + cwe[:, None] * y, None)
            out, _ = jax.lax.scan(body, jnp.zeros_like(xf), (W1, b1, W2, b2, cw.T))
            return out.reshape(Bx, Tx, Dx)
        key = jax.random.key(seed)
        k0, k1, k2, k3 = jax.random.split(key, 4)
        s_d = 1.0 / np.sqrt(D)
        s_f = 1.0 / np.sqrt(F)
        return {'x': jax.random.normal(k0, (B, T, D), jnp.float32), 'Wr': jax.random.uniform(k1, (D, E), jnp.float32, -s_d, s_d), 'br': jnp.zeros((E,), jnp.float32), 'W1': jax.random.uniform(k2, (E, D, F), jnp.float32, -s_d, s_d), 'b1': jnp.zeros((E, F), jnp.float32), 'W2': jax.random.uniform(k3, (E, F, D), jnp.float32, -s_f, s_f), 'b2': jnp.zeros((E, D), jnp.float32)}
    _L0_ffn_all = _L0_ffn_setup()
    _L0_ffn_in = {k: v for k, v in _L0_ffn_all.items() if k in ('Wr', 'br', 'W1', 'b1', 'W2', 'b2')}
    del _L0_ffn_all

    def _L1_attn_setup():
        import jax, jax.numpy as jnp
        import numpy as np
        import math
        D_MODEL = 128
        N_HEADS = 8
        FACTOR = 5
        B, L = (2, 512)
        key = jax.random.key(seed)
        ks = jax.random.split(key, 10)
        s = 1.0 / math.sqrt(D_MODEL)
        inp = {'x': jax.random.normal(ks[0], (B, L, D_MODEL), dtype=jnp.float32), 'samp_idx': jax.random.randint(ks[1], (FACTOR * L,), 0, L), 'Wq': jax.random.normal(ks[2], (D_MODEL, D_MODEL), dtype=jnp.float32) * s, 'bq': jnp.zeros((D_MODEL,), dtype=jnp.float32), 'Wk': jax.random.normal(ks[3], (D_MODEL, D_MODEL), dtype=jnp.float32) * s, 'bk': jnp.zeros((D_MODEL,), dtype=jnp.float32), 'Wv': jax.random.normal(ks[4], (D_MODEL, D_MODEL), dtype=jnp.float32) * s, 'bv': jnp.zeros((D_MODEL,), dtype=jnp.float32), 'Wo': jax.random.normal(ks[5], (D_MODEL, D_MODEL), dtype=jnp.float32) * s, 'bo': jnp.zeros((D_MODEL,), dtype=jnp.float32)}
        return inp
    _L1_attn_all = _L1_attn_setup()
    _L1_attn_in = {k: v for k, v in _L1_attn_all.items() if k in ('Wq', 'bq', 'Wk', 'bk', 'Wv', 'bv', 'Wo', 'bo', 'samp_idx')}
    del _L1_attn_all

    def _L1_ffn_setup():
        import jax, jax.numpy as jnp
        import numpy as np
        D_MODEL, N_GROUPS, N_EXPERTS = (128, 8, 8)
        TOP_K_L1, TOP_K_L2 = (2, 2)
        BATCH, SEQ = (2, 128)
        key = jax.random.key(seed)
        ks = jax.random.split(key, 6)
        d, G, E = (D_MODEL, N_GROUPS, N_EXPERTS)
        scale = 0.02
        x = jax.random.normal(ks[0], (BATCH, SEQ, d), dtype=jnp.float32)
        g1 = jax.random.normal(ks[1], (d, G), dtype=jnp.float32) * scale
        g2 = jax.random.normal(ks[2], (G, d, E), dtype=jnp.float32) * scale
        W1 = jax.random.normal(ks[3], (G, E, d, 2 * d), dtype=jnp.float32) * scale
        b1 = jnp.zeros((G, E, 2 * d), dtype=jnp.float32)
        W2 = jax.random.normal(ks[4], (G, E, 2 * d, d), dtype=jnp.float32) * scale
        b2 = jnp.zeros((G, E, d), dtype=jnp.float32)
        return {'x': x, 'g1': g1, 'g2': g2, 'W1': W1, 'b1': b1, 'W2': W2, 'b2': b2}
    _L1_ffn_all = _L1_ffn_setup()
    _L1_ffn_in = {k: v for k, v in _L1_ffn_all.items() if k in ('g1', 'g2', 'W1', 'b1', 'W2', 'b2')}
    del _L1_ffn_all
    return {'x': x, 'fside_BS_value': fside_BS_value, 'L0_tok_emb_table': _L0_tok_in['emb_table'], 'L0_tok_w_val': _L0_tok_in['w_val'], 'L0_tok_b_val': _L0_tok_in['b_val'], 'L0_tok_gamma_g': _L0_tok_in['gamma_g'], 'L0_tok_beta_g': _L0_tok_in['beta_g'], 'L0_tok_gamma_v': _L0_tok_in['gamma_v'], 'L0_tok_beta_v': _L0_tok_in['beta_v'], 'L0_attn_ln_gamma': _L0_attn_in['ln_gamma'], 'L0_attn_ln_beta': _L0_attn_in['ln_beta'], 'L0_attn_Win': _L0_attn_in['Win'], 'L0_attn_bin_': _L0_attn_in['bin_'], 'L0_attn_Wout': _L0_attn_in['Wout'], 'L0_attn_bout': _L0_attn_in['bout'], 'L0_attn_Lambda_re': _L0_attn_in['Lambda_re'], 'L0_attn_Lambda_im': _L0_attn_in['Lambda_im'], 'L0_attn_Bmat': _L0_attn_in['Bmat'], 'L0_attn_C_re': _L0_attn_in['C_re'], 'L0_attn_C_im': _L0_attn_in['C_im'], 'L0_attn_Dvec': _L0_attn_in['Dvec'], 'L0_ffn_Wr': _L0_ffn_in['Wr'], 'L0_ffn_br': _L0_ffn_in['br'], 'L0_ffn_W1': _L0_ffn_in['W1'], 'L0_ffn_b1': _L0_ffn_in['b1'], 'L0_ffn_W2': _L0_ffn_in['W2'], 'L0_ffn_b2': _L0_ffn_in['b2'], 'L1_attn_Wq': _L1_attn_in['Wq'], 'L1_attn_bq': _L1_attn_in['bq'], 'L1_attn_Wk': _L1_attn_in['Wk'], 'L1_attn_bk': _L1_attn_in['bk'], 'L1_attn_Wv': _L1_attn_in['Wv'], 'L1_attn_bv': _L1_attn_in['bv'], 'L1_attn_Wo': _L1_attn_in['Wo'], 'L1_attn_bo': _L1_attn_in['bo'], 'L1_attn_samp_idx': _L1_attn_in['samp_idx'], 'L1_ffn_g1': _L1_ffn_in['g1'], 'L1_ffn_g2': _L1_ffn_in['g2'], 'L1_ffn_W1': _L1_ffn_in['W1'], 'L1_ffn_b1': _L1_ffn_in['b1'], 'L1_ffn_W2': _L1_ffn_in['W2'], 'L1_ffn_b2': _L1_ffn_in['b2']}

def reference(x, fside_BS_value, L0_tok_emb_table, L0_tok_w_val, L0_tok_b_val, L0_tok_gamma_g, L0_tok_beta_g, L0_tok_gamma_v, L0_tok_beta_v, L0_attn_ln_gamma, L0_attn_ln_beta, L0_attn_Win, L0_attn_bin_, L0_attn_Wout, L0_attn_bout, L0_attn_Lambda_re, L0_attn_Lambda_im, L0_attn_Bmat, L0_attn_C_re, L0_attn_C_im, L0_attn_Dvec, L0_ffn_Wr, L0_ffn_br, L0_ffn_W1, L0_ffn_b1, L0_ffn_W2, L0_ffn_b2, L1_attn_Wq, L1_attn_bq, L1_attn_Wk, L1_attn_bk, L1_attn_Wv, L1_attn_bv, L1_attn_Wo, L1_attn_bo, L1_attn_samp_idx, L1_ffn_g1, L1_ffn_g2, L1_ffn_W1, L1_ffn_b1, L1_ffn_W2, L1_ffn_b2):
    import jax
    import jax.numpy as jnp

    def _L0_tok_ref(gene, value, emb_table, w_val, b_val, gamma_g, beta_g, gamma_v, beta_v):
        import jax, jax.numpy as jnp
        import numpy as np
        D_TOKEN = 128
        IN_FEATURE = 500
        VOCAB = 15000
        BATCH = 32
        EPS = 1e-05

        def layer_norm(x, gamma, beta):
            mu = jnp.mean(x, axis=-1, keepdims=True)
            var = jnp.mean(jnp.square(x - mu), axis=-1, keepdims=True)
            return (x - mu) * jax.lax.rsqrt(var + EPS) * gamma + beta
        g = emb_table[gene]
        g = layer_norm(g, gamma_g, beta_g)
        v = w_val[None] * value[..., None] + b_val[None]
        v = layer_norm(v, gamma_v, beta_v)
        return g + v

    def _L0_attn_ref(x, ln_gamma, ln_beta, Win, bin_, Wout, bout, Lambda_re, Lambda_im, Bmat, C_re, C_im, Dvec):
        import jax, jax.numpy as jnp
        import numpy as np
        import math
        D_MODEL = 128
        D_STATE = 64
        CHUNK = 4
        NC = D_MODEL // CHUNK
        B_SZ, L_SEQ = (8, 1024)

        def _layernorm(x, g, b, eps=1e-05):
            mu = jnp.mean(x, axis=-1, keepdims=True)
            var = jnp.mean((x - mu) ** 2, axis=-1, keepdims=True)
            return (x - mu) * jax.lax.rsqrt(var + eps) * g + b
        Bsz, L, Dm = x.shape
        nc, n = Lambda_re.shape
        cs = Dm // nc
        z = _layernorm(x, ln_gamma, ln_beta)
        z = z @ Win + bin_
        omega = jnp.arange(L, dtype=jnp.float32)
        Lam = Lambda_re + 1j * Lambda_im
        expo = jnp.exp(Lam[:, :, None] * omega[None, None])
        CB = (C_re + 1j * C_im) * Bmat
        k = jnp.real(jnp.einsum('cn,cnl->cl', CB, expo))
        k2 = jnp.concatenate([k, k[:, ::-1]], axis=1)
        kf = jnp.fft.rfft(k2, n=2 * L, axis=1)
        u = z.reshape(Bsz, L, nc, cs)
        uf = jnp.fft.rfft(u, n=2 * L, axis=1)
        yf = uf * kf.T[None, :, :, None]
        y = jnp.fft.irfft(yf, n=2 * L, axis=1)[:, :L]
        y = y + u * Dvec[None, None, :, None]
        y = y.reshape(Bsz, L, Dm)
        y = y @ Wout + bout
        y = jax.nn.gelu(y, approximate=False)
        return x + y

    def _L0_ffn_ref(x, Wr, br, W1, b1, W2, b2):
        import jax, jax.numpy as jnp
        import numpy as np
        B, T, D, F, E, K = (8, 256, 128, 512, 8, 2)

        def _moe_forward(x, Wr, br, W1, b1, W2, b2):
            Bx, Tx, Dx = x.shape
            xf = x.reshape(-1, Dx)
            logits = xf @ Wr + br
            probs = jax.nn.softmax(logits, axis=-1)
            vals, idx = jax.lax.top_k(probs, K)
            cw = (jax.nn.one_hot(idx, E, dtype=x.dtype) * vals[..., None]).sum(axis=1)

            def body(acc, params):
                W1e, b1e, W2e, b2e, cwe = params
                h = jax.nn.relu(xf @ W1e + b1e)
                y = h @ W2e + b2e
                return (acc + cwe[:, None] * y, None)
            out, _ = jax.lax.scan(body, jnp.zeros_like(xf), (W1, b1, W2, b2, cw.T))
            return out.reshape(Bx, Tx, Dx)
        return _moe_forward(x, Wr, br, W1, b1, W2, b2)

    def _L1_attn_ref(x, Wq, bq, Wk, bk, Wv, bv, Wo, bo, samp_idx):
        import jax, jax.numpy as jnp
        import numpy as np
        import math
        D_MODEL = 128
        N_HEADS = 8
        FACTOR = 5
        B, L = (2, 512)
        B_, L_, D = x.shape
        H = N_HEADS
        dk = D // H
        scale = 1.0 / math.sqrt(dk)

        def proj(W, b):
            y = jnp.einsum('bld,ed->ble', x, W) + b
            return y.reshape(B_, L_, H, dk).transpose(0, 2, 1, 3)
        q = proj(Wq, bq)
        k = proj(Wk, bk)
        v = proj(Wv, bv)
        K_sample = k[:, :, samp_idx, :]
        QKs = jnp.einsum('bhle,bhse->bhls', q, K_sample) * scale
        M = QKs.max(-1) - QKs.mean(-1)
        U = jnp.argmax(M, axis=-1)
        q_red = jnp.take_along_axis(q, U[:, :, None, None], axis=2)
        scores = jnp.einsum('bhle,bhse->bhls', q_red, k) * scale
        attn = jax.nn.softmax(scores, axis=-1)
        context = jnp.einsum('bhls,bhse->bhle', attn, v)
        context = jnp.broadcast_to(context, (B_, H, L_, dk))
        context = context.transpose(0, 2, 1, 3).reshape(B_, L_, D)
        return jnp.einsum('bld,ed->ble', context, Wo) + bo

    def _L1_ffn_ref(x, g1, g2, W1, b1, W2, b2):
        import jax, jax.numpy as jnp
        import numpy as np
        D_MODEL, N_GROUPS, N_EXPERTS = (128, 8, 8)
        TOP_K_L1, TOP_K_L2 = (2, 2)
        BATCH, SEQ = (2, 128)
        B, S, d = x.shape
        G, E = (g1.shape[1], g2.shape[2])
        xt = x.reshape(-1, d)
        logits1 = xt @ g1
        v1, i1 = jax.lax.top_k(logits1, TOP_K_L1)
        w1 = jax.nn.softmax(v1.astype(jnp.float32), axis=-1).astype(x.dtype)
        c1 = jnp.sum(jax.nn.one_hot(i1, G, dtype=x.dtype) * w1[..., None], axis=1)
        logits2 = jnp.einsum('td,gde->tge', xt, g2)
        v2, i2 = jax.lax.top_k(logits2, TOP_K_L2)
        w2 = jax.nn.softmax(v2.astype(jnp.float32), axis=-1).astype(x.dtype)
        c2 = jnp.sum(jax.nn.one_hot(i2, E, dtype=x.dtype) * w2[..., None], axis=2)
        h = jax.nn.relu(jnp.einsum('td,gedh->tgeh', xt, W1) + b1)
        y = jnp.einsum('tgeh,gehd->tged', h, W2) + b2
        group_out = jnp.einsum('tged,tge->tgd', y, c2)
        out = jnp.einsum('tgd,tg->td', group_out, c1)
        return out.reshape(B, S, d)
    h = _L0_tok_ref(x, fside_BS_value, L0_tok_emb_table, L0_tok_w_val, L0_tok_b_val, L0_tok_gamma_g, L0_tok_beta_g, L0_tok_gamma_v, L0_tok_beta_v)
    h = h + _L0_attn_ref(_layernorm(h, axis=-1), L0_attn_ln_gamma, L0_attn_ln_beta, L0_attn_Win, L0_attn_bin_, L0_attn_Wout, L0_attn_bout, L0_attn_Lambda_re, L0_attn_Lambda_im, L0_attn_Bmat, L0_attn_C_re, L0_attn_C_im, L0_attn_Dvec)
    h = h + _L0_ffn_ref(_layernorm(h, axis=-1), L0_ffn_Wr, L0_ffn_br, L0_ffn_W1, L0_ffn_b1, L0_ffn_W2, L0_ffn_b2)
    h = h + _L1_attn_ref(_layernorm(h, axis=-1), L1_attn_Wq, L1_attn_bq, L1_attn_Wk, L1_attn_bk, L1_attn_Wv, L1_attn_bv, L1_attn_Wo, L1_attn_bo, L1_attn_samp_idx)
    h = h + _L1_ffn_ref(_layernorm(h, axis=-1), L1_ffn_g1, L1_ffn_g2, L1_ffn_W1, L1_ffn_b1, L1_ffn_W2, L1_ffn_b2)
    return h

_drawn_inputs = setup_inputs


def setup_inputs(seed=0):
    import zlib

    import numpy as np

    out = dict(_drawn_inputs(seed))
    spreads = {'L0_tok_gamma_g': (1.0, 0.2),
     'L0_tok_beta_g': (0.0, 0.1),
     'L0_tok_gamma_v': (1.0, 0.2),
     'L0_tok_beta_v': (0.0, 0.1),
     'L0_attn_ln_gamma': (1.0, 0.2),
     'L0_attn_ln_beta': (0.0, 0.1),
     'L0_attn_bin_': (0.0, 0.1),
     'L0_attn_bout': (0.0, 0.8),
     'L0_attn_Lambda_re': (-0.5, 0.2),
     'L0_ffn_br': (0.0, 0.8),
     'L0_ffn_b1': (0.0, 0.8),
     'L0_ffn_b2': (0.0, 0.8),
     'L1_attn_bq': (0.0, 0.38),
     'L1_attn_bk': (0.0, 0.8),
     'L1_attn_bv': (0.0, 0.724),
     'L1_attn_bo': (0.0, 0.8),
     'L1_ffn_b1': (0.0, 0.8),
     'L1_ffn_b2': (0.0, 0.8)}
    factors = {'L0_ffn_Wr': 5.7,
     'L0_ffn_W1': 6.353,
     'L0_ffn_W2': 5.862,
     'L1_ffn_g1': 8.0,
     'L1_ffn_g2': 8.0,
     'L1_ffn_W1': 8.0,
     'L1_ffn_W2': 8.0}
    for name, (base, spread) in spreads.items():
        noise = np.random.default_rng([zlib.crc32(name.encode()), seed]).standard_normal(out[name].shape)
        drawn = base * np.exp(spread * noise) if base else spread * noise
        out[name] = jnp.asarray(drawn.astype(out[name].dtype))
    for name, factor in factors.items():
        out[name] = (out[name] * factor).astype(out[name].dtype)
    return out
```

```python
from contextlib import ExitStack
import math

import concourse.bass as bass
from concourse import mybir

F32 = mybir.dt.float32
BF16 = mybir.dt.bfloat16
I32 = mybir.dt.int32
U32 = mybir.dt.uint32
ALU = mybir.AluOpType
ACT = mybir.ActivationFunctionType
AX = mybir.AxisListType

D = 128
B, L = 8, 500
R = 125
J = L // R
NT = B * J
NC, NS, CS = 32, 64, 4
KA, KB = 16, 32
KROW = 1024
GM = L + (J - 1) * R
EPS = 1e-5
MAGIC = 1.5 * 2.0 ** 23
H, DK, NSAMP = 8, 16, 2560


class Ffn:

    def __init__(self, n, groups, experts, picks, hidden, wide, w1, b1, w2, b2):
        self.n, self.G, self.E, self.K = n, groups, groups * experts, picks
        self.HC = hidden // 128
        self.wide = wide
        self.names = w1, b1, w2, b2
        full = (NT * R * picks + 127 * self.E) // 128
        self.tiles = -(-full // U) * U
        self.banks = self.E * NT // 512 or 1
        self.wcols = hidden + self.HC
        self.w1_at = 0 if n else W0_AT
        self.w2_at = self.w1_at + self.E * self.wcols


U = 4
W0_AT = 24576
FFN = [Ffn(0, 1, 8, 2, 512, 8, "L0_ffn_W1", "L0_ffn_b1", "L0_ffn_W2", "L0_ffn_b2"),
       Ffn(1, 8, 8, 4, 256, 72, "L1_ffn_W1", "L1_ffn_b1", "L1_ffn_W2", "L1_ffn_b2")]
BIGC = FFN[1].w2_at + FFN[1].E * 256
TAB = FFN[1].tiles + U


def ap(t, offset, dims):
    return bass.AP(tensor=t, offset=offset, ap=[list(d) for d in dims])


class Steps:

    def __init__(self, eng, sem):
        self.eng, self.sem, self.n = eng, sem, 0

    def did(self, instruction):
        self.n += 1
        instruction.then_inc(self.sem, 1)
        return self.n

    def then(self, instruction):
        self.did(instruction)
        self.settle()

    def settle(self):
        self.eng.wait_ge(self.sem, self.n)


def bank_plan():
    plan = [("tokens", 0, "dve"), ("ssm", 0, "dve")]
    plan += [("lags", i, "dve") for i in range(4)] + [("zbias", 0, "dve")]
    plan += [("xT", b, "act") for b in range(B)] + [("z", b, "dve") for b in range(B)]
    for g in range(9):
        if g < 8:
            plan += [("conv", g, "act")]
        if g > 0:
            plan += [("convT", g - 1, "dve")]
    plan += [("yT", b, "act" if b % 2 else "dve") for b in range(B)] + [("out0", b, "act") for b in range(B)]
    for f in (0, 1):
        plan += [(f"b1T{f}", 0, "dve")] + [(f"rT{f}", b, "act") for b in range(B)] + [(f"router{f}", b, "dve") for b in range(B)]
        plan += [(f"count{f}", 0, "dve")] + [(f"rank{f}", i, "dve") for i in range(FFN[f].banks)]
        plan += [(f"ends{f}", 0, "dve"), (f"expert{f}", 0, "dve")]
        for b in range(B):
            plan += [(f"cT{f}", b, "act"), (f"bias{f}", b, "dve")]
        if f == 0:
            plan += [("wT", 0, "dve"), ("cols", 0, "dve"), ("cnt", 0, "dve"), ("cntrow", 0, "dve")]
            plan += [("aT", b, "act") for b in range(B)] + [("xbar", 0, "dve"), ("kbar", 0, "dve")]
            plan += [("skip", i, "dve") for i in range(-len(plan) % 4)]
            plan += [("qk", i, "act") for i in range(4)]
            for b in range(B):
                plan += [("score", 4 * (8 * b + i) + k, "dve") for i in range(4) for k in range(4)]
                if b < B - 1:
                    plan += [("qk", 4 * b + 4 + i, "act") for i in range(4)]
                plan += [("score", 4 * (8 * b + i) + k, "dve") for i in range(4, 8) for k in range(4)]
            plan += [(w, 0, "dve") for w in ("MT", "hotT", "xsel", "qsel", "u")] + [("ss", 0, "act")]
            plan += [(w, 0, "dve") for w in ("attT", "xa", "ctx")] + [("outa", i, "dve") for i in range(2)]
    return plan


def tower_kernel(nc, a, out):
    plan = bank_plan()
    at, evacs, nth, nfill = {}, {"act": 0, "dve": 0}, [], []
    for n, (what, i, eng) in enumerate(plan):
        whole = what != "skip" and (what != "score" or i % 4 == 3)
        evacs[eng] += whole
        nth.append(evacs[eng] + (what == "score" and not whole))
        nfill.append((nfill[-1] if nfill else 0) + whole)
        at[what, i] = n

    with ExitStack() as ctx:
        sems = {}

        def S(name):
            if name not in sems:
                sems[name] = ctx.enter_context(nc.semaphore(name))
            return sems[name]

        def sb(name, shape, dt=F32):
            return ctx.enter_context(nc.sbuf_tensor(name, shape, dt))

        slots = nc.dram_tensor("slots", (TAB * 128, D), F32)
        results = [nc.dram_tensor(f"results{c.n}", (c.tiles * 128, D), F32) for c in FFN]
        kappa = nc.dram_tensor("kappa", (NC, KROW), F32)

        ps = ctx.enter_context(nc.psum_tensor("ps", [128, 8, 512], F32))
        big = sb("big", [128, BIGC])
        h = sb("h", [R, NT, D])
        xbuf = sb("xbuf", [128, NT * D])
        x = xbuf[0:R, :].rearrange("p (t d) -> p t d", t=NT)
        tbuf = sb("tbuf", [128, NT * D])
        zbuf = sb("zbuf", [128, NT * D])
        xT = tbuf[:, 0:NT * R].rearrange("p (t r) -> p t r", t=NT)
        gw = tbuf[0:R, :].rearrange("p (t d) -> p t d", t=NT)
        vw = zbuf[0:R, :].rearrange("p (t d) -> p t d", t=NT)
        z = zbuf[0:R, :].rearrange("p (j c b r) -> p j c b r", j=J, c=NC, b=B)
        yT = zbuf[:, 0:NT * R].rearrange("p (t r) -> p t r", t=NT)
        cst = sb("cst", [128, 640])
        ident = cst[:, 0:128]
        G = big[:, 0:NC * GM].rearrange("p (c m) -> p c m", c=NC)
        wv = big[0:R, 0:512].rearrange("p (j d) -> p j d", j=J)
        bv = big[0:R, 512:1024].rearrange("p (j d) -> p j d", j=J)

        early = big[:, 12288:14336]
        ids32 = early[0:NT, 0:R].bitcast(I32)
        ids32f = early[0:NT, 128:128 + R]
        val32 = early[0:NT, 256:256 + R]
        idsT = sb("idsT", [R, NT], I32)
        valT = sb("valT", [R, NT])
        aside = big[:, NC * GM + 160:NC * GM + 1760]
        rows = aside[0:R, 0:5 * D].rearrange("p (q d) -> p q d", q=5)
        wsm = aside[:, 7 * D:9 * D].rearrange("p (q d) -> p q d", q=2)
        lnc = sb("lnc", [128, 4])
        rowv = aside[0:1, 9 * D:12 * D].rearrange("p (q d) -> p q d", q=3)
        ones = sb("ones", [128, 128])
        bnst = sb("bnst", [R, NT, 6])
        mv = sb("mv", [R, NT, 2])
        rs = sb("rs", [R, NT])
        rs2 = sb("rs2", [R, NT])
        ssm5 = early[0:NC, 384:384 + 10 * NS].rearrange("c (q r n) -> c q r n", q=5, r=2)
        dskip = sb("dskip", [KA, NC])
        sp5 = early[:, 1024:1024 + 5 * NC].rearrange("p (q c) -> p q c", q=5)
        cc = early[:, 1184:1184 + 2 * NC].rearrange("p (q c) -> p q c", q=2)
        alpha = sb("alpha", [128, 4])
        itI = sb("itI", [128, KA + KB], I32)
        itF = sb("itF", [128, KA + KB])
        NPH = 2 * NC * KA + NC * KB
        scr = big[:, 1024:1024 + 3 * NPH]
        ph, qn, mg = scr[:, 0:NPH], scr[:, NPH:2 * NPH], scr[:, 2 * NPH:3 * NPH]
        e1 = big[:, 7168:7168 + NC * KA].rearrange("p (c l) -> p c l", c=NC)
        e1r = big[:, 11776:11776 + NC * KA].rearrange("p (c l) -> p c l", c=NC)
        e2 = big[:, 7680:7680 + 2 * NC * KB].rearrange("p (c l) -> p c l", c=NC)
        kk = big[0:KA, 9728:9728 + 2 * NC * KB].rearrange("p (c l) -> p c l", c=NC)
        ltri = sb("ltri", [128, 2, 128], BF16)
        onesb = sb("onesb", [128, 128], BF16)
        tileno = sb("tileno", [64, TAB])
        em8I = sb("em8I", [R, 8], I32)
        em8 = sb("em8", [R, 8])
        wr = sb("wr", [128, 2, 72])
        brow = sb("brow", [1, 8])
        b2 = sb("b2", [64, 2, D])
        b1r = sb("b1r", [128, 2, 128])
        table = [sb(f"table{f}", [1, TAB], I32) for f in (0, 1)]
        place = [sb(f"place{f}", [R, 4, NT], I32) for f in (0, 1)]
        gate = [sb(f"gate{f}", [R, 4, NT]) for f in (0, 1)]
        sm = sb("sm", [R, 12, NT])
        ntile = sb("ntile", [R, 3, 64])
        ncol = sb("ncol", [64, 2])
        ncolb = sb("ncolb", [64, 1], BF16)
        bbt = aside[0:R, 6 * D:7 * D]
        y = gw
        ys = xbuf[:, 0:8 * 512].rearrange("p (g t) -> p g t", g=8)
        wg = aside[:, 5 * D:6 * D]

        got = [tbuf[0:R, D * n:D * n + D] for n in range(8)]

        def mask_views(f):
            c = FFN[f]
            m = c.E * NT
            v = {}
            if f == 0:
                free, o = zbuf[0:R, :], 0
            else:
                free, o = big[0:R, W0_AT:W0_AT + 8192], 0
            def take(name, n, dt=F32):
                nonlocal o
                w = n if dt == F32 else n // 2
                t = free[:, o:o + w]
                v[name] = t if dt == F32 else t.bitcast(dt)
                o += w
            for name in ("members", "upto", "before", "chain"):
                take(name, m, BF16)
            take("lg", 256)
            take("rest", 512)
            for name in ("oh1", "oh2", "eh1", "eh2", "pick"):
                take(name, 512)
            if f == 0:
                v["slot"], v["gates"], v["tmp"] = (tbuf[0:R, 256 * n:256 * n + 256] for n in range(3))
            else:
                v["le"], v["tmp"] = zbuf[0:R, 0:2048], zbuf[0:R, 2048:4096]
                v["slot"], v["gates"] = tbuf[0:R, 0:2048], tbuf[0:R, 2048:4096]
            return v
        cT = cst[0:64, 128:128 + L]

        tail = big[:, W0_AT:W0_AT + 8192]
        tail_at = 0

        def take(n, rows_=128):
            nonlocal tail_at
            t = tail[0:rows_, tail_at:tail_at + n]
            tail_at += n
            return t
        azero = tail[:, 0:1808]
        wqT = take(256).rearrange("p (s m) -> p s m", s=2)
        wkT = take(256).rearrange("p (s m) -> p s m", s=2)
        wkn = take(256).rearrange("p (s d) -> p s d", s=2)
        brow2 = take(512, 1).rearrange("p (w s m) -> p w s m", w=2, s=2)
        uz = take(512)
        own = take(16).rearrange("p (s h) -> p s h", s=2)
        wvT, woT = take(128), take(128)
        wraw = take(512).rearrange("p (w d) -> p w d", w=4)
        borow = take(256, 1).rearrange("p (w d) -> p w d", w=2)
        own16 = take(8)
        bcol = take(5)
        kcol = take(16).rearrange("p (s b) -> p s b", s=2)
        sidx = take(20)
        sidf, shi, slo = take(20), take(20), take(20)
        i500 = take(500)
        hot_lo = zbuf[:, 2640:3920].bitcast(BF16)[:, 0:20 * R].rearrange("p (s l) -> p s l", s=20)
        hot_hi = take(40).bitcast(BF16).rearrange("p (s l) -> p s l", s=20)
        cnt = take(J, R)
        maskrow = take(250, 1).bitcast(BF16)
        selrow = take(64, 1).bitcast(BF16)
        xbar = take(B)
        qs = take(2000).rearrange("p (o s t) -> p o s t", o=2, s=2)
        ks = take(2000).rearrange("p (o s t) -> p o s t", o=2, s=2)
        mcol = zbuf[0:R, 0:256].rearrange("p (j n) -> p j n", j=J)
        mrow = zbuf[0:64, 256:256 + L]
        hot = zbuf[0:64, 768:768 + L]
        hotT = zbuf[0:R, 1280:1280 + 256].rearrange("p (j n) -> p j n", j=J)
        xsel = zbuf[:, 1536:1600]
        qsel = zbuf[:, 1600:1728].rearrange("p (s n) -> p s n", s=2)
        att = zbuf[0:64, 1728:1728 + L]
        attT = zbuf[0:R, 2240:2240 + 256].rearrange("p (j n) -> p j n", j=J)
        xa = zbuf[:, 2496:2560]
        cmul, ctxv = zbuf[:, 2560:2624], zbuf[:, 2624:2632]
        ctxb = zbuf[:, 2632:2632 + B * R].rearrange("p (b r) -> p b r", b=B)
        m8 = zbuf[0:64, 3640:3648]
        i8 = zbuf[0:64, 3648:3656].bitcast(U32)
        i8f = zbuf[0:64, 3656:3657]
        nmx, asum = zbuf[0:64, 3660:3661], zbuf[0:64, 3661:3662]
        SCALE = 1.0 / math.sqrt(DK)

        class Ring:
            def __init__(self, c):
                o = 0
                def take(n, w):
                    nonlocal o
                    r = [zbuf[:, o + w * i:o + w * i + w] for i in range(n)]
                    o += n * w
                    return r
                self.rows, self.rT, self.w1 = take(U, 128), take(2, 128), take(2, c.wcols)
                self.hid, self.res = take(2, 128 * c.HC), take(U, 128)

        block = ctx.enter_context(nc.Block())

        def bank(n):
            return ps[:, n % 8, :]

        def wait_bank(eng, what, i=0):
            eng.wait_ge(S("bank_filled"), nfill[at[what, i]])

        def wait_evac(eng, what, i=0):
            n = at[what, i]
            eng.wait_ge(S("emptied_" + plan[n][2]), nth[n])

        def load_weights(eng, c):
            w1, b1, w2, _ = c.names
            g = "g e" if c.n else "e"
            src = a[w1].rearrange("g e d h -> (g e) d h") if c.n else a[w1]
            src2 = a[w2].rearrange("g e h d -> (g e) h d") if c.n else a[w2]
            w1v = big[:, c.w1_at:c.w1_at + c.E * c.wcols].rearrange("p (e w) -> p e w", e=c.E)
            w2v = big[:, c.w2_at:c.w2_at + c.E * c.HC * D].rearrange("p (e k d) -> p e k d", e=c.E, k=c.HC)
            hid = 128 * c.HC
            step = 8 if c.n else 4
            late = 32 if c.n else c.E
            for e in range(0, c.E, step):
                eng.dma_start(w1v[:, e:e + step, 0:hid], src[e:e + step].rearrange("e d h -> d e h")).then_inc(S(f"w{c.n}_ld"), 16)
                if e + step <= late - 8 or not c.n:
                    for i in range(e, e + step):
                        eng.dma_start(w2v[:, i], src2[i].rearrange("(k h) d -> h k d", k=c.HC)).then_inc(S(f"w{c.n}_ld"), 16)

        def rows_of(t, tau):
            return t[:, :].rearrange("(n p) d -> n p d", p=128)[bass.ds(tau, 1)].rearrange("n p d -> p (n d)")

        def weight_loads(c):
            return c.E // (8 if c.n else 4) + (24 if c.n else 8)

        def expert_dma(sp, c):
            p, ring = f"f{c.n}_", Ring(c)
            if c.n:
                sp.wait_ge(S("f1_placed"), 1)
                w2v = big[:, c.w2_at:c.w2_at + c.E * c.HC * D].rearrange("p (e k d) -> p e k d", e=c.E, k=c.HC)
                src2 = a[c.names[2]].rearrange("g e h d -> (g e) h d")
                for i in range(24, c.E):
                    sp.dma_start(w2v[:, i], src2[i].rearrange("(k h) d -> h k d", k=c.HC)).then_inc(S("w1_late"), 16)

            sp.wait_ge(S(p + "scattered"), 16 * NT * c.K)
            for u in range(U):
                sp.dma_start(ring.rows[u], rows_of(slots, u)).then_inc(S(p + f"row_ld{u}"), 16)
            with sp.Fori(0, c.tiles // U) as i:
                for u in range(U):
                    sp.wait_ge(S(p + "turned"), i * U + (u + 1))
                    sp.dma_start(ring.rows[u], rows_of(slots, i * U + (u + U))).then_inc(S(p + f"row_ld{u}"), 16)
            for u in range(U):
                sp.wait_ge(S(p + f"res_st{u}"), 16 * (c.tiles // U + 1))
                sp.wait_ge(S(p + f"row_ld{u}"), 16 * (c.tiles // U + 1))
            sp.wait_ge(S(p + "w1_ready"), c.tiles + 4)
            sp.wait_ge(S(p + "rT_ready"), c.tiles + 4)
            sp.wait_ge(S(p + "hid_dve"), c.tiles + 3)
            sp.wait_ge(S(p + "hid_act"), c.tiles + 3)
            sp.sem_inc(S(p + "results_in"), 1)

        def expert_vector(dve, c, me):
            p, ring, v = f"f{c.n}_", Ring(c), nc.vector
            w1v = big[:, c.w1_at:c.w1_at + c.E * c.wcols].rearrange("p (e w) -> p e w", e=c.E)
            half = c.HC // 2
            hid = 128 * c.HC

            def stage(tau, u):
                e = dve.value_load(table[c.n][0:1, bass.ds(tau, 1)], min_val=0, max_val=c.E - 1)
                v.tensor_copy(ring.w1[u % 2], w1v[:, bass.ds(e, 1), :].rearrange("p e w -> p (e w)")).then_inc(S(p + "w1_ready"), 1)

            def turn(u):
                v.tensor_copy(ring.rT[u % 2], ps[:, u % 2, 0:128]).then_inc(S(p + "rT_ready"), 1)

            def rectify(u):
                w = ring.w1[u % 2]
                for k in range(half, c.HC):
                    last = v.tensor_scalar(ring.hid[u % 2][:, 128 * k:128 * k + 128], ps[:, 4 + u % 2, 128 * k:128 * k + 128],
                                           w[:, hid + k:hid + k + 1], 0.0, ALU.add, ALU.max)
                last.then_inc(S(p + "hid_dve"), 1)

            dve.sem_inc(S(p + "w1_ready"), 2)
            dve.sem_inc(S(p + "rT_ready"), 2)
            dve.sem_inc(S(p + "hid_dve"), 2)
            dve.wait_ge(S(f"w{c.n}_ld"), 16 * weight_loads(c))
            stage(0, 0)
            dve.wait_ge(S(p + "turned"), 1)
            turn(0)
            stage(1, 1)
            dve.wait_ge(S(p + "hid_filled"), 3)
            rectify(0)
            dve.wait_ge(S(p + "turned"), 2)
            turn(1)
            with dve.Fori(0, c.tiles // U) as i:
                for u in range(U):
                    dve.wait_ge(S(p + "hid_filled"), i * U + (u + 3))
                    dve.wait_ge(S(p + "hid_dve"), i * U + (u + 3))
                    dve.wait_ge(S(p + "hid_act"), i * U + (u + 3))
                    stage(i * U + (u + 2), u)
                    dve.wait_ge(S(p + "turned"), i * U + (u + 3))
                    turn(u)
                    dve.wait_ge(S(p + "hid_filled"), i * U + (u + 4))
                    dve.wait_ge(S(p + "res_filled"), i * U + (u + 2))
                    rectify(u + 1)

        def expert_scalar(act, c):
            p, ring, s = f"f{c.n}_", Ring(c), nc.scalar
            half, hid = c.HC // 2, 128 * c.HC

            def rectify(u):
                w = ring.w1[u % 2]
                for k in range(half):
                    last = s.activation(ring.hid[u % 2][:, 128 * k:128 * k + 128], ps[:, 2 + u % 2, 128 * k:128 * k + 128],
                                        ACT.Relu, bias=w[:, hid + k:hid + k + 1])
                last.then_inc(S(p + "hid_act"), 1)
            act.sem_inc(S(p + "hid_act"), 2)
            act.sem_inc(S(p + "res_ready"), 2)
            for u in range(U):
                act.sem_inc(S(p + f"res_st{u}"), 16)
            act.wait_ge(S(p + "hid_filled"), 3)
            act.wait_ge(S(p + "w1_ready"), 3)
            rectify(0)
            with act.Fori(0, c.tiles // U) as i:
                for u in range(U):
                    act.wait_ge(S(p + "hid_filled"), i * U + (u + 4))
                    act.wait_ge(S(p + "res_filled"), i * U + (u + 2))
                    rectify(u + 1)
                    act.wait_ge(S(p + "res_filled"), i * U + (u + 3))
                    act.wait_ge(S(p + f"res_st{u}"), i * 16 + 16)
                    s.copy(ring.res[u], ps[:, 6 + u % 2, 0:D]).then_inc(S(p + "res_ready"), 1)
                    act.wait_ge(S(p + "res_ready"), i * U + (u + 3))
                    act.dma_start(rows_of(results[c.n], i * U + u), ring.res[u]).then_inc(S(p + f"res_st{u}"), 16)

        def expert_tensor(pe, c):
            p, ring, t = f"f{c.n}_", Ring(c), nc.tensor
            w2v = big[:, c.w2_at:c.w2_at + c.E * c.HC * D].rearrange("p (e k d) -> p e k d", e=c.E, k=c.HC)

            def turn(u):
                t.transpose(ps[:, u % 2, 0:128], ring.rows[u % U], ident).then_inc(S(p + "turned"), 1)

            def first(u):
                for k in range(c.HC):
                    last = t.matmul(ps[:, (2 if k < c.HC // 2 else 4) + u % 2, 128 * k:128 * k + 128], ring.w1[u % 2][:, 128 * k:128 * k + 128],
                                    ring.rT[u % 2], start=True, stop=True)
                last.then_inc(S(p + "hid_filled"), 1)

            def second(tau, u):
                e = pe.value_load(table[c.n][0:1, bass.ds(tau, 1)], min_val=0, max_val=c.E - 1)
                for k in range(c.HC):
                    last = t.matmul(ps[:, 6 + u % 2, 0:D], ring.hid[u % 2][:, 128 * k:128 * k + 128],
                                    w2v[:, bass.ds(e, 1), k, :].rearrange("p e d -> p (e d)"), start=k == 0, stop=k == c.HC - 1)
                last.then_inc(S(p + "res_filled"), 1)

            pe.sem_inc(S(p + "hid_filled"), 2)
            pe.sem_inc(S(p + "res_filled"), 2)
            pe.wait_ge(S(p + "row_ld0"), 16)
            turn(0)
            pe.wait_ge(S(p + "row_ld1"), 16)
            turn(1)
            pe.wait_ge(S(p + "w1_ready"), 3)
            pe.wait_ge(S(p + "rT_ready"), 3)
            first(0)
            if c.n:
                pe.wait_ge(S("w1_late"), 16 * (c.E - 24))
            with pe.Fori(0, c.tiles // U) as i:
                for u in range(U):
                    pe.wait_ge(S(p + f"row_ld{(u + 2) % U}"), i * 16 + (16 if u < 2 else 32))
                    pe.wait_ge(S(p + "rT_ready"), i * U + (u + 3))
                    turn(u + 2)
                    pe.wait_ge(S(p + "w1_ready"), i * U + (u + 4))
                    pe.wait_ge(S(p + "rT_ready"), i * U + (u + 4))
                    pe.wait_ge(S(p + "hid_dve"), i * U + (u + 2))
                    pe.wait_ge(S(p + "hid_act"), i * U + (u + 2))
                    first(u + 1)
                    pe.wait_ge(S(p + "hid_dve"), i * U + (u + 3))
                    pe.wait_ge(S(p + "hid_act"), i * U + (u + 3))
                    pe.wait_ge(S(p + "res_ready"), i * U + (u + 1))
                    second(i * U + u, u)

        @block.sync
        def _(sp):
            def load(dst, src, sem):
                sp.dma_start(dst, src).then_inc(S(sem), 16)
            load(ids32[:, :], a["x"].rearrange("b (j p) -> (b j) p", p=R), "ld_ids")
            load(val32[:, :], a["fside_BS_value"].rearrange("b (j p) -> (b j) p", p=R), "ld_ids")
            for q, n in enumerate(["Lambda_re", "Lambda_im", "C_re", "C_im", "Bmat"]):
                for r in range(2):
                    load(ssm5[:, q, r, :], a["L0_attn_" + n], "ld_ssm")
            sp.wait_ge(S("dskip_zero"), 1)
            load(dskip[KA - 1:KA, :], a["L0_attn_Dvec"].rearrange("(o n) -> o n", o=1), "ld_ssm")
            load(wv, a["L0_tok_w_val"].rearrange("(j p) d -> p j d", p=R), "ld_val")
            load(bv, a["L0_tok_b_val"].rearrange("(j p) d -> p j d", p=R), "ld_val")
            for q, n in enumerate(["gamma_g", "beta_g", "gamma_v", "beta_v"]):
                load(rows[:, q, :], a["L0_tok_" + n].partition_broadcast(R), "ld_val")
            load(wsm[:, 0, :], a["L0_attn_Win"], "ld_w")
            load(wsm[:, 1, :], a["L0_attn_Wout"], "ld_w")
            load(lnc[:, 0:1], a["L0_attn_ln_gamma"].rearrange("(d o) -> d o", o=1), "ld_w")
            load(lnc[:, 1:2], a["L0_attn_ln_beta"].rearrange("(d o) -> d o", o=1), "ld_w")
            load(rowv[:, 0, :], a["L0_attn_bin_"].rearrange("(o d) -> o d", o=1), "ld_w")
            load(rowv[:, 1, :], a["L0_attn_bout"].rearrange("(o d) -> o d", o=1), "ld_w")
            sp.wait_ge(S("zeros_ready"), 1)
            for n in range(TAB // 12):
                sp.dma_start(slots[:, :].rearrange("(n p r) d -> n p (r d)", p=128, r=12)[n],
                             xbuf[:, 0:12 * D]).then_inc(S("cleared"), 16)
            load(wr[:, 0, 0:8], a["L0_ffn_Wr"], "ld_router")
            load(wr[:, 1, 0:8], a["L1_ffn_g1"], "ld_router")
            load(wr[:, 1, 8:72].rearrange("p (g e) -> p g e", g=8), a["L1_ffn_g2"].rearrange("g d e -> d g e"), "ld_router")
            load(brow[:, :], a["L0_ffn_br"].rearrange("(o n) -> o n", o=1), "ld_router")
            load(b1r[0:32, 0, :], a["L0_ffn_b1"].rearrange("e (k h) -> (e k) h", k=4), "ld_router")
            load(b1r[:, 1, :], a["L1_ffn_b1"].rearrange("g e (k h) -> (g e k) h", k=2), "ld_router")
            load(b2[0:8, 0, :], a["L0_ffn_b2"], "ld_router")
            load(b2[:, 1, :], a["L1_ffn_b2"].rearrange("g e d -> (g e) d"), "ld_router")
            sp.wait_ge(S("lags_ready"), 1)
            sp.dma_start(ap(kappa, KROW // 2, [[KB, KA], [KROW, NC], [1, KB]]), kk[:, :, 0:KB]).then_inc(S("kappa_st"), 16)
            sp.dma_start(ap(kappa, 0, [[KB, KA], [KROW, NC], [1, KB]]), kk[:, :, KB:2 * KB]).then_inc(S("kappa_st"), 16)
            sp.wait_ge(S("kappa_st"), 32)
            sp.wait_ge(S("values_read"), 1)
            for q in range(8):
                sp.dma_start(G[:, 4 * q:4 * q + 4, :],
                             ap(kappa, 4 * q * KROW + KROW // 2 - L, [[1, 128], [KROW, 4], [1, GM]])
                             ).then_inc(S(f"strip{q}"), 16)
            sp.wait_ge(S("bank_filled"), nfill[at["out0", B - 1]])
            load_weights(sp, FFN[0])
            load_weights(sp, FFN[1])
            for f in (0, 1):
                expert_dma(sp, FFN[f])
                if f == 0:
                    sp.wait_ge(S("azero_ready"), 1)
                    for w, n in enumerate(("Wq", "Wk", "Wv", "Wo")):
                        load(wraw[:, w, :], a["L1_attn_" + n], "ld_attn")
                    for half in range(2):
                        for i in range(4):
                            hd = DK * (4 * half + i)
                            load(wkn[32 * i:32 * i + DK, half, :], a["L1_attn_Wk"][hd:hd + DK, :], "ld_attn")
                        for w, n in enumerate(("bq", "bk")):
                            load(brow2[:, w, half, :].rearrange("p (i m) -> p i m", i=4)[:, :, 0:DK],
                                 a["L1_attn_" + n].rearrange("(o s i e) -> s o i e", o=1, s=2, e=DK)[half], "ld_attn")
                    load(borow[:, 0, :], a["L1_attn_bv"].rearrange("(o d) -> o d", o=1), "ld_attn")
                    load(borow[:, 1, :], a["L1_attn_bo"].rearrange("(o d) -> o d", o=1), "ld_attn")
                    load(sidx.bitcast(I32), a["L1_attn_samp_idx"].rearrange("(p s) -> p s", p=128), "ld_attn")
            sp.wait_ge(S("done"), 1)
            sp.dma_start(out.rearrange("b (j p) d -> p (b j) d", p=R), h[:, :, :]).then_inc(S("out_st"), 16)
            sp.wait_ge(S("out_st"), 16)

        @block.gpsimd
        def _(pool):
            me = Steps(pool, S("pool_step"))
            gp = nc.gpsimd
            gp.memset(dskip[:, :], 0.0).then_inc(S("dskip_zero"), 1)
            gp.memset(xbuf[:, 0:12 * D], 0.0).then_inc(S("zeros_ready"), 1)
            me.did(gp.memset(ones[:, :], 1.0))
            me.then(gp.memset(ident, 0.0))
            gp.affine_select(out=ident, in_=ident, compare_op=ALU.not_equal, fill=1.0, base=0,
                             pattern=[[-1, 128]], channel_multiplier=1).then_inc(S("ident_ready"), 1)
            me.did(gp.iota(itI[:, 0:KA], pattern=[[KB, KA]], base=0, channel_multiplier=0))
            me.then(gp.iota(itI[:, KA:KA + KB], pattern=[[1, KB]], base=0, channel_multiplier=0))
            for col, top, bot in ((0, math.pi / 2, 0.0), (1, 0.0, -math.pi / 2), (2, math.pi / 2, math.pi)):
                me.then(gp.memset(alpha[0:64, col:col + 1], top))
                me.then(gp.memset(alpha[64:128, col:col + 1], bot))
            gp.memset(alpha[:, 3:4], 0.0).then_inc(S("iota_ready"), 1)
            me.did(gp.memset(onesb[:, :], 1.0))
            me.then(gp.memset(ltri[:, :, :], 1.0))
            for k, op in ((0, ALU.is_gt), (1, ALU.is_ge)):
                me.then(gp.affine_select(out=ltri[:, k, :], in_=ltri[:, k, :], compare_op=op, fill=0.0, base=0,
                                         pattern=[[1, 128]], channel_multiplier=-1))
            me.did(gp.iota(tileno[:, :].bitcast(I32), pattern=[[1, TAB]], base=0, channel_multiplier=0))
            gp.iota(em8I[:, :], pattern=[[1, 8]], base=-8, channel_multiplier=0).then_inc(S("iota2_ready"), 1)
            pool.wait_ge(S("ids_ready"), 1)
            for t in range(NT):
                gp.indirect_dma_start(gw[:, t, :], None, a["L0_tok_emb_table"],
                                      bass.IndirectOffsetOnAxis(ap=idsT[:, t:t + 1], axis=0)
                                      ).then_inc(S(f"gathered{t // J}"), 16)
            pool.wait_ge(S("ld_val"), 96)
            me.then(gp.tensor_tensor(out=bbt[:, :], in0=rows[:, 1, :], in1=rows[:, 3, :], op=ALU.add))
            for b in range(B):
                pool.wait_ge(S("vn_ready"), b + 1)
                v = vw[:, J * b:J * b + J, :]
                me.then(gp.tensor_tensor(out=v, in0=v, in1=rows[:, 2:3, :].broadcast_to([R, J, D]), op=ALU.mult))
                gp.tensor_tensor(out=v, in0=v, in1=bbt[:, :].unsqueeze(1).broadcast_to([R, J, D]),
                                 op=ALU.add).then_inc(S("vb_ready"), 1)
            for b in range(B):
                pool.wait_ge(S("x0_ready"), b + 1)
                v = h[:, J * b:J * b + J, :]
                gp.tensor_tensor(out=v, in0=v, in1=x[:, J * b:J * b + J, :], op=ALU.add).then_inc(S("hx_ready"), 1)

            for f in (0, 1):
                c = FFN[f]
                q = f"f{f}_"
                pool.wait_ge(S(q + "placed"), 1)
                if f == 0:
                    pool.wait_ge(S("cleared"), 16 * (TAB // 12))
                for k in range(c.K):
                    for t in range(NT):
                        gp.indirect_dma_start(slots[:, :], bass.IndirectOffsetOnAxis(ap=place[f][:, k, t:t + 1], axis=0),
                                              x[:, t, :], None).then_inc(S(q + "scattered"), 16)
                pool.wait_ge(S(q + "results_in"), 1)
                if f == 0:
                    gp.memset(azero, 0.0).then_inc(S("azero_ready"), 1)
                    me.did(gp.iota(i500.bitcast(I32), pattern=[[1, L]], base=0, channel_multiplier=0))
                    me.did(gp.memset(own16, 1.0))
                    me.settle()
                    me.then(gp.affine_select(out=own16, in_=own16, compare_op=ALU.is_ge, fill=0.0, base=0,
                                             pattern=[[-DK, H]], channel_multiplier=1))
                    me.then(gp.affine_select(out=own16, in_=own16, compare_op=ALU.is_ge, fill=0.0, base=DK - 1,
                                             pattern=[[DK, H]], channel_multiplier=-1))
                    pool.wait_ge(S("azero_ready"), 1)
                    for half in range(2):
                        for i in range(4):
                            me.then(gp.memset(own[32 * i:32 * i + 32, half, 4 * half + i:4 * half + i + 1], 1.0))
                    me.did(gp.memset(brow2[:, 0].rearrange("p s (i m) -> p (s i) m", i=4)[:, :, DK:DK + 1], 1.0))
                    me.then(gp.memset(selrow, 0.0))
                    gp.memset(selrow.rearrange("p (i m) -> p i m", i=4)[:, :, DK:DK + 1], 1.0).then_inc(S("aconst_ready"), 1)
                n = 0
                for t in range(NT):
                    for k in range(c.K):
                        if n >= 8:
                            pool.wait_ge(S(q + "combined"), n - 7)
                        gp.indirect_dma_start(got[n % 8], None, results[f][:, :],
                                              bass.IndirectOffsetOnAxis(ap=place[f][:, k, t:t + 1], axis=0)
                                              ).then_inc(S(q + f"got{n % 8}"), 16)
                        n += 1

        @block.vector
        def _(dve):
            me = Steps(dve, S("dve_step"))
            v = nc.vector

            def emptied(ins):
                ins.then_inc(S("emptied_dve"), 1)

            def stats(src, b, mean_var):
                for t in range(J * b, J * b + J):
                    me.did(v.bn_stats(bnst[:, t, :], src[:, t, :]))
                me.settle()
                for t in range(J * b, J * b + J):
                    me.did(v.bn_aggr(mean_var[:, t, :], bnst[:, t, :]))

            def invert(root, dst, base):
                dve.wait_ge(S("root_ready"), base)
                me.then(v.reciprocal(dst, root))

            def route(c, me, dve):
                f, m = c.n, mask_views(c.n)
                TT, TS = v.tensor_tensor, v.tensor_scalar
                q = f"f{f}_"
                e8 = em8[:, :]

                def v4(name, n):
                    return m[name][:, 0:n * 256].rearrange("p (i e t) -> p i e t", i=n, e=8)

                def small(k, n):
                    return sm[:, k:k + n, :]

                def over_e(t, n):
                    return t.unsqueeze(2).broadcast_to([R, n, 8, NT])

                def e8_over(n):
                    return e8.unsqueeze(1).unsqueeze(3).broadcast_to([R, n, 8, NT])

                def top(src, hot, n, best, index):
                    me.then(v.tensor_reduce(out=best, in_=src.rearrange("p i e t -> p i t e"), axis=AX.X, op=ALU.max))
                    me.then(TT(out=hot, in0=src, in1=over_e(best, n), op=ALU.is_equal))
                    me.then(TT(out=hot, in0=hot, in1=e8_over(n), op=ALU.mult))
                    me.then(v.tensor_reduce(out=index, in_=hot.rearrange("p i e t -> p i t e"), axis=AX.X, op=ALU.min))
                    me.then(TT(out=hot, in0=over_e(index, n), in1=e8_over(n), op=ALU.is_equal))

                def without(src, hot, flat):
                    me.then(v.scalar_tensor_tensor(flat(src), flat(hot), -1e30, flat(src), ALU.mult, ALU.add))

                def flat(t):
                    return t.rearrange("p i e t -> p (i e t)")

                for b in range(B):
                    wait_bank(dve, f"router{f}", b)
                    src = bank(at[f"router{f}", b])[0:R, 0:J * c.wide].rearrange("p (j e) -> p e j", j=J)
                    ins = v.tensor_copy(m["lg"].rearrange("p (e t) -> p e t", e=8)[:, :, J * b:J * b + J], src[:, 0:8, :])
                    if f:
                        me.did(ins)
                        ins = v.tensor_copy(m["le"].rearrange("p (e t) -> p e t", e=64)[:, :, J * b:J * b + J], src[:, 8:72, :])
                    emptied(ins)
                dve.wait_ge(S("emptied_dve"), nth[at[f"router{f}", B - 1]])
                lg = v4("lg", 1)
                oh = v4("oh1", 1), v4("oh2", 1)
                if f == 0:
                    me.did(v.tensor_copy(m["rest"][:, 0:256], m["lg"]))
                    top(lg, oh[0], 1, small(0, 1), small(2, 1))
                    without(lg, oh[0], flat)
                    top(lg, oh[1], 1, small(1, 1), small(2, 1))
                    r = m["rest"][:, 0:256].rearrange("p (i e t) -> p i e t", i=1, e=8)
                    me.did(TT(out=r, in0=r, in1=over_e(small(0, 1), 1), op=ALU.subtract))
                    TT(out=small(1, 1), in0=small(1, 1), in1=small(0, 1), op=ALU.subtract).then_inc(S("soft_in"), 1)
                    dve.wait_ge(S("soft_out"), 1)
                    me.then(v.tensor_reduce(out=small(2, 1), in_=r.rearrange("p i e t -> p i t e"), axis=AX.X, op=ALU.add))
                    me.then(v.reciprocal(gate[0][:, 0:1, :], small(2, 1)))
                    me.did(TT(out=gate[0][:, 1:2, :], in0=small(1, 1), in1=gate[0][:, 0:1, :], op=ALU.mult))
                    me.then(TT(out=flat(v4("eh1", 1)), in0=flat(oh[0]), in1=flat(oh[1]), op=ALU.add))
                    me.did(v.tensor_copy(m["members"], flat(v4("eh1", 1))))
                    for k in range(2):
                        me.did(TT(out=v4("eh1", 2)[:, k:k + 1], in0=oh[k], in1=over_e(gate[0][:, k:k + 1, :], 1), op=ALU.mult)) if k else \
                            me.then(TT(out=v4("pick", 1), in0=oh[0], in1=over_e(gate[0][:, 0:1, :], 1), op=ALU.mult))
                    me.settle()
                    me.then(TT(out=m["gates"], in0=flat(v4("pick", 1)), in1=m["eh1"][:, 256:512], op=ALU.add))
                else:
                    le = m["le"].rearrange("p (g e t) -> p g e t", g=8, e=8)
                    tmp = m["tmp"].rearrange("p (g e t) -> p g e t", g=8, e=8)
                    top(lg, oh[0], 1, small(0, 1), small(2, 1))
                    without(lg, oh[0], flat)
                    top(lg, oh[1], 1, small(1, 1), small(2, 1))
                    rest = v4("rest", 2)
                    for i in range(2):
                        hot_g = oh[i][:, 0].unsqueeze(2).broadcast_to([R, 8, 8, NT])
                        me.then(TT(out=tmp, in0=le, in1=hot_g, op=ALU.mult))
                        me.then(v.tensor_reduce(out=rest[:, i], in_=tmp.rearrange("p g e t -> p e t g"), axis=AX.X, op=ALU.add))
                    eh = v4("eh1", 2), v4("eh2", 2)
                    top(rest, eh[0], 2, small(4, 2), small(8, 2))
                    without(rest, eh[0], flat)
                    top(rest, eh[1], 2, small(6, 2), small(8, 2))
                    me.did(TT(out=small(10, 2), in0=small(6, 2), in1=small(4, 2), op=ALU.subtract))
                    TT(out=small(1, 1), in0=small(1, 1), in1=small(0, 1), op=ALU.subtract).then_inc(S("soft_in"), 1)
                    dve.wait_ge(S("soft_out"), 2)
                    me.did(TS(small(0, 1), small(1, 1), 1.0, None, ALU.add))
                    me.then(TS(small(4, 2), small(10, 2), 1.0, None, ALU.add))
                    me.did(v.reciprocal(small(0, 1), small(0, 1)))
                    me.then(v.reciprocal(small(4, 2), small(4, 2)))
                    me.did(TT(out=small(1, 1), in0=small(1, 1), in1=small(0, 1), op=ALU.mult))
                    me.then(TT(out=small(6, 2), in0=small(10, 2), in1=small(4, 2), op=ALU.mult))
                    for i in range(2):
                        for j in range(2):
                            me.did(TT(out=gate[1][:, 2 * i + j, :], in0=sm[:, i, :], in1=sm[:, 4 + 2 * j + i, :], op=ALU.mult))
                    me.settle()
                    for what, out_ in (("members", m["members"]), ("gates", m["gates"])):
                        for i in range(2):
                            pk = v4("pick", 2)[:, i:i + 1]
                            if what == "members":
                                me.then(TT(out=pk, in0=eh[0][:, i:i + 1], in1=eh[1][:, i:i + 1], op=ALU.add))
                            else:
                                o_ = rest[:, i:i + 1]
                                me.did(TT(out=pk, in0=eh[0][:, i:i + 1], in1=over_e(gate[1][:, 2 * i:2 * i + 1, :], 1), op=ALU.mult))
                                me.then(TT(out=o_, in0=eh[1][:, i:i + 1], in1=over_e(gate[1][:, 2 * i + 1:2 * i + 2, :], 1), op=ALU.mult))
                                me.then(TT(out=pk, in0=pk, in1=o_, op=ALU.add))
                            hot_g = oh[i][:, 0].unsqueeze(2).broadcast_to([R, 8, 8, NT])
                            dst = tmp if i == 0 else m["slot"].rearrange("p (g e t) -> p g e t", g=8, e=8)
                            me.then(TT(out=dst, in0=hot_g, in1=pk[:, 0].unsqueeze(1).broadcast_to([R, 8, 8, NT]), op=ALU.mult))
                        me.then(TT(out=out_, in0=m["tmp"], in1=m["slot"], op=ALU.add))
                ch = m["chain"].rearrange("p (e t) -> p e t", t=NT)
                me.then(v.memset(m["chain"], 1.0))
                me.then(v.memset(ch[:, :, 0:1], 0.0))
                v.tensor_tensor_scan(m["upto"], m["chain"], m["members"], 0.0, ALU.mult, ALU.add).then_inc(S(q + "counted"), 1)
                dve.wait_ge(S(q + "counted"), 1)
                TT(out=m["before"], in0=m["upto"], in1=m["members"], op=ALU.subtract).then_inc(S(q + "counted"), 1)
                wait_bank(dve, f"count{f}")
                pc = bank(at[f"count{f}", 0])
                nt, run, first = ntile[:, 0, 0:c.E], ntile[:, 1, 0:c.E], ntile[:, 2, 0:c.E]
                me.did(TS(nt, pc[0:R, 0:c.E], 127.0, 1.0 / 128.0, ALU.add, ALU.mult))
                emptied(TS(ncol[0:c.E, 0:1], pc[0:c.E, 64:65], 127.0, 1.0 / 128.0, ALU.add, ALU.mult))
                dve.wait_ge(S("emptied_dve"), nth[at[f"count{f}", 0]])
                me.did(TS(nt, nt, 127.0 / 256.0, MAGIC, ALU.subtract, ALU.add))
                me.then(TS(ncol[0:c.E, 0:1], ncol[0:c.E, 0:1], 127.0 / 256.0, MAGIC, ALU.subtract, ALU.add))
                me.did(TS(nt, nt, MAGIC, None, ALU.subtract))
                TS(ncolb[0:c.E, :], ncol[0:c.E, 0:1], MAGIC, None, ALU.subtract).then_inc(S(q + "counted"), 1)
                me.did(v.memset(first, 1.0))
                me.settle()
                dve.wait_ge(S(q + "counted"), 3)
                me.then(v.tensor_tensor_scan(run, first, nt, 0.0, ALU.mult, ALU.add))
                me.then(TT(out=first, in0=run, in1=nt, op=ALU.subtract))
                me.then(TS(first, first, 128.0, None, ALU.mult))
                ne = c.E // c.banks
                for i in range(c.banks):
                    wait_bank(dve, f"rank{f}", i)
                    w = slice(ne * NT * i, ne * NT * (i + 1))
                    emptied(TT(out=m["slot"][:, w].rearrange("p (e t) -> p e t", t=NT),
                               in0=bank(at[f"rank{f}", i])[0:R, 0:ne * NT].rearrange("p (e t) -> p e t", t=NT),
                               in1=first[:, ne * i:ne * i + ne].unsqueeze(2).broadcast_to([R, ne, NT]), op=ALU.add))
                wait_bank(dve, f"ends{f}")
                emptied(v.tensor_copy(ncol[0:c.E, 1:2], bank(at[f"ends{f}", 0])[0:c.E, 0:1]))
                dve.wait_ge(S("emptied_dve"), nth[at[f"ends{f}", 0]])
                over = m["pick"][0:c.E, 0:TAB // 2].bitcast(BF16)
                TS(over, tileno[0:c.E, :], ncol[0:c.E, 1:2], None, ALU.is_ge).then_inc(S(q + "counted"), 1)
                wait_bank(dve, f"expert{f}")
                emptied(TS(table[f][:, :], bank(at[f"expert{f}", 0])[0:1, 0:TAB], float(c.E - 1), None, ALU.min))
                S_ = m["slot"]
                if f == 0:
                    for k in range(2):
                        me.then(TT(out=m["tmp"], in0=flat(oh[k]), in1=S_, op=ALU.mult))
                        me.then(v.tensor_reduce(out=sm[:, k, :], in_=m["tmp"].rearrange("p (e t) -> p t e", t=NT), axis=AX.X, op=ALU.add))
                else:
                    s4 = S_.rearrange("p (g e t) -> p g e t", g=8, e=8)
                    for i in range(2):
                        hot_g = oh[i][:, 0].unsqueeze(2).broadcast_to([R, 8, 8, NT])
                        me.then(TT(out=tmp, in0=s4, in1=hot_g, op=ALU.mult))
                        me.then(v.tensor_reduce(out=rest[:, i], in_=tmp.rearrange("p g e t -> p e t g"), axis=AX.X, op=ALU.add))
                    for j in range(2):
                        me.then(TT(out=v4("pick", 2), in0=eh[j], in1=rest, op=ALU.mult))
                        for i in range(2):
                            me.then(v.tensor_reduce(out=sm[:, 2 * i + j, :], in_=v4("pick", 2)[:, i].rearrange("p e t -> p t e"),
                                                    axis=AX.X, op=ALU.add))
                v.tensor_copy(place[f][:, 0:c.K, :], sm[:, 0:c.K, :]).then_inc(S(q + "placed"), 1)

            def attention(me, dve):
                TT, TS = v.tensor_tensor, v.tensor_scalar
                dve.wait_ge(S("ld_attn"), 16 * 19)
                dve.wait_ge(S("aconst_ready"), 1)
                me.did(v.tensor_copy(i500, i500.bitcast(I32)))
                me.then(v.tensor_copy(sidf, sidx.bitcast(I32)))
                me.then(TS(shi, sidf, 0.0, float(L), ALU.is_lt, ALU.mult))
                me.then(TT(out=sidf, in0=sidf, in1=shi, op=ALU.add))
                me.then(TS(sidf, sidf, 0.0, float(L - 1), ALU.max, ALU.min))
                me.then(TS(shi, sidf, float(R), None, ALU.is_ge))
                for k in range(2, J):
                    me.then(v.scalar_tensor_tensor(shi, sidf, float(R * k), shi, ALU.is_ge, ALU.add))
                me.then(v.scalar_tensor_tensor(slo, shi, -float(R), sidf, ALU.mult, ALU.add))
                me.did(TT(out=hot_hi, in0=shi.unsqueeze(2).broadcast_to([128, 20, J]),
                          in1=i500[:, 0:J].unsqueeze(1).broadcast_to([128, 20, J]), op=ALU.is_equal))
                TT(out=hot_lo, in0=slo.unsqueeze(2).broadcast_to([128, 20, R]),
                   in1=i500[:, 0:R].unsqueeze(1).broadcast_to([128, 20, R]), op=ALU.is_equal).then_inc(S("hots_ready"), 1)
                wait_bank(dve, "wT")
                pw = bank(at["wT", 0])
                for w, dst in enumerate((wqT, wkT)):
                    me.did(v.tensor_copy(dst.rearrange("p s (i m) -> p (s i) m", i=4)[:, :, 0:DK],
                                         pw[:, 128 * w:128 * w + 128].rearrange("p (n e) -> p n e", n=H)))
                me.did(v.tensor_copy(wvT, pw[:, 256:384]))
                emptied(v.tensor_copy(woT, pw[:, 384:512]))
                wait_bank(dve, "cols")
                emptied(v.tensor_copy(bcol, bank(at["cols", 0])[:, 0:5]))
                wait_bank(dve, "cnt")
                emptied(v.tensor_copy(cnt, bank(at["cnt", 0])[0:R, 0:J]))
                wait_bank(dve, "cntrow")
                emptied(TS(maskrow, bank(at["cntrow", 0])[0:1, 0:L], 0.0, -1e30, ALU.is_equal, ALU.mult))
                for b in range(B):
                    stats(h, b, mv)
                me.settle()
                v.tensor_scalar(rs[:, :], mv[:, :, 1], EPS, None, ALU.add).then_inc(S("var_ready"), 1)
                invert(rs[:, :], rs[:, :], 6)
                for b in range(B):
                    for t in range(J * b, J * b + J):
                        last = TS(x[:, t, :], h[:, t, :], mv[:, t, 0:1], rs[:, t:t + 1], ALU.subtract, ALU.mult)
                    last.then_inc(S("xa_ready"), 1)
                wait_bank(dve, "xbar")
                emptied(TS(xbar, bank(at["xbar", 0])[:, 0:B], 1.0 / NSAMP, None, ALU.mult))
                wait_bank(dve, "kbar")
                for half in range(2):
                    me.did(TS(kcol[:, half, :], bank(at["kbar", 0])[:, B * half:B * half + B],
                              bcol[:, 2 + half:3 + half], -1.0, ALU.add, ALU.mult))
                me.settle()
                for half in range(2):
                    last = TS(kcol[:, half, :], kcol[:, half, :], bcol[:, 2 + half:3 + half], None, ALU.add)
                emptied(last)
                for g in range(8 * B):
                    b, half, j = g // 8, g // 4 % 2, g % 4
                    n = at["score", 4 * g]
                    wait_bank(dve, "score", 4 * g + 3)
                    emptied(v.tensor_reduce(out=mcol[:, j, H * b + 4 * half:H * b + 4 * half + 4],
                                            in_=ps[0:R, n % 8:n % 8 + 4, 0:L], axis=AX.X, op=ALU.max))
                wait_bank(dve, "MT")
                emptied(v.tensor_copy(mrow, bank(at["MT", 0])[0:64, 0:L]))
                dve.wait_ge(S("emptied_dve"), nth[at["MT", 0]])
                me.then(v.max(m8, mrow))
                me.then(v.max_index(i8, m8, mrow))
                me.then(v.tensor_copy(i8f, i8[:, 0:1]))
                TS(hot, i500[0:64, :], i8f, None, ALU.is_equal).then_inc(S("hot_ready"), 1)
                wait_bank(dve, "hotT")
                emptied(v.tensor_copy(hotT, bank(at["hotT", 0])[0:R, 0:256].rearrange("p (j n) -> p j n", j=J)))
                wait_bank(dve, "xsel")
                emptied(v.tensor_copy(xsel, bank(at["xsel", 0])[:, 0:64]))
                wait_bank(dve, "qsel")
                for half in range(2):
                    last = v.scalar_tensor_tensor(qsel[:, half, :].rearrange("p (b h) -> p b h", b=B),
                                                  bank(at["qsel", 0])[:, 64 * half:64 * half + 64].rearrange("p (b h) -> p b h", b=B),
                                                  bcol[:, half:half + 1], own[:, half, :].unsqueeze(1).broadcast_to([128, B, H]),
                                                  ALU.add, ALU.mult)
                emptied(last)
                wait_bank(dve, "u")
                emptied(v.tensor_copy(bass.AP(tensor=uz.tensor, offset=uz.offset, ap=[list(uz.ap[0]), [72, B], [1, H]]),
                                      bank(at["u", 0])[:, 0:64].rearrange("p (b h) -> p b h", b=B)))
                wait_bank(dve, "ss")
                me.then(v.tensor_reduce(out=nmx, in_=bank(at["ss", 0])[0:64, 0:L], axis=AX.X, op=ALU.max))
                TS(nmx, nmx, -SCALE, None, ALU.mult).then_inc(S("nmx_ready"), 1)
                wait_evac(dve, "ss")
                me.then(v.reciprocal(asum, asum))
                TS(att, att, asum, None, ALU.mult).then_inc(S("att_ready"), 1)
                wait_bank(dve, "attT")
                emptied(v.tensor_copy(attT, bank(at["attT", 0])[0:R, 0:256].rearrange("p (j n) -> p j n", j=J)))
                wait_bank(dve, "xa")
                emptied(v.tensor_copy(xa, bank(at["xa", 0])[:, 0:64]))
                wait_bank(dve, "ctx")
                emptied(TT(out=cmul.rearrange("p (b h) -> p b h", b=B), in0=bank(at["ctx", 0])[:, 0:64].rearrange("p (b h) -> p b h", b=B),
                           in1=own16.unsqueeze(1).broadcast_to([128, B, H]), op=ALU.mult))
                dve.wait_ge(S("emptied_dve"), nth[at["ctx", 0]])
                me.then(v.tensor_reduce(out=ctxv, in_=cmul.rearrange("p (b h) -> p b h", b=B), axis=AX.X, op=ALU.add))
                TS(ctxb, ctxv.unsqueeze(2).broadcast_to([128, B, R]), bcol[:, 4:5], None, ALU.add).then_inc(S("ctx_ready"), 1)
                for i in range(2):
                    wait_bank(dve, "outa", i)
                    for b in range(4 * i, 4 * i + 4):
                        hv = h[:, J * b:J * b + J, :]
                        k = b - 4 * i
                        row = bank(at["outa", i])[0:R, D * k:D * k + D].unsqueeze(1).broadcast_to([R, J, D])
                        last = TT(out=hv, in0=row, in1=hv, op=ALU.add)
                    emptied(last)
                dve.wait_ge(S("emptied_dve"), nth[at["outa", 1]])

            dve.wait_ge(S("ld_ids"), 32)
            v.tensor_copy(ids32f[:, :], ids32[:, :]).then_inc(S("ids_float"), 1)
            wait_bank(dve, "tokens")
            v.tensor_copy(idsT[:, :], bank(at["tokens", 0])[0:R, 0:NT]).then_inc(S("ids_ready"), 1)
            emptied(v.tensor_copy(valT[:, :], bank(at["tokens", 0])[0:R, 32:32 + NT]))
            wait_bank(dve, "ssm")
            emptied(v.tensor_copy(sp5[:, :, :], bank(at["ssm", 0])[:, 0:5 * NC].rearrange("p (q c) -> p q c", q=5)))
            dve.wait_ge(S("emptied_dve"), nth[at["ssm", 0]])
            dve.wait_ge(S("iota_ready"), 1)
            me.then(v.tensor_copy(itF[:, :], itI[:, :]))

            def lagmul(dst, q, lo, n):
                return v.tensor_tensor(out=dst, in0=sp5[:, q, :].unsqueeze(2).broadcast_to([128, NC, n]),
                                       in1=itF[:, lo:lo + n].unsqueeze(1).broadcast_to([128, NC, n]), op=ALU.mult)
            na, nb = NC * KA, NC * KB
            pa, pa2, pb = ph[:, 0:na], ph[:, na:2 * na], ph[:, 2 * na:]
            ma, mb = mg[:, 0:na], mg[:, na:na + nb]

            def cl(t, n):
                return t.rearrange("p (c l) -> p c l", l=n)
            me.did(lagmul(cl(ma, KA), 0, 0, KA))
            lagmul(cl(mb, KB), 0, KA, KB).then_inc(S("exponents_ready"), 1)
            me.did(lagmul(cl(pa, KA), 1, 0, KA))
            me.did(lagmul(cl(pb, KB), 1, KA, KB))
            me.settle()
            me.did(v.tensor_scalar(pa2, pa, alpha[:, 1:2], None, ALU.add))
            me.did(v.tensor_scalar(pb, pb, alpha[:, 2:3], None, ALU.add))
            me.settle()
            me.then(v.tensor_scalar(pa, pa, alpha[:, 0:1], None, ALU.add))
            me.then(v.tensor_scalar(qn, ph, 1.0 / (2.0 * math.pi), MAGIC, ALU.mult, ALU.add))
            me.then(v.tensor_scalar(qn, qn, MAGIC, None, ALU.subtract))
            me.then(v.scalar_tensor_tensor(ph, qn, -6.28125, ph, ALU.mult, ALU.add))
            me.then(v.scalar_tensor_tensor(ph, qn, -(2.0 * math.pi - 6.28125), ph, ALU.mult, ALU.add))
            v.tensor_scalar(ph, ph, 3.1415925, -3.1415925, ALU.min, ALU.max).then_inc(S("phases_ready"), 1)
            me.did(v.tensor_tensor(out=cc[:, 0, :], in0=sp5[:, 2, :], in1=sp5[:, 4, :], op=ALU.mult))
            me.did(v.tensor_tensor(out=cc[:, 1, :], in0=sp5[:, 3, :], in1=sp5[:, 4, :], op=ALU.mult))
            me.settle()
            dve.wait_ge(S("sines_ready"), 1)

            def cb(q):
                return cc[:, q, :].unsqueeze(2).broadcast_to([128, NC, KA])
            me.did(v.tensor_tensor(out=cl(pa, KA), in0=cl(pa, KA), in1=cb(0), op=ALU.mult))
            me.did(v.tensor_tensor(out=cl(pa2, KA), in0=cl(pa2, KA), in1=cb(1), op=ALU.mult))
            me.settle()
            me.then(v.tensor_tensor(out=pa, in0=pa, in1=pa2, op=ALU.subtract))
            me.did(v.tensor_tensor(out=e1[:, :, :], in0=cl(pa, KA), in1=cl(ma, KA), op=ALU.mult))
            me.did(v.tensor_tensor(out=e1r[:, :, :], in0=cl(pa, KA)[:, :, ::-1], in1=cl(ma, KA)[:, :, ::-1], op=ALU.mult))
            me.did(v.tensor_tensor(out=e2[:, :, 0:KB], in0=cl(pb, KB), in1=cl(mb, KB), op=ALU.mult))
            v.tensor_tensor(out=e2[:, :, KB:2 * KB], in0=cl(pb, KB)[:, :, ::-1], in1=cl(mb, KB)[:, :, ::-1],
                            op=ALU.mult).then_inc(S("factors_ready"), 1)
            for q in range(4):
                wait_bank(dve, "lags", q)
                emptied(v.tensor_copy(kk[:, 8 * q:8 * q + 8, :],
                                      bank(at["lags", q])[0:KA, :].rearrange("p (c l) -> p c l", c=8)))
            dve.wait_ge(S("emptied_dve"), nth[at["lags", 3]])
            v.tensor_tensor(out=kk[:, :, 2 * KB - 1], in0=kk[:, :, 2 * KB - 1], in1=dskip[:, :],
                            op=ALU.add).then_inc(S("lags_ready"), 1)
            dve.wait_ge(S("ld_w"), 96)
            v.tensor_scalar(wg[:, :], wsm[:, 0, :], lnc[:, 0:1], None, ALU.mult).then_inc(S("wg_ready"), 1)
            v.tensor_copy(cst[:, 512:640], lnc[:, 1:2].broadcast_to([128, 128])).then_inc(S("wg_ready"), 1)
            dve.wait_ge(S("ld_val"), 96)
            for t in range(NT):
                me.did(v.scalar_tensor_tensor(vw[:, t, :], wv[:, t % J, :], valT[:, t:t + 1], bv[:, t % J, :],
                                              ALU.mult, ALU.add))
            me.settle()
            v.tensor_copy(cst[0:1, 128:129], valT[0:1, 0:1]).then_inc(S("values_read"), 1)
            for b in range(B):
                stats(vw, b, mv)
            me.settle()
            v.tensor_scalar(rs[:, :], mv[:, :, 1], EPS, None, ALU.add).then_inc(S("var_ready"), 1)
            invert(rs[:, :], rs[:, :], 1)
            for b in range(B):
                for t in range(J * b, J * b + J):
                    last = v.tensor_scalar(vw[:, t, :], vw[:, t, :], mv[:, t, 0:1], rs[:, t:t + 1], ALU.subtract, ALU.mult)
                last.then_inc(S("vn_ready"), 1)
            wait_bank(dve, "zbias")
            emptied(v.tensor_copy(rows[:, 4, :], bank(at["zbias", 0])[0:R, 0:D]))
            dve.wait_ge(S("vn_ready"), B)
            for b in range(B):
                dve.wait_ge(S(f"gathered{b}"), 16 * J)
                stats(gw, b, mv)
            me.settle()
            v.tensor_scalar(rs[:, :], mv[:, :, 1], EPS, None, ALU.add).then_inc(S("var_ready"), 1)
            invert(rs[:, :], rs[:, :], 2)
            for b in range(B):
                for t in range(J * b, J * b + J):
                    me.did(v.scalar_tensor_tensor(gw[:, t, :], gw[:, t, :], mv[:, t, 0:1], rows[:, 0, :], ALU.subtract, ALU.mult))
            me.settle()
            for b in range(B):
                dve.wait_ge(S("vb_ready"), b + 1)
                for t in range(J * b, J * b + J):
                    me.did(v.scalar_tensor_tensor(h[:, t, :], gw[:, t, :], rs[:, t:t + 1], vw[:, t, :], ALU.mult, ALU.add))
            me.settle()
            for b in range(B):
                stats(h, b, mv)
            me.settle()
            v.tensor_scalar(rs[:, :], mv[:, :, 1], EPS, None, ALU.add).then_inc(S("var_ready"), 1)
            invert(rs[:, :], rs[:, :], 3)
            dve.wait_ge(S("cleared"), 16 * (TAB // 12))
            for b in range(B):
                for t in range(J * b, J * b + J):
                    last = v.tensor_scalar(x[:, t, :], h[:, t, :], mv[:, t, 0:1], rs[:, t:t + 1], ALU.subtract, ALU.mult)
                last.then_inc(S("x0_ready"), 1)
            me.then(v.tensor_tensor(out=rs2[:, :], in0=rs[:, :], in1=rs[:, :], op=ALU.mult))
            me.then(v.tensor_tensor(out=rs2[:, :], in0=rs2[:, :], in1=mv[:, :, 1], op=ALU.mult))
            v.tensor_scalar(rs2[:, :], rs2[:, :], EPS, None, ALU.add).then_inc(S("var_ready"), 1)
            invert(rs2[:, :], rs2[:, :], 4)
            for b in range(B):
                wait_bank(dve, "z", b)
                pz = bank(at["z", b])[0:R, :].rearrange("p (j d) -> p j d", j=J)
                for j in range(J):
                    t = J * b + j
                    last = v.scalar_tensor_tensor(z[:, j, :, b, :], pz[:, j, :].rearrange("p (c r) -> p c r", c=NC),
                                                  rs2[:, t:t + 1], rows[:, 4, :].rearrange("p (c r) -> p c r", c=NC),
                                                  ALU.mult, ALU.add)
                emptied(last)
            for q in range(8):
                wait_bank(dve, "convT", q)
                pc = bank(at["convT", q])[0:R, :].rearrange("p (j k b r) -> p j k b r", j=J, k=4, b=B)
                yv = y[:, :, :].rearrange("p (b j) (q k r) -> p j q k b r", j=J, q=8, r=CS)
                for j in range(J):
                    last = v.tensor_copy(yv[:, j, q], pc[:, j])
                emptied(last)
            for b in range(0, B, 2):
                wait_bank(dve, "yT", b)
                emptied(v.tensor_copy(yT[:, J * b:J * b + J, :], bank(at["yT", b])[:, 0:L].rearrange("p (j t) -> p j t", j=J)))
            for b in range(B):
                dve.wait_ge(S("hx_ready"), b + 1)
                wait_evac(dve, "out0", b)
                hv = h[:, J * b:J * b + J, :]
                me.did(v.tensor_tensor(out=hv, in0=hv, in1=x[:, J * b:J * b + J, :], op=ALU.add))
            me.settle()
            dve.wait_ge(S("iota2_ready"), 1)
            me.did(v.tensor_copy(em8[:, :], em8I[:, :]))
            me.then(v.tensor_copy(tileno[:, :], tileno[:, :].bitcast(I32)))
            for f in (0, 1):
                c = FFN[f]
                q = f"f{f}_"
                wait_bank(dve, f"b1T{f}")
                dve.wait_ge(S("bank_filled"), nfill[at["out0", B - 1]])
                w1v = big[:, c.w1_at:c.w1_at + c.E * c.wcols].rearrange("p (e w) -> p e w", e=c.E)
                emptied(v.tensor_copy(w1v[:, :, 128 * c.HC:], bank(at[f"b1T{f}", 0])[:, 0:c.E * c.HC].rearrange("p (e k) -> p e k", e=c.E)))
                for b in range(B):
                    stats(h, b, mv)
                me.settle()
                v.tensor_scalar(rs[:, :], mv[:, :, 1], EPS, None, ALU.add).then_inc(S("var_ready"), 1)
                invert(rs[:, :], rs[:, :], 5 + 2 * f)
                for b in range(B):
                    for t in range(J * b, J * b + J):
                        last = v.tensor_scalar(x[:, t, :], h[:, t, :], mv[:, t, 0:1], rs[:, t:t + 1], ALU.subtract, ALU.mult)
                    last.then_inc(S(f"x{f + 1}_ready"), 1)
                route(c, me, dve)
                for b in range(B):
                    wait_bank(dve, f"bias{f}", b)
                    hv = h[:, J * b:J * b + J, :]
                    emptied(v.tensor_tensor(out=hv, in0=bank(at[f"bias{f}", b])[0:R, :].rearrange("p (j d) -> p j d", j=J),
                                            in1=hv, op=ALU.add))
                dve.wait_ge(S("emptied_dve"), nth[at[f"bias{f}", B - 1]])
                expert_vector(dve, c, me)
                n = 0
                for t in range(NT):
                    for k in range(c.K):
                        dve.wait_ge(S(q + f"got{n % 8}"), 16 * (n // 8 + 1))
                        if k:
                            dve.wait_ge(S(q + "combined"), n)
                        v.scalar_tensor_tensor(h[:, t, :], got[n % 8], gate[f][:, k, t:t + 1], h[:, t, :],
                                               ALU.mult, ALU.add).then_inc(S(q + "combined"), 1)
                        n += 1
                dve.wait_ge(S(q + "combined"), n)
                if f == 0:
                    attention(me, dve)
            v.tensor_copy(cst[0:1, 128:129], valT[0:1, 0:1]).then_inc(S("done"), 1)

        @block.scalar
        def _(act):
            me = Steps(act, S("act_step"))
            s = nc.scalar

            def emptied(ins):
                ins.then_inc(S("emptied_act"), 1)

            def root(n, t):
                act.wait_ge(S("var_ready"), n)
                s.activation(t, t, ACT.Sqrt).then_inc(S("root_ready"), 1)
            act.wait_ge(S("exponents_ready"), 1)
            na, nb = NC * KA, NC * KB
            me.did(s.activation(mg[:, 0:na + nb], mg[:, 0:na + nb], ACT.Exp))
            act.wait_ge(S("phases_ready"), 1)
            me.settle()
            s.activation(ph, ph, ACT.Sin).then_inc(S("sines_ready"), 1)
            root(1, rs[:, :])
            root(2, rs[:, :])
            root(3, rs[:, :])
            root(4, rs2[:, :])
            for b in range(B):
                wait_bank(act, "xT", b)
                emptied(s.copy(xT[:, J * b:J * b + J, :], bank(at["xT", b])[:, 0:L].rearrange("p (j t) -> p j t", j=J)))
            act.wait_ge(S("hx_ready"), B)
            for q in range(8):
                wait_bank(act, "conv", q)
                emptied(s.copy(ys[:, q, 0:L], bank(at["conv", q])[:, 0:L]))
            for b in range(1, B, 2):
                wait_bank(act, "yT", b)
                emptied(s.copy(yT[:, J * b:J * b + J, :], bank(at["yT", b])[:, 0:L].rearrange("p (j t) -> p j t", j=J)))
            for b in range(B):
                wait_bank(act, "out0", b)
                emptied(s.activation(x[:, J * b:J * b + J, :], bank(at["out0", b])[0:R, :].rearrange("p (j d) -> p j d", j=J),
                                     ACT.Gelu))

            for f in (0, 1):
                c = FFN[f]
                root(5 + 2 * f, rs[:, :])
                for b in range(B):
                    wait_bank(act, f"rT{f}", b)
                    emptied(s.copy(xT[:, J * b:J * b + J, :], bank(at[f"rT{f}", b])[:, 0:L].rearrange("p (j t) -> p j t", j=J)))
                act.wait_ge(S("soft_in"), f + 1)
                m = mask_views(f)
                if f == 0:
                    me.did(s.activation(m["rest"][:, 0:256], m["rest"][:, 0:256], ACT.Exp))
                    s.activation(sm[:, 1, :], sm[:, 1, :], ACT.Exp).then_inc(S("soft_out"), 1)
                else:
                    me.did(s.activation(sm[:, 1, :], sm[:, 1, :], ACT.Exp))
                    s.activation(sm[:, 10:12, :], sm[:, 10:12, :], ACT.Exp).then_inc(S("soft_out"), 1)
                for b in range(B):
                    wait_bank(act, f"cT{f}", b)
                    emptied(s.copy(cT[0:c.E, :], bank(at[f"cT{f}", b])[0:c.E, 0:L]))
                expert_scalar(act, c)
                if f == 0:
                    root(6, rs[:, :])
                    for b in range(B):
                        wait_bank(act, "aT", b)
                        emptied(s.copy(xT[:, J * b:J * b + J, :], bank(at["aT", b])[:, 0:L].rearrange("p (j t) -> p j t", j=J)))
                    act.wait_ge(S("emptied_dve"), nth[at["kbar", 0]])
                    for b in range(B):
                        if b >= 2:
                            act.wait_ge(S("bank_filled"), nfill[at["score", 4 * (8 * (b - 2) + 7) + 3]])
                        for i in range(4):
                            wait_bank(act, "qk", 4 * b + i)
                            half = i % 2
                            dst, col = ((qs, bcol[:, half:half + 1]), (ks, kcol[:, half, b:b + 1]))[i // 2]
                            emptied(s.activation(dst[:, b % 2, half, :], bank(at["qk", 4 * b + i])[:, 0:L], ACT.Identity, bias=col))
                    wait_bank(act, "ss")
                    act.wait_ge(S("nmx_ready"), 1)
                    emptied(s.activation(att, bank(at["ss", 0])[0:64, 0:L], ACT.Exp, bias=nmx, scale=SCALE, accum_out=asum))

        @block.tensor
        def _(pe):
            t = nc.tensor
            order = iter(range(len(plan)))

            def use(what, i=0):
                n = next(order)
                while plan[n][0] == "skip":
                    n = next(order)
                assert plan[n][:2] == (what, i)
                if n >= 8 and nth[n - 8] and (what != "score" or i % 4 == 0):
                    m = n - 4 if what == "score" else n - 8
                    for eng in ("act", "dve"):
                        counts = [nth[k] for k in range(n - 8, m) if plan[k][2] == eng] if what == "score" else \
                            [nth[n - 8]] * (plan[n - 8][2] == eng)
                        if counts:
                            pe.wait_ge(S("emptied_" + eng), max(counts))
                return bank(n)

            def filled(ins):
                ins.then_inc(S("bank_filled"), 1)

            def attention_products():
                pe.wait_ge(S("ld_attn"), 16 * 19)
                pe.wait_ge(S("aconst_ready"), 1)
                p = use("wT")
                for w in range(4):
                    last = t.transpose(p[:, 128 * w:128 * w + 128], wraw[:, w, :], ident)
                filled(last)
                p = use("cols")
                for n, row in enumerate((brow2[:, 0, 0], brow2[:, 0, 1], brow2[:, 1, 0], brow2[:, 1, 1], borow[:, 0])):
                    last = t.matmul(p[:, n:n + 1], row, ones[0:1, 0:1], start=True, stop=True)
                filled(last)
                pe.wait_ge(S("hots_ready"), 1)
                p = use("cnt")
                for n in range(20):
                    last = t.matmul(p[0:R, 0:J], hot_lo[:, n, :], hot_hi[:, n, :], start=n == 0, stop=n == 19)
                filled(last)
                wait_evac(pe, "cnt")
                p = use("cntrow")
                for j in range(J):
                    last = t.matmul(p[0:1, R * j:R * j + R], cnt[:, j:j + 1], ident[0:R, 0:R], start=True, stop=True)
                filled(last)
                for b in range(B):
                    pe.wait_ge(S("xa_ready"), b + 1)
                    p = use("aT", b)
                    for j in range(J):
                        last = t.transpose(p[:, R * j:R * j + R], x[:, J * b + j, :], ident[0:R, 0:R])
                    filled(last)
                p = use("xbar")
                for b in range(B):
                    for j in range(J):
                        last = t.matmul(p[:, b:b + 1], x[:, J * b + j, :], cnt[:, j:j + 1], start=j == 0, stop=j == J - 1)
                filled(last)
                wait_evac(pe, "xbar")
                p = use("kbar")
                for half in range(2):
                    last = t.matmul(p[:, B * half:B * half + B], wkT[:, half, :], xbar, start=True, stop=True)
                filled(last)
                wait_evac(pe, "cntrow")
                wait_evac(pe, "aT", B - 1)

                def qk(b):
                    rhs = xT[:, J * b:J * b + J, :].rearrange("p j t -> p (j t)")
                    for i in range(4):
                        p = use("qk", 4 * b + i)
                        if i < 2:
                            filled(t.matmul(p[:, 0:L], wqT[:, i, :], rhs, start=True, stop=True))
                        else:
                            t.matmul(p[:, 0:L], wkT[:, i - 2, :], rhs, start=True, stop=False)
                            filled(t.matmul(p[:, 0:L], selrow, maskrow, start=False, stop=True))

                def scores(b, first, last_):
                    for g in range(8 * b + first, 8 * b + last_):
                        half, j = g // 4 % 2, g % 4
                        four = [use("score", 4 * g + i) for i in range(4)]
                        for i, p in enumerate(four):
                            w = slice(32 * i, 32 * i + 32)
                            last = t.matmul(p[0:R, 0:L], qs[w, b % 2, half, R * j:R * j + R], ks[w, b % 2, half, :],
                                            start=True, stop=True)
                        filled(last)
                qk(0)
                for b in range(B):
                    wait_evac(pe, "qk", 4 * b + 3)
                    scores(b, 0, 4)
                    if b < B - 1:
                        qk(b + 1)
                    scores(b, 4, 8)
                wait_evac(pe, "score", 4 * 8 * B - 1)
                p = use("MT")
                for j in range(J):
                    last = t.transpose(p[0:64, R * j:R * j + R], mcol[:, j, :], ident[0:R, 0:R])
                filled(last)
                pe.wait_ge(S("hot_ready"), 1)
                p = use("hotT")
                for j in range(J):
                    last = t.transpose(p[0:R, 64 * j:64 * j + 64], hot[:, R * j:R * j + R], ident[0:64, 0:64])
                filled(last)

                def rows_times(p, cols):
                    for b in range(B):
                        for j in range(J):
                            ins = t.matmul(p[:, H * b:H * b + H], x[:, J * b + j, :], cols[:, j, H * b:H * b + H],
                                           start=j == 0, stop=j == J - 1)
                    return ins
                wait_evac(pe, "hotT")
                filled(rows_times(use("xsel"), hotT))
                wait_evac(pe, "xsel")
                p = use("qsel")
                for half in range(2):
                    last = t.matmul(p[:, 64 * half:64 * half + 64], wqT[:, half, :], xsel, start=True, stop=True)
                filled(last)
                wait_evac(pe, "qsel")
                p = use("u")
                for half in range(2):
                    last = t.matmul(p[:, 0:64], wkn[:, half, :], qsel[:, half, :], start=half == 0, stop=half == 1)
                filled(last)
                wait_evac(pe, "u")
                p = use("ss")
                for b in range(B):
                    last = t.matmul(p[0:64, 0:L], uz[:, 64 * b:64 * b + 64], xT[:, J * b:J * b + J, :].rearrange("p j t -> p (j t)"),
                                    start=b == 0, stop=b == B - 1)
                filled(last)
                pe.wait_ge(S("att_ready"), 1)
                p = use("attT")
                for j in range(J):
                    last = t.transpose(p[0:R, 64 * j:64 * j + 64], att[:, R * j:R * j + R], ident[0:64, 0:64])
                filled(last)
                wait_evac(pe, "attT")
                filled(rows_times(use("xa"), attT))
                wait_evac(pe, "xa")
                p = use("ctx")
                filled(t.matmul(p[:, 0:64], wvT, xa, start=True, stop=True))
                pe.wait_ge(S("ctx_ready"), 1)
                for i in range(2):
                    p = use("outa", i)
                    for k in range(4):
                        t.matmul(p[0:R, D * k:D * k + D], ctxb[:, 4 * i + k, :], woT, start=True, stop=False)
                        last = t.matmul(p[0:R, D * k:D * k + D], ones[0:1, 0:R], borow[:, 1, :], start=False, stop=True)
                    filled(last)

            pe.wait_ge(S("ident_ready"), 1)
            pe.wait_ge(S("ids_float"), 1)
            p = use("tokens")
            t.transpose(p[0:R, 0:NT], ids32f[:, :], ident[0:NT, 0:NT])
            filled(t.transpose(p[0:R, 32:32 + NT], val32[:, :], ident[0:NT, 0:NT]))
            pe.wait_ge(S("ld_ssm"), 16 * 11)
            p = use("ssm")
            for q in range(5):
                last = t.transpose(p[:, NC * q:NC * q + NC], ssm5[:, q, :, :].rearrange("c r n -> c (r n)"), ident[0:NC, 0:NC])
            filled(last)
            pe.wait_ge(S("factors_ready"), 1)
            for q in range(4):
                p = use("lags", q)
                for c in range(8):
                    for r, e in enumerate((e1, e1r)):
                        w = KB * (2 * c + r)
                        last = t.matmul(p[0:KA, w:w + KB], e[:, 8 * q + c, :], e2[:, 8 * q + c, KB * r:KB * r + KB],
                                        start=True, stop=True)
                filled(last)
            pe.wait_ge(S("wg_ready"), 2)
            p = use("zbias")
            t.matmul(p[0:R, 0:D], cst[:, 512:512 + R], wsm[:, 0, :], start=True, stop=False)
            filled(t.matmul(p[0:R, 0:D], ones[0:1, 0:R], rowv[:, 0, :], start=False, stop=True))
            for b in range(B):
                pe.wait_ge(S("x0_ready"), b + 1)
                p = use("xT", b)
                for j in range(J):
                    last = t.transpose(p[:, R * j:R * j + R], x[:, J * b + j, :], ident[0:R, 0:R])
                filled(last)
            for b in range(B):
                wait_evac(pe, "xT", b)
                p = use("z", b)
                for j in range(J):
                    last = t.matmul(p[0:R, D * j:D * j + D], xT[:, J * b + j, :], wg[:, :], start=True, stop=True)
                filled(last)
            wait_evac(pe, "z", B - 1)
            for q in range(9):
                if q < 8:
                    pe.wait_ge(S(f"strip{q}"), 16)
                    p = use("conv", q)
                    for i in range(J):
                        for k in range(4):
                            c = 4 * q + k
                            last = t.matmul(p[32 * k:32 * k + 32, 0:L], z[:, i, c].rearrange("p b r -> p (b r)"),
                                            G[0:R, c, R * i:R * i + L][:, ::-1], start=i == 0, stop=i == J - 1)
                    filled(last)
                if q > 0:
                    wait_evac(pe, "conv", q - 1)
                    p = use("convT", q - 1)
                    for j in range(J):
                        last = t.transpose(p[0:R, D * j:D * j + D], ys[:, q - 1, R * j:R * j + R], ident)
                    filled(last)
            wait_evac(pe, "convT", 7)
            for b in range(B):
                p = use("yT", b)
                for j in range(J):
                    last = t.transpose(p[:, R * j:R * j + R], y[:, J * b + j, :], ident[0:R, 0:R])
                filled(last)
            for b in range(B):
                wait_evac(pe, "yT", b)
                p = use("out0", b)
                for j in range(J):
                    t.matmul(p[0:R, D * j:D * j + D], yT[:, J * b + j, :], wsm[:, 1, :], start=True, stop=False)
                    last = t.matmul(p[0:R, D * j:D * j + D], ones[0:1, 0:R], rowv[:, 1, :], start=False, stop=True)
                filled(last)

            for f in (0, 1):
                c = FFN[f]
                q = f"f{f}_"
                m = mask_views(f)
                pe.wait_ge(S("ld_router"), 128)
                p = use(f"b1T{f}")
                filled(t.transpose(p[:, 0:c.E * c.HC], b1r[0:c.E * c.HC, f, :], ident[0:c.E * c.HC, 0:c.E * c.HC]))
                for b in range(B):
                    pe.wait_ge(S(f"x{f + 1}_ready"), b + 1)
                    p = use(f"rT{f}", b)
                    for j in range(J):
                        last = t.transpose(p[:, R * j:R * j + R], x[:, J * b + j, :], ident[0:R, 0:R])
                    filled(last)
                for b in range(B):
                    wait_evac(pe, f"rT{f}", b)
                    p = use(f"router{f}", b)
                    for j in range(J):
                        w = p[0:R, c.wide * j:c.wide * j + c.wide]
                        last = t.matmul(w, xT[:, J * b + j, :], wr[:, f, 0:c.wide], start=True, stop=f == 1)
                        if f == 0:
                            last = t.matmul(w, ones[0:1, 0:R], brow[:, :], start=False, stop=True)
                    filled(last)
                pe.wait_ge(S(q + "counted"), 1)
                p = use(f"count{f}")
                total = m["upto"].rearrange("p (e t) -> p e t", t=NT)[:, :, NT - 1]
                t.matmul(p[0:R, 0:c.E], onesb[0:R, 0:R], total, start=True, stop=True)
                filled(t.matmul(p[0:c.E, 64:65], total, onesb[0:R, 0:1], start=True, stop=True))
                pe.wait_ge(S(q + "counted"), 2)
                for i in range(c.banks):
                    p = use(f"rank{f}", i)
                    n = c.E * NT // c.banks
                    t.matmul(p[0:R, 0:n], ltri[0:R, 0, 0:R], m["members"][:, n * i:n * i + n], start=True, stop=False)
                    filled(t.matmul(p[0:R, 0:n], onesb[0:R, 0:R], m["before"][:, n * i:n * i + n], start=False, stop=True))
                pe.wait_ge(S(q + "counted"), 3)
                p = use(f"ends{f}")
                filled(t.matmul(p[0:c.E, 0:1], ltri[0:c.E, 1, 0:c.E], ncolb[0:c.E, :], start=True, stop=True))
                pe.wait_ge(S(q + "counted"), 4)
                p = use(f"expert{f}")
                filled(t.matmul(p[0:1, 0:TAB], onesb[0:c.E, 0:1], m["pick"][0:c.E, 0:TAB // 2].bitcast(BF16), start=True, stop=True))
                gates = m["gates"].rearrange("p (e t) -> p e t", t=NT)
                for b in range(B):
                    p = use(f"cT{f}", b)
                    for j in range(J):
                        last = t.transpose(p[0:c.E, R * j:R * j + R], gates[:, :, J * b + j], ident[0:R, 0:R])
                    filled(last)
                    wait_evac(pe, f"cT{f}", b)
                    p = use(f"bias{f}", b)
                    for j in range(J):
                        last = t.matmul(p[0:R, D * j:D * j + D], cT[0:c.E, R * j:R * j + R], b2[0:c.E, f, :], start=True, stop=True)
                    filled(last)
                wait_evac(pe, f"bias{f}", B - 1)
                expert_tensor(pe, c)
                pe.wait_ge(S(q + "res_ready"), c.tiles + 2)
                pe.wait_ge(S(q + "rT_ready"), c.tiles + 4)
                pe.wait_ge(S(q + "hid_dve"), c.tiles + 3)
                pe.wait_ge(S(q + "hid_act"), c.tiles + 3)
                if f == 0:
                    attention_products()


_OUTS = [((8, 500, 128), 'float32')]


def kernel(**inputs):
    import numpy as _np
    import concourse.bacc as _bacc
    from concourse import mybir as _mybir
    from concourse.bass_utils import run_bass_kernel_spmd as _run

    nc = _bacc.Bacc("TRN2", target_bir_lowering=False, num_devices=1)
    arrays, args = {}, {}
    for name in inputs:
        arr = _np.ascontiguousarray(inputs[name])
        arrays[f"in_{name}_dram"] = arr
        args[name] = nc.dram_tensor(f"in_{name}_dram", arr.shape, _mybir.dt.from_np(arr.dtype), kind="ExternalInput").ap()
    shape, dtype = _OUTS[0]
    out = nc.dram_tensor("out_0_dram", shape, _mybir.dt.from_np(_np.dtype(dtype)), kind="ExternalOutput").ap()
    tower_kernel(nc, args, out)
    r = _run(nc, [arrays], core_ids=[0])
    return r.results[0]["out_0_dram"]
```

```python
from contextlib import ExitStack
import math

import concourse.bass as bass
from concourse import mybir

F32 = mybir.dt.float32
BF16 = mybir.dt.bfloat16
F16 = mybir.dt.float16
I32 = mybir.dt.int32
U32 = mybir.dt.uint32
ALU = mybir.AluOpType
ACT = mybir.ActivationFunctionType
AX = mybir.AxisListType

D = 128
B, L = 8, 500
R = 125
J = L // R
NT = B * J
NC, NS, CS = 32, 64, 4
KA, KB = 16, 32
KROW = 1024
GM = L + (J - 1) * R
EPS = 1e-5
MIDROW = 2048
MAGIC = 1.5 * 2.0 ** 23
H, DK, NSAMP = 8, 16, 2560


class Ffn:

    def __init__(self, n, groups, experts, picks, hidden, wide, w1, b1, w2, b2):
        self.n, self.G, self.E, self.K = n, groups, groups * experts, picks
        self.HC = hidden // 128
        self.wide = wide
        self.names = w1, b1, w2, b2
        full = (NT * R * picks + 127 * self.E) // 128
        self.tiles = -(-full // U) * U
        self.banks = self.E * NT // 512 or 1
        self.wcols = hidden + self.HC
        self.w1_at = 0 if n else W0_AT
        self.w2_at = self.w1_at + self.E * self.wcols


U = 4
W0_AT = 24576
FFN = [Ffn(0, 1, 8, 2, 512, 8, "L0_ffn_W1", "L0_ffn_b1", "L0_ffn_W2", "L0_ffn_b2"),
       Ffn(1, 8, 8, 4, 256, 72, "L1_ffn_W1", "L1_ffn_b1", "L1_ffn_W2", "L1_ffn_b2")]
W2_EARLY = 16
A_AT = FFN[1].w2_at + W2_EARLY * 256
BIGC = FFN[1].w2_at + FFN[1].E * 256
TAB = FFN[1].tiles + U


def ap(t, offset, dims):
    return bass.AP(tensor=t, offset=offset, ap=[list(d) for d in dims])


class Steps:

    def __init__(self, eng, sem):
        self.eng, self.sem, self.n = eng, sem, 0

    def did(self, instruction):
        self.n += 1
        instruction.then_inc(self.sem, 1)
        return self.n

    def then(self, instruction):
        self.did(instruction)
        self.settle()

    def settle(self):
        self.eng.wait_ge(self.sem, self.n)


def bank_plan():
    plan = [("tokens", 0, "dve"), ("ssm", 0, "dve")]
    plan += [("lags", i, "dve") for i in range(4)] + [("zbias", 0, "dve")]
    plan += [("xT", b, "act") for b in range(B)] + [("z", b, "dve") for b in range(B)]
    for g in range(9):
        if g < 8:
            plan += [("conv", g, "act")]
        if g > 0:
            plan += [("convT", g - 1, "dve")]
    plan += [("yT", b, "act" if b % 2 else "dve") for b in range(B)] + [("out0", b, "act") for b in range(B)]
    for f in (0, 1):
        plan += [(f"b1T{f}", 0, "dve")] + [(f"rT{f}", b, "act") for b in range(B)] + [(f"router{f}", b, "dve") for b in range(B)]
        plan += [(f"count{f}", 0, "dve")] + [(f"rank{f}", i, "dve") for i in range(FFN[f].banks)]
        plan += [(f"ends{f}", 0, "dve"), (f"expert{f}", 0, "dve"), (f"holder{f}", 0, "dve")]
        for b in range(B):
            plan += [(f"cT{f}", b, "act"), (f"bias{f}", b, "dve")]
        if f == 0:
            plan += [("wT", 0, "dve"), ("cols", 0, "dve"), ("cnt", 0, "dve"), ("cntrow", 0, "dve")]
            plan += [("aT", b, "act") for b in range(B)] + [("xbar", 0, "dve"), ("kbar", 0, "dve")]
            plan += [("skip", i, "") for i in range(-len(plan) % 4)]
            pair = lambda b: [("qk", 2 * b, "act"), ("qk", 2 * b + 1, "act"), ("skip", 0, ""), ("skip", 1, "")]
            plan += pair(0) + pair(1)
            for b in range(B):
                plan += [("score", 4 * (8 * b + i) + k, "dve") for i in range(4) for k in range(4)]
                if b < B - 2:
                    plan += pair(b + 2)
                plan += [("score", 4 * (8 * b + i) + k, "dve") for i in range(4, 8) for k in range(4)]
            plan += [(w, 0, "dve") for w in ("MT", "hotT", "xsel", "qsel", "u")] + [("ss", 0, "act")]
            plan += [(w, 0, "dve") for w in ("attT", "xa", "ctx")] + [("outa", i, "dve") for i in range(2)]
    return plan


def tower_kernel(nc, a, out):
    plan = bank_plan()
    at, evacs, nth, nfill = {}, {"act": 0, "dve": 0}, [], []
    for n, (what, i, eng) in enumerate(plan):
        if what == "skip":
            plan[n] = (what, i, plan[n - 8][2])
            nth.append(nth[n - 8])
            nfill.append(nfill[-1])
            continue
        whole = what != "score" or i % 4 == 3
        evacs[eng] += whole
        nth.append(evacs[eng] + (what == "score" and not whole))
        nfill.append((nfill[-1] if nfill else 0) + whole)
        at[what, i] = n

    with ExitStack() as ctx:
        sems = {}

        def S(name):
            if name not in sems:
                sems[name] = ctx.enter_context(nc.semaphore(name))
            return sems[name]

        def sb(name, shape, dt=F32):
            return ctx.enter_context(nc.sbuf_tensor(name, shape, dt))

        xrows = nc.dram_tensor("xrows", (R * NT, D), F32)
        results = [nc.dram_tensor(f"results{c.n}", (c.tiles * 128, D), F32) for c in FFN]
        kappa = nc.dram_tensor("kappa", (NC, KROW), F32)
        parts_d = nc.dram_tensor("parts", (B, 2, 3, D, L), BF16)

        ps = ctx.enter_context(nc.psum_tensor("ps", [128, 8, 512], F32))
        big = sb("big", [128, BIGC])
        h = sb("h", [R, NT, D])
        xbuf = sb("xbuf", [128, NT * D])
        x = xbuf[0:R, :].rearrange("p (t d) -> p t d", t=NT)
        tbuf = sb("tbuf", [128, NT * D])
        zbuf = sb("zbuf", [128, NT * D])
        xT = tbuf[:, 0:NT * R].rearrange("p (t r) -> p t r", t=NT)
        gw = tbuf[0:R, :].rearrange("p (t d) -> p t d", t=NT)
        vw = zbuf[0:R, :].rearrange("p (t d) -> p t d", t=NT)
        z = zbuf[0:R, :].rearrange("p (j c b r) -> p j c b r", j=J, c=NC, b=B)
        yT = zbuf[:, 0:NT * R].rearrange("p (t r) -> p t r", t=NT)
        cst = sb("cst", [128, 640])
        ident = cst[:, 0:128]
        G = big[:, 0:NC * GM].rearrange("p (c m) -> p c m", c=NC)
        wv = big[0:R, 0:512].rearrange("p (j d) -> p j d", j=J)
        bv = big[0:R, 512:1024].rearrange("p (j d) -> p j d", j=J)

        early = big[:, 12288:14336]
        ids32 = early[0:NT, 0:R].bitcast(I32)
        ids32f = early[0:NT, 128:128 + R]
        val32 = early[0:NT, 256:256 + R]
        idsT = sb("idsT", [R, NT], I32)
        valT = sb("valT", [R, NT])
        aside = big[:, NC * GM + 160:NC * GM + 1760]
        rows = aside[0:R, 0:5 * D].rearrange("p (q d) -> p q d", q=5)
        wsm = aside[:, 7 * D:9 * D].rearrange("p (q d) -> p q d", q=2)
        lnc = sb("lnc", [128, 4])
        rowv = aside[0:1, 9 * D:12 * D].rearrange("p (q d) -> p q d", q=3)
        ones = sb("ones", [128, 128])
        bnst = sb("bnst", [R, NT, 6])
        mv = sb("mv", [R, NT, 2])
        rs = sb("rs", [R, NT])
        rs2 = sb("rs2", [R, NT])
        ssm5 = early[0:NC, 384:384 + 10 * NS].rearrange("c (q r n) -> c q r n", q=5, r=2)
        dskip = sb("dskip", [KA, NC])
        sp5 = early[:, 1024:1024 + 5 * NC].rearrange("p (q c) -> p q c", q=5)
        cc = early[:, 1184:1184 + 2 * NC].rearrange("p (q c) -> p q c", q=2)
        alpha = sb("alpha", [128, 4])
        itI = sb("itI", [128, KA + KB], I32)
        itF = sb("itF", [128, KA + KB])
        NPH = 2 * NC * KA + NC * KB
        scr = big[:, 1024:1024 + 3 * NPH]
        ph, qn, mg = scr[:, 0:NPH], scr[:, NPH:2 * NPH], scr[:, 2 * NPH:3 * NPH]
        e1 = big[:, 7168:7168 + NC * KA].rearrange("p (c l) -> p c l", c=NC)
        e1r = big[:, 11776:11776 + NC * KA].rearrange("p (c l) -> p c l", c=NC)
        e2 = big[:, 7680:7680 + 2 * NC * KB].rearrange("p (c l) -> p c l", c=NC)
        kk = big[0:KA, 9728:9728 + 2 * NC * KB].rearrange("p (c l) -> p c l", c=NC)
        ltri = sb("ltri", [128, 2, 128], BF16)
        onesb = sb("onesb", [128, 128], BF16)
        tileno = sb("tileno", [128, TAB])
        tokno = sb("tokno", [R, NT])
        holder = sb("holder", [128, TAB], I32)
        em8I = sb("em8I", [R, 8], I32)
        em8 = sb("em8", [R, 8])
        wr = sb("wr", [128, 2, 72])
        brow = sb("brow", [1, 8])
        b2 = sb("b2", [64, 2, D])
        b1r = sb("b1r", [128, 2, 128])
        table = [sb(f"table{f}", [1, TAB], I32) for f in (0, 1)]
        place = [sb("place", [R, 4, NT], I32)] * 2
        gate = [sb("gate", [R, 4, NT])] * 2
        sm = sb("sm", [R, 12, NT])
        ntile = sb("ntile", [R, 3, 64])
        ncol = sb("ncol", [64, 2])
        ncolb = sb("ncolb", [64, 1], BF16)
        bbt = aside[0:R, 6 * D:7 * D]
        y = gw
        ys = xbuf[:, 0:8 * 512].rearrange("p (g t) -> p g t", g=8)
        wg = aside[:, 5 * D:6 * D]

        got = [tbuf[0:R, D * n:D * n + D] for n in range(8)]

        def mask_views(f):
            c = FFN[f]
            m = c.E * NT
            v = {}
            if f == 0:
                free, o = zbuf[0:R, :], 0
            else:
                free, o = big[0:R, W0_AT:W0_AT + 8192], 0
            def take(name, n, dt=F32):
                nonlocal o
                w = n if dt == F32 else n // 2
                t = free[:, o:o + w]
                v[name] = t if dt == F32 else t.bitcast(dt)
                o += w
            for name in ("members", "upto", "before", "chain"):
                take(name, m, BF16)
            take("lg", 256)
            take("rest", 512)
            for name in ("oh1", "oh2", "eh1", "eh2", "pick"):
                take(name, 512)
            if f == 0:
                v["slot"], v["gates"], v["tmp"] = (tbuf[0:R, 256 * n:256 * n + 256] for n in range(3))
            else:
                v["le"], v["tmp"] = zbuf[0:R, 0:2048], zbuf[0:R, 2048:4096]
                v["slot"], v["gates"] = tbuf[0:R, 0:2048], tbuf[0:R, 2048:4096]
            return v
        cT = cst[0:64, 128:128 + L]

        def hot_views(f):
            base = zbuf[0:R, 0:1792] if f else tbuf[0:R, 768:2560]
            return (base[:, 0:512].bitcast(F16).rearrange("p (o j n) -> p o j n", o=2, j=J),
                    base[:, 512:512 + 4 * TAB].bitcast(F16).rearrange("p (o j n) -> p o j n", o=2, j=J),
                    base[:, 1280:1792].rearrange("p (o j n) -> p o j n", o=2, j=J // 2))

        tail = big[:, A_AT:W0_AT]
        tail_at = 0

        def take(n, rows_=128):
            nonlocal tail_at
            t = tail[0:rows_, tail_at:tail_at + n]
            tail_at += n
            assert tail_at <= W0_AT - A_AT
            return t
        uz = take(512)
        wqT, wkT, wvT, woT = (take(128) for _ in range(4))
        wraw = take(512).rearrange("p (w d) -> p w d", w=4)
        arow = take(512, 1).rearrange("p (w d) -> p w d", w=4)
        own16 = take(8)
        bcol = take(3)
        kcol = take(8)
        sidx = take(20)
        sidf, shi, slo = take(20), take(20), take(20)
        i500 = take(500)
        hot_lo = tbuf[:, 2816:4066].bitcast(BF16).rearrange("p (s l) -> p s l", s=20)
        hot_hi = take(40).bitcast(BF16).rearrange("p (s l) -> p s l", s=20)
        cnt = take(J, R)
        maskrow = take(250, 1).bitcast(BF16)
        xbar = take(B)
        q_parts, k_parts = (0, 0, 0, 1, 1, 2), (0, 1, 2, 0, 1, 0)
        SROWS = 6 * DK + 1
        stack = big[:, W0_AT:W0_AT + 2 * 2 * H * L // 2].bitcast(BF16).rearrange("p (w o h t) -> p w o h t", w=2, o=2, h=H)
        parts = zbuf[:, 256:1756].bitcast(BF16).rearrange("p (w n t) -> p w n t", w=2, n=3)
        qk_rest = zbuf[:, 1756:2756].rearrange("p (w t) -> p w t", w=2)
        mcol = zbuf[0:R, 0:256].rearrange("p (j n) -> p j n", j=J)
        mrow = zbuf[0:64, 256:256 + L]
        hot = zbuf[0:64, 768:768 + L]
        hotT = zbuf[0:R, 1280:1280 + 256].rearrange("p (j n) -> p j n", j=J)
        xsel = zbuf[:, 1536:1600]
        qsel = zbuf[:, 1600:1664]
        att = zbuf[0:64, 1728:1728 + L]
        attT = zbuf[0:R, 2240:2240 + 256].rearrange("p (j n) -> p j n", j=J)
        xa = zbuf[:, 2496:2560]
        cmul, ctxv = zbuf[:, 2560:2624], zbuf[:, 2624:2632]
        ctxb = zbuf[:, 2632:2632 + B * R].rearrange("p (b r) -> p b r", b=B)
        m8 = zbuf[0:64, 3640:3648]
        i8 = zbuf[0:64, 3648:3656].bitcast(U32)
        i8f = zbuf[0:64, 3656:3657]
        nmx, asum = zbuf[0:64, 3660:3661], zbuf[0:64, 3661:3662]
        SCALE = 1.0 / math.sqrt(DK)

        class Ring:
            def __init__(self, c):
                o = 0
                def take(n, w):
                    nonlocal o
                    r = [zbuf[:, o + w * i:o + w * i + w] for i in range(n)]
                    o += n * w
                    return r
                self.rows, self.rT = take(U, 128), take(U, 128)
                self.w1 = [tbuf[:, c.wcols * i:c.wcols * i + c.wcols] for i in range(U)]
                self.hid, self.res = take(2, 128 * c.HC), take(U, 128)
                self.res2 = [zbuf[:, o - 256 * n:o - 256 * n + 256].rearrange("p (o d) -> p o d", o=2) for n in (2, 1)]

        block = ctx.enter_context(nc.Block())

        def bank(n):
            return ps[:, n % 8, :]

        def wait_bank(eng, what, i=0):
            eng.wait_ge(S("bank_filled"), nfill[at[what, i]])

        def wait_evac(eng, what, i=0):
            n = at[what, i]
            eng.wait_ge(S("emptied_" + plan[n][2]), nth[n])

        def load_weights(eng, c):
            w1, b1, w2, _ = c.names
            g = "g e" if c.n else "e"
            src = a[w1].rearrange("g e d h -> (g e) d h") if c.n else a[w1]
            src2 = a[w2].rearrange("g e h d -> (g e) h d") if c.n else a[w2]
            w1v = big[:, c.w1_at:c.w1_at + c.E * c.wcols].rearrange("p (e w) -> p e w", e=c.E)
            w2v = big[:, c.w2_at:c.w2_at + c.E * c.HC * D].rearrange("p (e k d) -> p e k d", e=c.E, k=c.HC)
            hid = 128 * c.HC
            step = 8 if c.n else 4
            early = W2_EARLY if c.n else c.E
            for e in range(0, c.E, step):
                eng.dma_start(w1v[:, e:e + step, 0:hid], src[e:e + step].rearrange("e d h -> d e h")).then_inc(S(f"w{c.n}_ld"), 16)
                if e < early:
                    for i in range(e, e + step):
                        eng.dma_start(w2v[:, i], src2[i].rearrange("(k h) d -> h k d", k=c.HC)).then_inc(S(f"w{c.n}_ld"), 16)

        def weight_loads(c):
            return c.E // (8 if c.n else 4) + (W2_EARLY if c.n else 8)

        def tile_experts(eng, c, tau):
            packed = eng.value_load(table[c.n][0:1, bass.ds(tau, 1)], min_val=0, max_val=c.E ** U - 1)
            bits = c.E.bit_length() - 1
            return [(packed >> bits * u) & (c.E - 1) for u in range(U)]

        def store_rows(sp, c):
            sp.wait_ge(S(f"x{c.n + 1}_ready"), B)
            for lo, hi in ((0, 112), (112, R)):
                sp.dma_start(xrows[:, :].rearrange("(p t) d -> p (t d)", p=R)[lo:hi], xbuf[lo:hi, :]).then_inc(S(f"x{c.n + 1}_st"), 16)

        def expert_dma(sp, c):
            p = f"f{c.n}_"
            if c.n:
                w2v = big[:, c.w2_at:c.w2_at + c.E * c.HC * D].rearrange("p (e k d) -> p e k d", e=c.E, k=c.HC)
                src2 = a[c.names[2]].rearrange("g e h d -> (g e) h d")
                sp.wait_ge(S("emptied_dve"), nth[at["outa", 1]])
                for i in range(W2_EARLY, c.E):
                    if i == (W0_AT - c.w2_at) // 256:
                        sp.wait_ge(S("f1_placed"), 1)
                    sp.dma_start(w2v[:, i], src2[i].rearrange("(k h) d -> h k d", k=c.HC)).then_inc(S("w1_late"), 16)

            for u in range(0, U, 2):
                    sp.wait_ge(S(p + f"res_st{u}"), 16 * (c.tiles // U + 1))
            sp.wait_ge(S(p + "w1_ready"), c.tiles + 5)
            sp.wait_ge(S(p + "rT_ready"), c.tiles + 4)
            sp.wait_ge(S(p + "hid_dve"), c.tiles + 3)
            sp.wait_ge(S(p + "hid_act"), c.tiles + 3)
            sp.sem_inc(S(p + "results_in"), 1)

        def expert_vector(dve, c, me):
            p, ring, v = f"f{c.n}_", Ring(c), nc.vector
            w1v = big[:, c.w1_at:c.w1_at + c.E * c.wcols].rearrange("p (e w) -> p e w", e=c.E)
            half = c.HC // 2
            hid = 128 * c.HC

            def stage(e, u):
                v.tensor_copy(ring.w1[u % U], w1v[:, bass.ds(e, 1), :].rearrange("p e w -> p (e w)")).then_inc(S(p + "w1_ready"), 1)

            def turn(u):
                v.tensor_copy(ring.rT[u % U], ps[:, u % 2, 0:128]).then_inc(S(p + "rT_ready"), 1)

            def rectify(u):
                w = ring.w1[u % U]
                for k in range(half, c.HC):
                    last = v.tensor_scalar(ring.hid[u % 2][:, 128 * k:128 * k + 128], ps[:, 4 + u % 2, 128 * k:128 * k + 128],
                                           w[:, hid + k:hid + k + 1], 0.0, ALU.add, ALU.max)
                last.then_inc(S(p + "hid_dve"), 1)

            dve.sem_inc(S(p + "w1_ready"), 2)
            dve.sem_inc(S(p + "rT_ready"), 2)
            dve.sem_inc(S(p + "hid_dve"), 2)
            dve.wait_ge(S(f"w{c.n}_ld"), 16 * weight_loads(c))
            experts = tile_experts(dve, c, 0)
            dve.wait_ge(S("bank_filled"), nfill[at[f"bias{c.n}", B - 1]])
            stage(experts[0], 0)
            dve.wait_ge(S(p + "turned"), 1)
            turn(0)
            stage(experts[1], 1)
            dve.wait_ge(S(p + "hid_filled"), 3)
            rectify(0)
            dve.wait_ge(S(p + "turned"), 2)
            turn(1)
            stage(experts[2], 2)
            with dve.Fori(0, c.tiles // U) as i:
                experts = tile_experts(dve, c, i * U + 3)
                for u in range(U):
                    dve.wait_ge(S(p + "hid_filled"), i * U + (u + 4))
                    turn(u + 2)
                    rectify(u + 1)
                    stage(experts[u], u + 3)

        def expert_scalar(act, c):
            p, ring, s = f"f{c.n}_", Ring(c), nc.scalar
            half, hid = c.HC // 2, 128 * c.HC

            def rectify(u):
                w = ring.w1[u % U]
                for k in range(half):
                    last = s.activation(ring.hid[u % 2][:, 128 * k:128 * k + 128], ps[:, 2 + u % 2, 128 * k:128 * k + 128],
                                        ACT.Relu, bias=w[:, hid + k:hid + k + 1])
                last.then_inc(S(p + "hid_act"), 1)
            act.sem_inc(S(p + "hid_act"), 2)
            act.sem_inc(S(p + "res_ready"), 2)
            for u in range(0, U, 2):
                act.sem_inc(S(p + f"res_st{u}"), 16)
            act.wait_ge(S(p + "hid_filled"), 3)
            act.wait_ge(S(p + "w1_ready"), 3)
            rectify(0)
            with act.Fori(0, c.tiles // U) as i:
                for u in range(U):
                    act.wait_ge(S(p + "hid_filled"), i * U + (u + 4))
                    rectify(u + 1)
                    act.wait_ge(S(p + "res_filled"), i * U + (u + 3))
                    if u % 2 == 0:
                        act.wait_ge(S(p + f"res_st{u}"), i * 16 + 16)
                    s.copy(ring.res[u], ps[:, 6 + u % 2, 0:D]).then_inc(S(p + "res_ready"), 1)
                    if u % 2 == 1:
                        act.wait_ge(S(p + "res_ready"), i * U + (u + 3))
                        act.dma_start(results[c.n][:, :].rearrange("(n o p) d -> n p o d", p=128, o=2)[bass.ds(i * (U // 2) + u // 2, 1)]
                                      .rearrange("n p o d -> p (n o) d"),
                                      ring.res2[u // 2]).then_inc(S(p + f"res_st{u - 1}"), 16)

        def expert_tensor(pe, c):
            p, ring, t = f"f{c.n}_", Ring(c), nc.tensor
            w2v = big[:, c.w2_at:c.w2_at + c.E * c.HC * D].rearrange("p (e k d) -> p e k d", e=c.E, k=c.HC)

            def turn(u):
                t.transpose(ps[:, u % 2, 0:128], ring.rows[u % U], ident).then_inc(S(p + "turned"), 1)

            def first(u):
                for k in range(c.HC):
                    last = t.matmul(ps[:, (2 if k < c.HC // 2 else 4) + u % 2, 128 * k:128 * k + 128], ring.w1[u % U][:, 128 * k:128 * k + 128],
                                    ring.rT[u % U], start=True, stop=True)
                last.then_inc(S(p + "hid_filled"), 1)

            def second(e, u):
                for k in range(c.HC):
                    last = t.matmul(ps[:, 6 + u % 2, 0:D], ring.hid[u % 2][:, 128 * k:128 * k + 128],
                                    w2v[:, bass.ds(e, 1), k, :].rearrange("p e d -> p (e d)"), start=k == 0, stop=k == c.HC - 1)
                last.then_inc(S(p + "res_filled"), 1)

            pe.sem_inc(S(p + "hid_filled"), 2)
            pe.sem_inc(S(p + "res_filled"), 2)
            pe.wait_ge(S(p + "row_ld0"), 16)
            turn(0)
            pe.wait_ge(S(p + "row_ld1"), 16)
            turn(1)
            pe.wait_ge(S(p + "w1_ready"), 3)
            pe.wait_ge(S(p + "rT_ready"), 3)
            first(0)
            if c.n:
                pe.wait_ge(S("w1_late"), 16 * (c.E - W2_EARLY))
            with pe.Fori(0, c.tiles // U) as i:
                experts = tile_experts(pe, c, i * U)
                for u in range(U):
                    pe.wait_ge(S(p + f"row_ld{(u + 2) % U}"), i * 16 + (16 if u < 2 else 32))
                    turn(u + 2)
                    pe.wait_ge(S(p + "rT_ready"), i * U + (u + 4))
                    first(u + 1)
                    pe.wait_ge(S(p + "hid_dve"), i * U + (u + 3))
                    pe.wait_ge(S(p + "hid_act"), i * U + (u + 3))
                    second(experts[u], u)

        def attention_dma(sp):
            sp.wait_ge(S("emptied_dve"), nth[at["cntrow", 0]])
            every = stack[6 * DK:SROWS].rearrange("p w o h t -> p w (o h t)")
            sp.dma_start(every[:, 0, :].rearrange("p (n t) -> p n t", t=R),
                         onesb[0:1, 0:R].unsqueeze(1).broadcast_to([1, 2 * H * J, R])).then_inc(S("mask_in"), 16)
            sp.dma_start(every[:, 1, :].rearrange("p (n t) -> p n t", t=L),
                         maskrow.unsqueeze(1).broadcast_to([1, 2 * H, L])).then_inc(S("mask_in"), 16)
            for b in range(B):
                sp.wait_ge(S("parts_ready"), b + 1)
                sp.dma_start(ap(parts_d, b * 6 * D * L, [[L, D], [D * L, 6], [1, L]]),
                             parts.rearrange("p w n t -> p (w n) t")).then_inc(S("parts_st"), 16)
                sp.wait_ge(S("parts_st"), 16 * (b + 1))
                if b >= 2:
                    sp.wait_ge(S("bank_filled"), nfill[at["score", 4 * (8 * (b - 2) + 7) + 3]])
                for w, order in enumerate((q_parts, k_parts)):
                    for g, n in enumerate(order):
                        sp.dma_start(stack[DK * g:DK * g + DK, w, b % 2],
                                     ap(parts_d, (b * 6 + w * 3 + n) * D * L, [[L, DK], [DK * L, H], [1, L]])
                                     ).then_inc(S(f"stack{b % 2}"), 16)

        @block.sync
        def _(sp):
            def load(dst, src, sem):
                sp.dma_start(dst, src).then_inc(S(sem), 16)
            load(ids32[:, :], a["x"].rearrange("b (j p) -> (b j) p", p=R), "ld_ids")
            load(val32[:, :], a["fside_BS_value"].rearrange("b (j p) -> (b j) p", p=R), "ld_ids")
            for q, n in enumerate(["Lambda_re", "Lambda_im", "C_re", "C_im", "Bmat"]):
                for r in range(2):
                    load(ssm5[:, q, r, :], a["L0_attn_" + n], "ld_ssm")
            sp.wait_ge(S("dskip_zero"), 1)
            load(dskip[KA - 1:KA, :], a["L0_attn_Dvec"].rearrange("(o n) -> o n", o=1), "ld_ssm")
            load(wv, a["L0_tok_w_val"].rearrange("(j p) d -> p j d", p=R), "ld_val")
            load(bv, a["L0_tok_b_val"].rearrange("(j p) d -> p j d", p=R), "ld_val")
            for q, n in enumerate(["gamma_g", "beta_g", "gamma_v", "beta_v"]):
                load(rows[:, q, :], a["L0_tok_" + n].partition_broadcast(R), "ld_val")
            load(wsm[:, 0, :], a["L0_attn_Win"], "ld_w")
            load(wsm[:, 1, :], a["L0_attn_Wout"], "ld_w")
            load(lnc[:, 0:1], a["L0_attn_ln_gamma"].rearrange("(d o) -> d o", o=1), "ld_w")
            load(lnc[:, 1:2], a["L0_attn_ln_beta"].rearrange("(d o) -> d o", o=1), "ld_w")
            load(rowv[:, 0, :], a["L0_attn_bin_"].rearrange("(o d) -> o d", o=1), "ld_w")
            load(rowv[:, 1, :], a["L0_attn_bout"].rearrange("(o d) -> o d", o=1), "ld_w")
            load(wr[:, 0, 0:8], a["L0_ffn_Wr"], "ld_router")
            load(wr[:, 1, 0:8], a["L1_ffn_g1"], "ld_router")
            load(wr[:, 1, 8:72].rearrange("p (g e) -> p g e", g=8), a["L1_ffn_g2"].rearrange("g d e -> d g e"), "ld_router")
            load(brow[:, :], a["L0_ffn_br"].rearrange("(o n) -> o n", o=1), "ld_router")
            load(b1r[0:32, 0, :], a["L0_ffn_b1"].rearrange("e (k h) -> (e k) h", k=4), "ld_router")
            load(b1r[:, 1, :], a["L1_ffn_b1"].rearrange("g e (k h) -> (g e k) h", k=2), "ld_router")
            load(b2[0:8, 0, :], a["L0_ffn_b2"], "ld_router")
            load(b2[:, 1, :], a["L1_ffn_b2"].rearrange("g e d -> (g e) d"), "ld_router")
            sp.wait_ge(S("lags_ready"), 1)
            sp.dma_start(ap(kappa, KROW // 2, [[KB, KA], [KROW, NC], [1, KB]]), kk[:, :, 0:KB]).then_inc(S("kappa_st"), 16)
            sp.dma_start(ap(kappa, 0, [[KB, KA], [KROW, NC], [1, KB]]), kk[:, :, KB:2 * KB]).then_inc(S("kappa_st"), 16)
            sp.wait_ge(S("kappa_st"), 32)
            sp.wait_ge(S("values_read"), 1)
            for q in range(8):
                sp.dma_start(G[:, 4 * q:4 * q + 4, :],
                             ap(kappa, 4 * q * KROW + KROW // 2 - L, [[1, 128], [KROW, 4], [1, GM]])
                             ).then_inc(S(f"strip{q}"), 16)
            sp.wait_ge(S("bank_filled"), nfill[at["out0", B - 1]])
            load_weights(sp, FFN[0])
            for w, n in enumerate("qkvo"):
                load(wraw[:, w, :], a["L1_attn_W" + n], "ld_attn")
                load(arow[:, w, :], a["L1_attn_b" + n].rearrange("(o d) -> o d", o=1), "ld_attn")
            load(sidx.bitcast(I32), a["L1_attn_samp_idx"].rearrange("(p s) -> p s", p=128), "ld_attn")
            load_weights(sp, FFN[1])
            for f in (0, 1):
                store_rows(sp, FFN[f])
                expert_dma(sp, FFN[f])
                if f == 0:
                    attention_dma(sp)
            for b in range(B):
                sp.wait_ge(S("f1_combined"), FFN[1].K * J * (b + 1))
                sp.dma_start(out[b:b + 1].rearrange("b (j p) d -> p (b j) d", p=R), h[:, J * b:J * b + J, :]).then_inc(S("out_st"), 16)
            sp.wait_ge(S("out_st"), 16 * B)

        @block.gpsimd
        def _(pool):
            me = Steps(pool, S("pool_step"))
            gp = nc.gpsimd
            gp.memset(dskip[:, :], 0.0).then_inc(S("dskip_zero"), 1)
            me.did(gp.memset(ones[:, :], 1.0))
            me.then(gp.memset(ident, 0.0))
            gp.affine_select(out=ident, in_=ident, compare_op=ALU.not_equal, fill=1.0, base=0,
                             pattern=[[-1, 128]], channel_multiplier=1).then_inc(S("ident_ready"), 1)
            me.did(gp.iota(itI[:, 0:KA], pattern=[[KB, KA]], base=0, channel_multiplier=0))
            me.then(gp.iota(itI[:, KA:KA + KB], pattern=[[1, KB]], base=0, channel_multiplier=0))
            for col, top, bot in ((0, math.pi / 2, 0.0), (1, 0.0, -math.pi / 2), (2, math.pi / 2, math.pi)):
                me.then(gp.memset(alpha[0:64, col:col + 1], top))
                me.then(gp.memset(alpha[64:128, col:col + 1], bot))
            gp.memset(alpha[:, 3:4], 0.0).then_inc(S("iota_ready"), 1)
            me.did(gp.memset(onesb[:, :], 1.0))
            me.then(gp.memset(ltri[:, :, :], 1.0))
            for k, op in ((0, ALU.is_gt), (1, ALU.is_ge)):
                me.then(gp.affine_select(out=ltri[:, k, :], in_=ltri[:, k, :], compare_op=op, fill=0.0, base=0,
                                         pattern=[[1, 128]], channel_multiplier=-1))
            me.did(gp.iota(tokno[:, :].bitcast(I32), pattern=[[1, NT]], base=-MIDROW, channel_multiplier=NT))
            me.did(gp.iota(tileno[:, :].bitcast(I32), pattern=[[1, TAB]], base=0, channel_multiplier=0))
            gp.iota(em8I[:, :], pattern=[[1, 8]], base=-8, channel_multiplier=0).then_inc(S("iota2_ready"), 1)
            pool.wait_ge(S("ids_ready"), 1)
            for t in range(NT):
                gp.indirect_dma_start(gw[:, t, :], None, a["L0_tok_emb_table"],
                                      bass.IndirectOffsetOnAxis(ap=idsT[:, t:t + 1], axis=0)
                                      ).then_inc(S(f"gathered{t // J}"), 16)
            pool.wait_ge(S("ld_val"), 96)
            me.then(gp.tensor_tensor(out=bbt[:, :], in0=rows[:, 1, :], in1=rows[:, 3, :], op=ALU.add))
            for b in range(B):
                pool.wait_ge(S("vn_ready"), b + 1)
                v = vw[:, J * b:J * b + J, :]
                me.then(gp.tensor_tensor(out=v, in0=v, in1=rows[:, 2:3, :].broadcast_to([R, J, D]), op=ALU.mult))
                gp.tensor_tensor(out=v, in0=v, in1=bbt[:, :].unsqueeze(1).broadcast_to([R, J, D]),
                                 op=ALU.add).then_inc(S("vb_ready"), 1)
            for b in range(B):
                pool.wait_ge(S("x0_ready"), b + 1)
                v = h[:, J * b:J * b + J, :]
                gp.tensor_tensor(out=v, in0=v, in1=x[:, J * b:J * b + J, :], op=ALU.add).then_inc(S("hx_ready"), 1)

            pool.wait_ge(S("bank_filled"), nfill[at["out0", B - 1]])
            me.did(gp.memset(uz, 0.0))
            me.did(gp.iota(i500.bitcast(I32), pattern=[[1, L]], base=0, channel_multiplier=0))
            me.then(gp.memset(own16, 1.0))
            me.then(gp.affine_select(out=own16, in_=own16, compare_op=ALU.is_ge, fill=0.0, base=0,
                                     pattern=[[-DK, H]], channel_multiplier=1))
            gp.affine_select(out=own16, in_=own16, compare_op=ALU.is_ge, fill=0.0, base=DK - 1,
                             pattern=[[DK, H]], channel_multiplier=-1).then_inc(S("aconst_ready"), 1)

            for f in (0, 1):
                c = FFN[f]
                q = f"f{f}_"
                pool.wait_ge(S(q + "placed"), 1)
                hot_slot = hot_views(f)[0]
                for g in range(c.K * B):
                    if g >= 2:
                        pool.wait_ge(S(q + "hots_used"), g - 1)
                    for j in range(J // 2):
                        t = g % B * J + j
                        last = gp.tensor_scalar(hot_slot[:, g % 2, j], tileno[0:R, 0:128], sm[:, 8 + g // B, t:t + 1], None, ALU.is_equal)
                    last.then_inc(S(q + "hot_slot"), 1)
                pool.wait_ge(S(f"x{f + 1}_st"), 32)
                wait_evac(pool, f"holder{f}")
                ring = Ring(c)
                for tau in range(c.tiles + 2):
                    if tau >= U:
                        pool.wait_ge(S(q + "turned"), tau - U + 1)
                    gp.indirect_dma_start(ring.rows[tau % U], None, xrows[:, :],
                                          bass.IndirectOffsetOnAxis(ap=holder[:, tau:tau + 1], axis=0)
                                          ).then_inc(S(q + f"row_ld{tau % U}"), 16)
                pool.wait_ge(S(q + "results_in"), 1)
                n = 0
                for t in range(NT):
                    for k in range(c.K):
                        if n >= 8:
                            pool.wait_ge(S(q + "combined"), n - 7)
                        gp.indirect_dma_start(got[n % 8], None, results[f][:, :],
                                              bass.IndirectOffsetOnAxis(ap=place[f][:, k, t:t + 1], axis=0)
                                              ).then_inc(S(q + f"got{n % 8}"), 16)
                        n += 1
                if f == 0:
                    for b in range(B):
                        pool.wait_ge(S("part1_ready"), b + 1)
                        gp.tensor_tensor(out=qk_rest, in0=qk_rest, in1=parts[:, :, 0, :], op=ALU.subtract).then_inc(S("rest_ready"), 1)
                        pool.wait_ge(S("part2_ready"), b + 1)
                        pool.wait_ge(S("rest_ready"), b + 1)
                        gp.tensor_tensor(out=parts[:, :, 2, :], in0=qk_rest, in1=parts[:, :, 1, :], op=ALU.subtract).then_inc(S("parts_ready"), 1)

        @block.vector
        def _(dve):
            me = Steps(dve, S("dve_step"))
            v = nc.vector

            def emptied(ins):
                ins.then_inc(S("emptied_dve"), 1)

            def stats(src, b, mean_var):
                for t in range(J * b, J * b + J):
                    me.did(v.bn_stats(bnst[:, t, :], src[:, t, :]))
                me.settle()
                for t in range(J * b, J * b + J):
                    me.did(v.bn_aggr(mean_var[:, t, :], bnst[:, t, :]))

            def invert(root, dst, base):
                dve.wait_ge(S("root_ready"), base)
                me.then(v.reciprocal(dst, root))

            def route(c, me, dve):
                f, m = c.n, mask_views(c.n)
                TT, TS = v.tensor_tensor, v.tensor_scalar
                q = f"f{f}_"
                e8 = em8[:, :]

                def v4(name, n):
                    return m[name][:, 0:n * 256].rearrange("p (i e t) -> p i e t", i=n, e=8)

                def small(k, n):
                    return sm[:, k:k + n, :]

                def over_e(t, n):
                    return t.unsqueeze(2).broadcast_to([R, n, 8, NT])

                def e8_over(n):
                    return e8.unsqueeze(1).unsqueeze(3).broadcast_to([R, n, 8, NT])

                def top(src, hot, n, best, index):
                    me.then(v.tensor_reduce(out=best, in_=src.rearrange("p i e t -> p i t e"), axis=AX.X, op=ALU.max))
                    me.then(TT(out=hot, in0=src, in1=over_e(best, n), op=ALU.is_equal))
                    me.then(TT(out=hot, in0=hot, in1=e8_over(n), op=ALU.mult))
                    me.then(v.tensor_reduce(out=index, in_=hot.rearrange("p i e t -> p i t e"), axis=AX.X, op=ALU.min))
                    me.then(TT(out=hot, in0=over_e(index, n), in1=e8_over(n), op=ALU.is_equal))

                def without(src, hot, flat):
                    me.then(v.scalar_tensor_tensor(flat(src), flat(hot), -1e30, flat(src), ALU.mult, ALU.add))

                def flat(t):
                    return t.rearrange("p i e t -> p (i e t)")

                for b in range(B):
                    wait_bank(dve, f"router{f}", b)
                    src = bank(at[f"router{f}", b])[0:R, 0:J * c.wide].rearrange("p (j e) -> p e j", j=J)
                    ins = v.tensor_copy(m["lg"].rearrange("p (e t) -> p e t", e=8)[:, :, J * b:J * b + J], src[:, 0:8, :])
                    if f:
                        me.did(ins)
                        ins = v.tensor_copy(m["le"].rearrange("p (e t) -> p e t", e=64)[:, :, J * b:J * b + J], src[:, 8:72, :])
                    emptied(ins)
                dve.wait_ge(S("emptied_dve"), nth[at[f"router{f}", B - 1]])
                lg = v4("lg", 1)
                oh = v4("oh1", 1), v4("oh2", 1)
                if f == 0:
                    me.did(v.tensor_copy(m["rest"][:, 0:256], m["lg"]))
                    top(lg, oh[0], 1, small(0, 1), small(2, 1))
                    without(lg, oh[0], flat)
                    top(lg, oh[1], 1, small(1, 1), small(2, 1))
                    r = m["rest"][:, 0:256].rearrange("p (i e t) -> p i e t", i=1, e=8)
                    me.did(TT(out=r, in0=r, in1=over_e(small(0, 1), 1), op=ALU.subtract))
                    TT(out=small(1, 1), in0=small(1, 1), in1=small(0, 1), op=ALU.subtract).then_inc(S("soft_in"), 1)
                    dve.wait_ge(S("soft_out"), 1)
                    me.then(v.tensor_reduce(out=small(2, 1), in_=r.rearrange("p i e t -> p i t e"), axis=AX.X, op=ALU.add))
                    me.then(v.reciprocal(gate[0][:, 0:1, :], small(2, 1)))
                    me.did(TT(out=gate[0][:, 1:2, :], in0=small(1, 1), in1=gate[0][:, 0:1, :], op=ALU.mult))
                    me.then(TT(out=flat(v4("eh1", 1)), in0=flat(oh[0]), in1=flat(oh[1]), op=ALU.add))
                    me.did(v.tensor_copy(m["members"], flat(v4("eh1", 1))))
                    for k in range(2):
                        me.did(TT(out=v4("eh1", 2)[:, k:k + 1], in0=oh[k], in1=over_e(gate[0][:, k:k + 1, :], 1), op=ALU.mult)) if k else \
                            me.then(TT(out=v4("pick", 1), in0=oh[0], in1=over_e(gate[0][:, 0:1, :], 1), op=ALU.mult))
                    me.settle()
                    me.then(TT(out=m["gates"], in0=flat(v4("pick", 1)), in1=m["eh1"][:, 256:512], op=ALU.add))
                else:
                    le = m["le"].rearrange("p (g e t) -> p g e t", g=8, e=8)
                    tmp = m["tmp"].rearrange("p (g e t) -> p g e t", g=8, e=8)
                    top(lg, oh[0], 1, small(0, 1), small(2, 1))
                    without(lg, oh[0], flat)
                    top(lg, oh[1], 1, small(1, 1), small(2, 1))
                    rest = v4("rest", 2)
                    for i in range(2):
                        hot_g = oh[i][:, 0].unsqueeze(2).broadcast_to([R, 8, 8, NT])
                        me.then(TT(out=tmp, in0=le, in1=hot_g, op=ALU.mult))
                        me.then(v.tensor_reduce(out=rest[:, i], in_=tmp.rearrange("p g e t -> p e t g"), axis=AX.X, op=ALU.add))
                    eh = v4("eh1", 2), v4("eh2", 2)
                    top(rest, eh[0], 2, small(4, 2), small(8, 2))
                    without(rest, eh[0], flat)
                    top(rest, eh[1], 2, small(6, 2), small(8, 2))
                    me.did(TT(out=small(10, 2), in0=small(6, 2), in1=small(4, 2), op=ALU.subtract))
                    TT(out=small(1, 1), in0=small(1, 1), in1=small(0, 1), op=ALU.subtract).then_inc(S("soft_in"), 1)
                    dve.wait_ge(S("soft_out"), 2)
                    me.did(TS(small(0, 1), small(1, 1), 1.0, None, ALU.add))
                    me.then(TS(small(4, 2), small(10, 2), 1.0, None, ALU.add))
                    me.did(v.reciprocal(small(0, 1), small(0, 1)))
                    me.then(v.reciprocal(small(4, 2), small(4, 2)))
                    me.did(TT(out=small(1, 1), in0=small(1, 1), in1=small(0, 1), op=ALU.mult))
                    me.then(TT(out=small(6, 2), in0=small(10, 2), in1=small(4, 2), op=ALU.mult))
                    for i in range(2):
                        for j in range(2):
                            me.did(TT(out=gate[1][:, 2 * i + j, :], in0=sm[:, i, :], in1=sm[:, 4 + 2 * j + i, :], op=ALU.mult))
                    me.settle()
                    for what, out_ in (("members", m["members"]), ("gates", m["gates"])):
                        for i in range(2):
                            pk = v4("pick", 2)[:, i:i + 1]
                            if what == "members":
                                me.then(TT(out=pk, in0=eh[0][:, i:i + 1], in1=eh[1][:, i:i + 1], op=ALU.add))
                            else:
                                o_ = rest[:, i:i + 1]
                                me.did(TT(out=pk, in0=eh[0][:, i:i + 1], in1=over_e(gate[1][:, 2 * i:2 * i + 1, :], 1), op=ALU.mult))
                                me.then(TT(out=o_, in0=eh[1][:, i:i + 1], in1=over_e(gate[1][:, 2 * i + 1:2 * i + 2, :], 1), op=ALU.mult))
                                me.then(TT(out=pk, in0=pk, in1=o_, op=ALU.add))
                            hot_g = oh[i][:, 0].unsqueeze(2).broadcast_to([R, 8, 8, NT])
                            dst = tmp if i == 0 else m["slot"].rearrange("p (g e t) -> p g e t", g=8, e=8)
                            me.then(TT(out=dst, in0=hot_g, in1=pk[:, 0].unsqueeze(1).broadcast_to([R, 8, 8, NT]), op=ALU.mult))
                        me.then(TT(out=out_, in0=m["tmp"], in1=m["slot"], op=ALU.add))
                ch = m["chain"].rearrange("p (e t) -> p e t", t=NT)
                me.then(v.memset(m["chain"], 1.0))
                me.then(v.memset(ch[:, :, 0:1], 0.0))
                v.tensor_tensor_scan(m["upto"], m["chain"], m["members"], 0.0, ALU.mult, ALU.add).then_inc(S(q + "counted"), 1)
                dve.wait_ge(S(q + "counted"), 1)
                TT(out=m["before"], in0=m["upto"], in1=m["members"], op=ALU.subtract).then_inc(S(q + "counted"), 1)
                wait_bank(dve, f"count{f}")
                pc = bank(at[f"count{f}", 0])
                nt, run, first = ntile[:, 0, 0:c.E], ntile[:, 1, 0:c.E], ntile[:, 2, 0:c.E]
                me.did(TS(nt, pc[0:R, 0:c.E], 127.0, 1.0 / 128.0, ALU.add, ALU.mult))
                emptied(TS(ncol[0:c.E, 0:1], pc[0:c.E, 64:65], 127.0, 1.0 / 128.0, ALU.add, ALU.mult))
                dve.wait_ge(S("emptied_dve"), nth[at[f"count{f}", 0]])
                me.did(TS(nt, nt, 127.0 / 256.0, MAGIC, ALU.subtract, ALU.add))
                me.then(TS(ncol[0:c.E, 0:1], ncol[0:c.E, 0:1], 127.0 / 256.0, MAGIC, ALU.subtract, ALU.add))
                me.did(TS(nt, nt, MAGIC, None, ALU.subtract))
                TS(ncolb[0:c.E, :], ncol[0:c.E, 0:1], MAGIC, None, ALU.subtract).then_inc(S(q + "counted"), 1)
                me.did(v.memset(first, 1.0))
                me.settle()
                dve.wait_ge(S(q + "counted"), 3)
                me.then(v.tensor_tensor_scan(run, first, nt, 0.0, ALU.mult, ALU.add))
                me.then(TT(out=first, in0=run, in1=nt, op=ALU.subtract))
                me.then(TS(first, first, 128.0, None, ALU.mult))
                ne = c.E // c.banks
                for i in range(c.banks):
                    wait_bank(dve, f"rank{f}", i)
                    w = slice(ne * NT * i, ne * NT * (i + 1))
                    emptied(TT(out=m["slot"][:, w].rearrange("p (e t) -> p e t", t=NT),
                               in0=bank(at[f"rank{f}", i])[0:R, 0:ne * NT].rearrange("p (e t) -> p e t", t=NT),
                               in1=first[:, ne * i:ne * i + ne].unsqueeze(2).broadcast_to([R, ne, NT]), op=ALU.add))
                wait_bank(dve, f"ends{f}")
                emptied(v.tensor_copy(ncol[0:c.E, 1:2], bank(at[f"ends{f}", 0])[0:c.E, 0:1]))
                dve.wait_ge(S("emptied_dve"), nth[at[f"ends{f}", 0]])
                over = m["pick"][0:c.E, 0:TAB // 2].bitcast(BF16)
                TS(over, tileno[0:c.E, :], ncol[0:c.E, 1:2], None, ALU.is_ge).then_inc(S(q + "counted"), 1)
                wait_bank(dve, f"expert{f}")
                one = m["tmp"][0:1, 0:TAB]
                emptied(TS(one, bank(at[f"expert{f}", 0])[0:1, 0:TAB], float(c.E - 1), None, ALU.min))
                dve.wait_ge(S("emptied_dve"), nth[at[f"expert{f}", 0]])
                n = TAB - U + 1
                pair = m["rest"][0:1, 0:TAB - 1]
                me.then(v.scalar_tensor_tensor(pair[:, 0:TAB - 1], one[:, 1:TAB], float(c.E), one[:, 0:TAB - 1], ALU.mult, ALU.add))
                me.then(v.scalar_tensor_tensor(table[f][:, 0:n], pair[:, 2:n + 2], float(c.E ** 2), pair[:, 0:n], ALU.mult, ALU.add))
                S_ = m["slot"]
                if f == 0:
                    for k in range(2):
                        me.then(TT(out=m["tmp"], in0=flat(oh[k]), in1=S_, op=ALU.mult))
                        me.then(v.tensor_reduce(out=sm[:, k, :], in_=m["tmp"].rearrange("p (e t) -> p t e", t=NT), axis=AX.X, op=ALU.add))
                else:
                    s4 = S_.rearrange("p (g e t) -> p g e t", g=8, e=8)
                    for i in range(2):
                        hot_g = oh[i][:, 0].unsqueeze(2).broadcast_to([R, 8, 8, NT])
                        me.then(TT(out=tmp, in0=s4, in1=hot_g, op=ALU.mult))
                        me.then(v.tensor_reduce(out=rest[:, i], in_=tmp.rearrange("p g e t -> p e t g"), axis=AX.X, op=ALU.add))
                    for j in range(2):
                        me.then(TT(out=v4("pick", 2), in0=eh[j], in1=rest, op=ALU.mult))
                        for i in range(2):
                            me.then(v.tensor_reduce(out=sm[:, 2 * i + j, :], in_=v4("pick", 2)[:, i].rearrange("p e t -> p t e"),
                                                    axis=AX.X, op=ALU.add))
                me.did(v.tensor_copy(place[f][:, 0:c.K, :], sm[:, 0:c.K, :]))
                of, within = sm[:, 4:4 + c.K, :], sm[:, 8:8 + c.K, :]
                me.then(TS(of, sm[:, 0:c.K, :], 63.5, 1.0 / 128.0, ALU.subtract, ALU.mult))
                me.then(TS(of, of, MAGIC, None, ALU.add))
                me.then(TS(of, of, MAGIC, None, ALU.subtract))
                v.scalar_tensor_tensor(within, of, -128.0, sm[:, 0:c.K, :], ALU.mult, ALU.add).then_inc(S(q + "placed"), 1)
                hot_tile = hot_views(f)[1]
                for g in range(c.K * B):
                    if g >= 2:
                        dve.wait_ge(S(q + "hots_used"), g - 1)
                    for j in range(J):
                        t = g % B * J + j
                        last = TS(hot_tile[:, g % 2, j], tileno[0:R, :], sm[:, 4 + g // B, t:t + 1], tokno[:, t:t + 1], ALU.is_equal, ALU.mult)
                    last.then_inc(S(q + "hot_tile"), 1)
                wait_bank(dve, f"holder{f}")
                emptied(TS(holder[:, :], bank(at[f"holder{f}", 0])[:, 0:TAB], float(MIDROW), None, ALU.add))

            TT, TS = v.tensor_tensor, v.tensor_scalar

            def attention_weights(me, dve):
                dve.wait_ge(S("ld_attn"), 16 * 9)
                dve.wait_ge(S("aconst_ready"), 1)
                me.did(v.tensor_copy(i500, i500.bitcast(I32)))
                me.then(v.tensor_copy(sidf, sidx.bitcast(I32)))
                me.then(TS(shi, sidf, 0.0, float(L), ALU.is_lt, ALU.mult))
                me.then(TT(out=sidf, in0=sidf, in1=shi, op=ALU.add))
                me.then(TS(sidf, sidf, 0.0, float(L - 1), ALU.max, ALU.min))
                me.then(TS(shi, sidf, float(R), None, ALU.is_ge))
                for k in range(2, J):
                    me.then(v.scalar_tensor_tensor(shi, sidf, float(R * k), shi, ALU.is_ge, ALU.add))
                me.then(v.scalar_tensor_tensor(slo, shi, -float(R), sidf, ALU.mult, ALU.add))
                me.did(TT(out=hot_hi, in0=shi.unsqueeze(2).broadcast_to([128, 20, J]),
                          in1=i500[:, 0:J].unsqueeze(1).broadcast_to([128, 20, J]), op=ALU.is_equal))
                TT(out=hot_lo, in0=slo.unsqueeze(2).broadcast_to([128, 20, R]),
                   in1=i500[:, 0:R].unsqueeze(1).broadcast_to([128, 20, R]), op=ALU.is_equal).then_inc(S("hots_ready"), 1)
                wait_bank(dve, "wT")
                pw = bank(at["wT", 0])
                for w, dst in enumerate((wqT, wkT, wvT, woT)):
                    last = v.tensor_copy(dst, pw[:, 128 * w:128 * w + 128])
                emptied(last)
                wait_bank(dve, "cols")
                emptied(v.tensor_copy(bcol, bank(at["cols", 0])[:, 0:3]))
                wait_bank(dve, "cnt")
                emptied(v.tensor_copy(cnt, bank(at["cnt", 0])[0:R, 0:J]))
                wait_bank(dve, "cntrow")
                emptied(TS(maskrow, bank(at["cntrow", 0])[0:1, 0:L], 0.0, -1e30, ALU.is_equal, ALU.mult))

            def attention(me, dve):
                for b in range(B):
                    stats(h, b, mv)
                me.settle()
                v.tensor_scalar(rs[:, :], mv[:, :, 1], EPS, None, ALU.add).then_inc(S("var_ready"), 1)
                invert(rs[:, :], rs[:, :], 6)
                for b in range(B):
                    for t in range(J * b, J * b + J):
                        last = TS(x[:, t, :], h[:, t, :], mv[:, t, 0:1], rs[:, t:t + 1], ALU.subtract, ALU.mult)
                    last.then_inc(S("xa_ready"), 1)
                wait_bank(dve, "xbar")
                emptied(TS(xbar, bank(at["xbar", 0])[:, 0:B], 1.0 / NSAMP, None, ALU.mult))
                wait_bank(dve, "kbar")
                me.then(TS(kcol, bank(at["kbar", 0])[:, 0:B], bcol[:, 1:2], -1.0, ALU.add, ALU.mult))
                emptied(TS(kcol, kcol, bcol[:, 1:2], None, ALU.add))
                for g in range(8 * B):
                    b, half, j = g // 8, g // 4 % 2, g % 4
                    n = at["score", 4 * g]
                    wait_bank(dve, "score", 4 * g + 3)
                    emptied(v.tensor_reduce(out=mcol[:, j, H * b + 4 * half:H * b + 4 * half + 4],
                                            in_=ps[0:R, n % 8:n % 8 + 4, 0:L], axis=AX.X, op=ALU.max))
                wait_bank(dve, "MT")
                emptied(v.tensor_copy(mrow, bank(at["MT", 0])[0:64, 0:L]))
                dve.wait_ge(S("emptied_dve"), nth[at["MT", 0]])
                me.then(v.max(m8, mrow))
                me.then(v.max_index(i8, m8, mrow))
                me.then(v.tensor_copy(i8f, i8[:, 0:1]))
                TS(hot, i500[0:64, :], i8f, None, ALU.is_equal).then_inc(S("hot_ready"), 1)
                wait_bank(dve, "hotT")
                emptied(v.tensor_copy(hotT, bank(at["hotT", 0])[0:R, 0:256].rearrange("p (j n) -> p j n", j=J)))
                wait_bank(dve, "xsel")
                emptied(v.tensor_copy(xsel, bank(at["xsel", 0])[:, 0:64]))
                wait_bank(dve, "qsel")
                emptied(v.scalar_tensor_tensor(qsel.rearrange("p (b h) -> p b h", b=B),
                                               bank(at["qsel", 0])[:, 0:64].rearrange("p (b h) -> p b h", b=B),
                                               bcol[:, 0:1], own16.unsqueeze(1).broadcast_to([128, B, H]), ALU.add, ALU.mult))
                wait_bank(dve, "u")
                emptied(v.tensor_copy(bass.AP(tensor=uz.tensor, offset=uz.offset, ap=[list(uz.ap[0]), [72, B], [1, H]]),
                                      bank(at["u", 0])[:, 0:64].rearrange("p (b h) -> p b h", b=B)))
                wait_bank(dve, "ss")
                me.then(v.tensor_reduce(out=nmx, in_=bank(at["ss", 0])[0:64, 0:L], axis=AX.X, op=ALU.max))
                TS(nmx, nmx, -SCALE, None, ALU.mult).then_inc(S("nmx_ready"), 1)
                wait_evac(dve, "ss")
                me.then(v.reciprocal(asum, asum))
                TS(att, att, asum, None, ALU.mult).then_inc(S("att_ready"), 1)
                wait_bank(dve, "attT")
                emptied(v.tensor_copy(attT, bank(at["attT", 0])[0:R, 0:256].rearrange("p (j n) -> p j n", j=J)))
                wait_bank(dve, "xa")
                emptied(v.tensor_copy(xa, bank(at["xa", 0])[:, 0:64]))
                wait_bank(dve, "ctx")
                emptied(TT(out=cmul.rearrange("p (b h) -> p b h", b=B), in0=bank(at["ctx", 0])[:, 0:64].rearrange("p (b h) -> p b h", b=B),
                           in1=own16.unsqueeze(1).broadcast_to([128, B, H]), op=ALU.mult))
                dve.wait_ge(S("emptied_dve"), nth[at["ctx", 0]])
                me.then(v.tensor_reduce(out=ctxv, in_=cmul.rearrange("p (b h) -> p b h", b=B), axis=AX.X, op=ALU.add))
                TS(ctxb, ctxv.unsqueeze(2).broadcast_to([128, B, R]), bcol[:, 2:3], None, ALU.add).then_inc(S("ctx_ready"), 1)
                for i in range(2):
                    wait_bank(dve, "outa", i)
                    for b in range(4 * i, 4 * i + 4):
                        hv = h[:, J * b:J * b + J, :]
                        k = b - 4 * i
                        row = bank(at["outa", i])[0:R, D * k:D * k + D].unsqueeze(1).broadcast_to([R, J, D])
                        last = TT(out=hv, in0=row, in1=hv, op=ALU.add)
                    emptied(last)
                dve.wait_ge(S("emptied_dve"), nth[at["outa", 1]])

            dve.wait_ge(S("ld_ids"), 32)
            v.tensor_copy(ids32f[:, :], ids32[:, :]).then_inc(S("ids_float"), 1)
            wait_bank(dve, "tokens")
            v.tensor_copy(idsT[:, :], bank(at["tokens", 0])[0:R, 0:NT]).then_inc(S("ids_ready"), 1)
            emptied(v.tensor_copy(valT[:, :], bank(at["tokens", 0])[0:R, 32:32 + NT]))
            wait_bank(dve, "ssm")
            emptied(v.tensor_copy(sp5[:, :, :], bank(at["ssm", 0])[:, 0:5 * NC].rearrange("p (q c) -> p q c", q=5)))
            dve.wait_ge(S("emptied_dve"), nth[at["ssm", 0]])
            dve.wait_ge(S("iota_ready"), 1)
            me.then(v.tensor_copy(itF[:, :], itI[:, :]))

            def lagmul(dst, q, lo, n):
                return v.tensor_tensor(out=dst, in0=sp5[:, q, :].unsqueeze(2).broadcast_to([128, NC, n]),
                                       in1=itF[:, lo:lo + n].unsqueeze(1).broadcast_to([128, NC, n]), op=ALU.mult)
            na, nb = NC * KA, NC * KB
            pa, pa2, pb = ph[:, 0:na], ph[:, na:2 * na], ph[:, 2 * na:]
            ma, mb = mg[:, 0:na], mg[:, na:na + nb]

            def cl(t, n):
                return t.rearrange("p (c l) -> p c l", l=n)
            me.did(lagmul(cl(ma, KA), 0, 0, KA))
            lagmul(cl(mb, KB), 0, KA, KB).then_inc(S("exponents_ready"), 1)
            me.did(lagmul(cl(pa, KA), 1, 0, KA))
            me.did(lagmul(cl(pb, KB), 1, KA, KB))
            me.settle()
            me.did(v.tensor_scalar(pa2, pa, alpha[:, 1:2], None, ALU.add))
            me.did(v.tensor_scalar(pb, pb, alpha[:, 2:3], None, ALU.add))
            me.settle()
            me.then(v.tensor_scalar(pa, pa, alpha[:, 0:1], None, ALU.add))
            me.then(v.tensor_scalar(qn, ph, 1.0 / (2.0 * math.pi), MAGIC, ALU.mult, ALU.add))
            me.then(v.tensor_scalar(qn, qn, MAGIC, None, ALU.subtract))
            me.then(v.scalar_tensor_tensor(ph, qn, -6.28125, ph, ALU.mult, ALU.add))
            me.then(v.scalar_tensor_tensor(ph, qn, -(2.0 * math.pi - 6.28125), ph, ALU.mult, ALU.add))
            v.tensor_scalar(ph, ph, 3.1415925, -3.1415925, ALU.min, ALU.max).then_inc(S("phases_ready"), 1)
            me.did(v.tensor_tensor(out=cc[:, 0, :], in0=sp5[:, 2, :], in1=sp5[:, 4, :], op=ALU.mult))
            me.did(v.tensor_tensor(out=cc[:, 1, :], in0=sp5[:, 3, :], in1=sp5[:, 4, :], op=ALU.mult))
            me.settle()
            dve.wait_ge(S("sines_ready"), 1)

            def cb(q):
                return cc[:, q, :].unsqueeze(2).broadcast_to([128, NC, KA])
            me.did(v.tensor_tensor(out=cl(pa, KA), in0=cl(pa, KA), in1=cb(0), op=ALU.mult))
            me.did(v.tensor_tensor(out=cl(pa2, KA), in0=cl(pa2, KA), in1=cb(1), op=ALU.mult))
            me.settle()
            me.then(v.tensor_tensor(out=pa, in0=pa, in1=pa2, op=ALU.subtract))
            me.did(v.tensor_tensor(out=e1[:, :, :], in0=cl(pa, KA), in1=cl(ma, KA), op=ALU.mult))
            me.did(v.tensor_tensor(out=e1r[:, :, :], in0=cl(pa, KA)[:, :, ::-1], in1=cl(ma, KA)[:, :, ::-1], op=ALU.mult))
            me.did(v.tensor_tensor(out=e2[:, :, 0:KB], in0=cl(pb, KB), in1=cl(mb, KB), op=ALU.mult))
            v.tensor_tensor(out=e2[:, :, KB:2 * KB], in0=cl(pb, KB)[:, :, ::-1], in1=cl(mb, KB)[:, :, ::-1],
                            op=ALU.mult).then_inc(S("factors_ready"), 1)
            for q in range(4):
                wait_bank(dve, "lags", q)
                emptied(v.tensor_copy(kk[:, 8 * q:8 * q + 8, :],
                                      bank(at["lags", q])[0:KA, :].rearrange("p (c l) -> p c l", c=8)))
            dve.wait_ge(S("emptied_dve"), nth[at["lags", 3]])
            v.tensor_tensor(out=kk[:, :, 2 * KB - 1], in0=kk[:, :, 2 * KB - 1], in1=dskip[:, :],
                            op=ALU.add).then_inc(S("lags_ready"), 1)
            dve.wait_ge(S("ld_w"), 96)
            v.tensor_scalar(wg[:, :], wsm[:, 0, :], lnc[:, 0:1], None, ALU.mult).then_inc(S("wg_ready"), 1)
            v.tensor_copy(cst[:, 512:640], lnc[:, 1:2].broadcast_to([128, 128])).then_inc(S("wg_ready"), 1)
            dve.wait_ge(S("ld_val"), 96)
            for t in range(NT):
                me.did(v.scalar_tensor_tensor(vw[:, t, :], wv[:, t % J, :], valT[:, t:t + 1], bv[:, t % J, :],
                                              ALU.mult, ALU.add))
            me.settle()
            v.tensor_copy(cst[0:1, 128:129], valT[0:1, 0:1]).then_inc(S("values_read"), 1)
            for b in range(B):
                stats(vw, b, mv)
            me.settle()
            v.tensor_scalar(rs[:, :], mv[:, :, 1], EPS, None, ALU.add).then_inc(S("var_ready"), 1)
            invert(rs[:, :], rs[:, :], 1)
            for b in range(B):
                for t in range(J * b, J * b + J):
                    last = v.tensor_scalar(vw[:, t, :], vw[:, t, :], mv[:, t, 0:1], rs[:, t:t + 1], ALU.subtract, ALU.mult)
                last.then_inc(S("vn_ready"), 1)
            wait_bank(dve, "zbias")
            emptied(v.tensor_copy(rows[:, 4, :], bank(at["zbias", 0])[0:R, 0:D]))
            dve.wait_ge(S("vn_ready"), B)
            for b in range(B):
                dve.wait_ge(S(f"gathered{b}"), 16 * J)
                stats(gw, b, mv)
            me.settle()
            v.tensor_scalar(rs[:, :], mv[:, :, 1], EPS, None, ALU.add).then_inc(S("var_ready"), 1)
            invert(rs[:, :], rs[:, :], 2)
            for b in range(B):
                for t in range(J * b, J * b + J):
                    me.did(v.scalar_tensor_tensor(gw[:, t, :], gw[:, t, :], mv[:, t, 0:1], rows[:, 0, :], ALU.subtract, ALU.mult))
            me.settle()
            for b in range(B):
                dve.wait_ge(S("vb_ready"), b + 1)
                for t in range(J * b, J * b + J):
                    me.did(v.scalar_tensor_tensor(h[:, t, :], gw[:, t, :], rs[:, t:t + 1], vw[:, t, :], ALU.mult, ALU.add))
            me.settle()
            for b in range(B):
                stats(h, b, mv)
            me.settle()
            v.tensor_scalar(rs[:, :], mv[:, :, 1], EPS, None, ALU.add).then_inc(S("var_ready"), 1)
            invert(rs[:, :], rs[:, :], 3)
            for b in range(B):
                for t in range(J * b, J * b + J):
                    last = v.tensor_scalar(x[:, t, :], h[:, t, :], mv[:, t, 0:1], rs[:, t:t + 1], ALU.subtract, ALU.mult)
                last.then_inc(S("x0_ready"), 1)
            me.then(v.tensor_tensor(out=rs2[:, :], in0=rs[:, :], in1=rs[:, :], op=ALU.mult))
            me.then(v.tensor_tensor(out=rs2[:, :], in0=rs2[:, :], in1=mv[:, :, 1], op=ALU.mult))
            v.tensor_scalar(rs2[:, :], rs2[:, :], EPS, None, ALU.add).then_inc(S("var_ready"), 1)
            invert(rs2[:, :], rs2[:, :], 4)
            for b in range(B):
                wait_bank(dve, "z", b)
                pz = bank(at["z", b])[0:R, :].rearrange("p (j d) -> p j d", j=J)
                for j in range(J):
                    t = J * b + j
                    last = v.scalar_tensor_tensor(z[:, j, :, b, :], pz[:, j, :].rearrange("p (c r) -> p c r", c=NC),
                                                  rs2[:, t:t + 1], rows[:, 4, :].rearrange("p (c r) -> p c r", c=NC),
                                                  ALU.mult, ALU.add)
                emptied(last)
            for q in range(8):
                wait_bank(dve, "convT", q)
                pc = bank(at["convT", q])[0:R, :].rearrange("p (j k b r) -> p j k b r", j=J, k=4, b=B)
                yv = y[:, :, :].rearrange("p (b j) (q k r) -> p j q k b r", j=J, q=8, r=CS)
                for j in range(J):
                    last = v.tensor_copy(yv[:, j, q], pc[:, j])
                emptied(last)
            for b in range(0, B, 2):
                wait_bank(dve, "yT", b)
                emptied(v.tensor_copy(yT[:, J * b:J * b + J, :], bank(at["yT", b])[:, 0:L].rearrange("p (j t) -> p j t", j=J)))
            for b in range(B):
                dve.wait_ge(S("hx_ready"), b + 1)
                wait_evac(dve, "out0", b)
                hv = h[:, J * b:J * b + J, :]
                me.did(v.tensor_tensor(out=hv, in0=hv, in1=x[:, J * b:J * b + J, :], op=ALU.add))
            me.settle()
            dve.wait_ge(S("iota2_ready"), 1)
            me.did(v.tensor_copy(em8[:, :], em8I[:, :]))
            me.then(v.tensor_copy(tileno[:, :], tileno[:, :].bitcast(I32)))
            me.then(v.tensor_copy(tokno[:, :], tokno[:, :].bitcast(I32)))
            for f in (0, 1):
                c = FFN[f]
                q = f"f{f}_"
                wait_bank(dve, f"b1T{f}")
                dve.wait_ge(S("bank_filled"), nfill[at["out0", B - 1]])
                w1v = big[:, c.w1_at:c.w1_at + c.E * c.wcols].rearrange("p (e w) -> p e w", e=c.E)
                emptied(v.tensor_copy(w1v[:, :, 128 * c.HC:], bank(at[f"b1T{f}", 0])[:, 0:c.E * c.HC].rearrange("p (e k) -> p e k", e=c.E)))
                for b in range(B):
                    stats(h, b, mv)
                me.settle()
                v.tensor_scalar(rs[:, :], mv[:, :, 1], EPS, None, ALU.add).then_inc(S("var_ready"), 1)
                invert(rs[:, :], rs[:, :], 5 + 2 * f)
                for b in range(B):
                    for t in range(J * b, J * b + J):
                        last = v.tensor_scalar(x[:, t, :], h[:, t, :], mv[:, t, 0:1], rs[:, t:t + 1], ALU.subtract, ALU.mult)
                    last.then_inc(S(f"x{f + 1}_ready"), 1)
                route(c, me, dve)
                for b in range(B):
                    wait_bank(dve, f"bias{f}", b)
                    hv = h[:, J * b:J * b + J, :]
                    emptied(v.tensor_tensor(out=hv, in0=bank(at[f"bias{f}", b])[0:R, :].rearrange("p (j d) -> p j d", j=J),
                                            in1=hv, op=ALU.add))
                dve.wait_ge(S("emptied_dve"), nth[at[f"bias{f}", B - 1]])
                if f == 0:
                    attention_weights(me, dve)
                expert_vector(dve, c, me)
                n = 0
                for t in range(NT):
                    for k in range(c.K):
                        dve.wait_ge(S(q + f"got{n % 8}"), 16 * (n // 8 + 1))
                        if k:
                            dve.wait_ge(S(q + "combined"), n)
                        v.scalar_tensor_tensor(h[:, t, :], got[n % 8], gate[f][:, k, t:t + 1], h[:, t, :],
                                               ALU.mult, ALU.add).then_inc(S(q + "combined"), 1)
                        n += 1
                dve.wait_ge(S(q + "combined"), n)
                if f == 0:
                    attention(me, dve)

        @block.scalar
        def _(act):
            me = Steps(act, S("act_step"))
            s = nc.scalar

            def emptied(ins):
                ins.then_inc(S("emptied_act"), 1)

            def root(n, t):
                act.wait_ge(S("var_ready"), n)
                s.activation(t, t, ACT.Sqrt).then_inc(S("root_ready"), 1)
            act.wait_ge(S("exponents_ready"), 1)
            na, nb = NC * KA, NC * KB
            me.did(s.activation(mg[:, 0:na + nb], mg[:, 0:na + nb], ACT.Exp))
            act.wait_ge(S("phases_ready"), 1)
            me.settle()
            s.activation(ph, ph, ACT.Sin).then_inc(S("sines_ready"), 1)
            root(1, rs[:, :])
            root(2, rs[:, :])
            root(3, rs[:, :])
            root(4, rs2[:, :])
            for b in range(B):
                wait_bank(act, "xT", b)
                emptied(s.copy(xT[:, J * b:J * b + J, :], bank(at["xT", b])[:, 0:L].rearrange("p (j t) -> p j t", j=J)))
            act.wait_ge(S("hx_ready"), B)
            for q in range(8):
                wait_bank(act, "conv", q)
                emptied(s.copy(ys[:, q, 0:L], bank(at["conv", q])[:, 0:L]))
            for b in range(1, B, 2):
                wait_bank(act, "yT", b)
                emptied(s.copy(yT[:, J * b:J * b + J, :], bank(at["yT", b])[:, 0:L].rearrange("p (j t) -> p j t", j=J)))
            for b in range(B):
                wait_bank(act, "out0", b)
                emptied(s.activation(x[:, J * b:J * b + J, :], bank(at["out0", b])[0:R, :].rearrange("p (j d) -> p j d", j=J),
                                     ACT.Gelu))

            for f in (0, 1):
                c = FFN[f]
                root(5 + 2 * f, rs[:, :])
                for b in range(B):
                    wait_bank(act, f"rT{f}", b)
                    emptied(s.copy(xT[:, J * b:J * b + J, :], bank(at[f"rT{f}", b])[:, 0:L].rearrange("p (j t) -> p j t", j=J)))
                act.wait_ge(S("soft_in"), f + 1)
                m = mask_views(f)
                if f == 0:
                    me.did(s.activation(m["rest"][:, 0:256], m["rest"][:, 0:256], ACT.Exp))
                    s.activation(sm[:, 1, :], sm[:, 1, :], ACT.Exp).then_inc(S("soft_out"), 1)
                else:
                    me.did(s.activation(sm[:, 1, :], sm[:, 1, :], ACT.Exp))
                    s.activation(sm[:, 10:12, :], sm[:, 10:12, :], ACT.Exp).then_inc(S("soft_out"), 1)
                act.wait_ge(S(f"f{f}_placed"), 1)
                hot_slot, _, far = hot_views(f)
                for g in range(c.K * B):
                    if g >= 2:
                        act.wait_ge(S(f"f{f}_hots_used"), g - 1)
                    for j in range(J // 2):
                        t = g % B * J + J // 2 + j
                        me.did(s.activation(far[:, g % 2, j], tileno[0:R, 0:128], ACT.Abs, bias=sm[:, 8 + g // B, t:t + 1], scale=-1.0))
                    me.settle()
                    s.activation(hot_slot[:, g % 2, J // 2:], far[:, g % 2], ACT.Relu, bias=ones[0:R, 0:1],
                                 scale=-1.0).then_inc(S(f"f{f}_hot_slot_act"), 1)
                for b in range(B):
                    wait_bank(act, f"cT{f}", b)
                    emptied(s.copy(cT[0:c.E, :], bank(at[f"cT{f}", b])[0:c.E, 0:L]))
                expert_scalar(act, c)
                if f == 0:
                    root(6, rs[:, :])
                    for b in range(B):
                        wait_bank(act, "aT", b)
                        emptied(s.copy(xT[:, J * b:J * b + J, :], bank(at["aT", b])[:, 0:L].rearrange("p (j t) -> p j t", j=J)))
                    act.wait_ge(S("emptied_dve"), nth[at["kbar", 0]])
                    for b in range(B):
                        if b:
                            act.wait_ge(S("parts_ready"), b)
                            act.wait_ge(S("parts_st"), 16 * b)
                        for w, col in enumerate((bcol[:, 0:1], kcol[:, b:b + 1])):
                            wait_bank(act, "qk", 2 * b + w)
                            src = bank(at["qk", 2 * b + w])[:, 0:L]
                            me.did(s.activation(qk_rest[:, w, :], src, ACT.Identity, bias=col))
                            emptied(s.activation(parts[:, w, 0, :], src, ACT.Identity, bias=col))
                        me.settle()
                        act.wait_ge(S("emptied_act"), nth[at["qk", 2 * b + 1]])
                        act.sem_inc(S("part1_ready"), 1)
                        act.wait_ge(S("rest_ready"), b + 1)
                        s.copy(parts[:, :, 1, :], qk_rest).then_inc(S("part2_ready"), 1)
                    wait_bank(act, "ss")
                    act.wait_ge(S("nmx_ready"), 1)
                    emptied(s.activation(att, bank(at["ss", 0])[0:64, 0:L], ACT.Exp, bias=nmx, scale=SCALE, accum_out=asum))

        @block.tensor
        def _(pe):
            t = nc.tensor
            order = iter(range(len(plan)))

            def use(what, i=0):
                n = next(order)
                while plan[n][0] == "skip":
                    n = next(order)
                assert plan[n][:2] == (what, i)
                if n >= 8 and nth[n - 8] and (what != "score" or i % 4 == 0):
                    m = n - 4 if what == "score" else n - 8
                    for eng in ("act", "dve"):
                        counts = [nth[k] for k in range(n - 8, m) if plan[k][2] == eng] if what == "score" else \
                            [nth[n - 8]] * (plan[n - 8][2] == eng)
                        if counts:
                            pe.wait_ge(S("emptied_" + eng), max(counts))
                return bank(n)

            def filled(ins):
                ins.then_inc(S("bank_filled"), 1)

            def attention_weights():
                pe.wait_ge(S("ld_attn"), 16 * 9)
                p = use("wT")
                for w in range(4):
                    last = t.transpose(p[:, 128 * w:128 * w + 128], wraw[:, w, :], ident)
                filled(last)
                p = use("cols")
                for n in range(3):
                    last = t.matmul(p[:, n:n + 1], arow[:, n, :], ones[0:1, 0:1], start=True, stop=True)
                filled(last)
                pe.wait_ge(S("hots_ready"), 1)
                p = use("cnt")
                for n in range(20):
                    last = t.matmul(p[0:R, 0:J], hot_lo[:, n, :], hot_hi[:, n, :], start=n == 0, stop=n == 19)
                filled(last)
                wait_evac(pe, "cnt")
                p = use("cntrow")
                for j in range(J):
                    last = t.matmul(p[0:1, R * j:R * j + R], cnt[:, j:j + 1], ident[0:R, 0:R], start=True, stop=True)
                filled(last)
                wait_evac(pe, "cntrow")

            def attention_products():
                for b in range(B):
                    pe.wait_ge(S("xa_ready"), b + 1)
                    p = use("aT", b)
                    for j in range(J):
                        last = t.transpose(p[:, R * j:R * j + R], x[:, J * b + j, :], ident[0:R, 0:R])
                    filled(last)
                p = use("xbar")
                for b in range(B):
                    for j in range(J):
                        last = t.matmul(p[:, b:b + 1], x[:, J * b + j, :], cnt[:, j:j + 1], start=j == 0, stop=j == J - 1)
                filled(last)
                wait_evac(pe, "xbar")
                p = use("kbar")
                filled(t.matmul(p[:, 0:B], wkT, xbar, start=True, stop=True))
                wait_evac(pe, "aT", B - 1)

                def qk(b):
                    rhs = xT[:, J * b:J * b + J, :].rearrange("p j t -> p (j t)")
                    for w, weights in enumerate((wqT, wkT)):
                        filled(t.matmul(use("qk", 2 * b + w)[:, 0:L], weights, rhs, start=True, stop=True))

                def scores(b, first, last_):
                    for g in range(8 * b + first, 8 * b + last_):
                        half, j = g // 4 % 2, g % 4
                        four = [use("score", 4 * g + i) for i in range(4)]
                        for i, p in enumerate(four):
                            k = 4 * half + i
                            last = t.matmul(p[0:R, 0:L], stack[0:SROWS, 0, b % 2, k, R * j:R * j + R], stack[0:SROWS, 1, b % 2, k, :],
                                            start=True, stop=True)
                        filled(last)
                qk(0)
                qk(1)
                pe.wait_ge(S("mask_in"), 32)
                for b in range(B):
                    pe.wait_ge(S(f"stack{b % 2}"), 16 * 12 * (b // 2 + 1))
                    scores(b, 0, 4)
                    if b < B - 2:
                        qk(b + 2)
                    scores(b, 4, 8)
                wait_evac(pe, "score", 4 * 8 * B - 1)
                p = use("MT")
                for j in range(J):
                    last = t.transpose(p[0:64, R * j:R * j + R], mcol[:, j, :], ident[0:R, 0:R])
                filled(last)
                pe.wait_ge(S("hot_ready"), 1)
                p = use("hotT")
                for j in range(J):
                    last = t.transpose(p[0:R, 64 * j:64 * j + 64], hot[:, R * j:R * j + R], ident[0:64, 0:64])
                filled(last)

                def rows_times(p, cols):
                    for b in range(B):
                        for j in range(J):
                            ins = t.matmul(p[:, H * b:H * b + H], x[:, J * b + j, :], cols[:, j, H * b:H * b + H],
                                           start=j == 0, stop=j == J - 1)
                    return ins
                wait_evac(pe, "hotT")
                filled(rows_times(use("xsel"), hotT))
                wait_evac(pe, "xsel")
                p = use("qsel")
                filled(t.matmul(p[:, 0:64], wqT, xsel, start=True, stop=True))
                wait_evac(pe, "qsel")
                p = use("u")
                filled(t.matmul(p[:, 0:64], wraw[:, 1, :], qsel, start=True, stop=True))
                wait_evac(pe, "u")
                p = use("ss")
                for b in range(B):
                    last = t.matmul(p[0:64, 0:L], uz[:, 64 * b:64 * b + 64], xT[:, J * b:J * b + J, :].rearrange("p j t -> p (j t)"),
                                    start=b == 0, stop=b == B - 1)
                filled(last)
                pe.wait_ge(S("att_ready"), 1)
                p = use("attT")
                for j in range(J):
                    last = t.transpose(p[0:R, 64 * j:64 * j + 64], att[:, R * j:R * j + R], ident[0:64, 0:64])
                filled(last)
                wait_evac(pe, "attT")
                filled(rows_times(use("xa"), attT))
                wait_evac(pe, "xa")
                p = use("ctx")
                filled(t.matmul(p[:, 0:64], wvT, xa, start=True, stop=True))
                pe.wait_ge(S("ctx_ready"), 1)
                for i in range(2):
                    p = use("outa", i)
                    for k in range(4):
                        t.matmul(p[0:R, D * k:D * k + D], ctxb[:, 4 * i + k, :], woT, start=True, stop=False)
                        last = t.matmul(p[0:R, D * k:D * k + D], ones[0:1, 0:R], arow[:, 3, :], start=False, stop=True)
                    filled(last)

            pe.wait_ge(S("ident_ready"), 1)
            pe.wait_ge(S("ids_float"), 1)
            p = use("tokens")
            t.transpose(p[0:R, 0:NT], ids32f[:, :], ident[0:NT, 0:NT])
            filled(t.transpose(p[0:R, 32:32 + NT], val32[:, :], ident[0:NT, 0:NT]))
            pe.wait_ge(S("ld_ssm"), 16 * 11)
            p = use("ssm")
            for q in range(5):
                last = t.transpose(p[:, NC * q:NC * q + NC], ssm5[:, q, :, :].rearrange("c r n -> c (r n)"), ident[0:NC, 0:NC])
            filled(last)
            pe.wait_ge(S("factors_ready"), 1)
            for q in range(4):
                p = use("lags", q)
                for c in range(8):
                    for r, e in enumerate((e1, e1r)):
                        w = KB * (2 * c + r)
                        last = t.matmul(p[0:KA, w:w + KB], e[:, 8 * q + c, :], e2[:, 8 * q + c, KB * r:KB * r + KB],
                                        start=True, stop=True)
                filled(last)
            pe.wait_ge(S("wg_ready"), 2)
            p = use("zbias")
            t.matmul(p[0:R, 0:D], cst[:, 512:512 + R], wsm[:, 0, :], start=True, stop=False)
            filled(t.matmul(p[0:R, 0:D], ones[0:1, 0:R], rowv[:, 0, :], start=False, stop=True))
            for b in range(B):
                pe.wait_ge(S("x0_ready"), b + 1)
                p = use("xT", b)
                for j in range(J):
                    last = t.transpose(p[:, R * j:R * j + R], x[:, J * b + j, :], ident[0:R, 0:R])
                filled(last)
            for b in range(B):
                wait_evac(pe, "xT", b)
                p = use("z", b)
                for j in range(J):
                    last = t.matmul(p[0:R, D * j:D * j + D], xT[:, J * b + j, :], wg[:, :], start=True, stop=True)
                filled(last)
            wait_evac(pe, "z", B - 1)
            for q in range(9):
                if q < 8:
                    pe.wait_ge(S(f"strip{q}"), 16)
                    p = use("conv", q)
                    for i in range(J):
                        for k in range(4):
                            c = 4 * q + k
                            last = t.matmul(p[32 * k:32 * k + 32, 0:L], z[:, i, c].rearrange("p b r -> p (b r)"),
                                            G[0:R, c, R * i:R * i + L][:, ::-1], start=i == 0, stop=i == J - 1)
                    filled(last)
                if q > 0:
                    wait_evac(pe, "conv", q - 1)
                    p = use("convT", q - 1)
                    for j in range(J):
                        last = t.transpose(p[0:R, D * j:D * j + D], ys[:, q - 1, R * j:R * j + R], ident)
                    filled(last)
            wait_evac(pe, "convT", 7)
            for b in range(B):
                p = use("yT", b)
                for j in range(J):
                    last = t.transpose(p[:, R * j:R * j + R], y[:, J * b + j, :], ident[0:R, 0:R])
                filled(last)
            for b in range(B):
                wait_evac(pe, "yT", b)
                p = use("out0", b)
                for j in range(J):
                    t.matmul(p[0:R, D * j:D * j + D], yT[:, J * b + j, :], wsm[:, 1, :], start=True, stop=False)
                    last = t.matmul(p[0:R, D * j:D * j + D], ones[0:1, 0:R], rowv[:, 1, :], start=False, stop=True)
                filled(last)

            for f in (0, 1):
                c = FFN[f]
                q = f"f{f}_"
                m = mask_views(f)
                pe.wait_ge(S("ld_router"), 128)
                p = use(f"b1T{f}")
                filled(t.transpose(p[:, 0:c.E * c.HC], b1r[0:c.E * c.HC, f, :], ident[0:c.E * c.HC, 0:c.E * c.HC]))
                for b in range(B):
                    pe.wait_ge(S(f"x{f + 1}_ready"), b + 1)
                    p = use(f"rT{f}", b)
                    for j in range(J):
                        last = t.transpose(p[:, R * j:R * j + R], x[:, J * b + j, :], ident[0:R, 0:R])
                    filled(last)
                for b in range(B):
                    wait_evac(pe, f"rT{f}", b)
                    p = use(f"router{f}", b)
                    for j in range(J):
                        w = p[0:R, c.wide * j:c.wide * j + c.wide]
                        last = t.matmul(w, xT[:, J * b + j, :], wr[:, f, 0:c.wide], start=True, stop=f == 1)
                        if f == 0:
                            last = t.matmul(w, ones[0:1, 0:R], brow[:, :], start=False, stop=True)
                    filled(last)
                pe.wait_ge(S(q + "counted"), 1)
                p = use(f"count{f}")
                total = m["upto"].rearrange("p (e t) -> p e t", t=NT)[:, :, NT - 1]
                t.matmul(p[0:R, 0:c.E], onesb[0:R, 0:R], total, start=True, stop=True)
                filled(t.matmul(p[0:c.E, 64:65], total, onesb[0:R, 0:1], start=True, stop=True))
                pe.wait_ge(S(q + "counted"), 2)
                for i in range(c.banks):
                    p = use(f"rank{f}", i)
                    n = c.E * NT // c.banks
                    t.matmul(p[0:R, 0:n], ltri[0:R, 0, 0:R], m["members"][:, n * i:n * i + n], start=True, stop=False)
                    filled(t.matmul(p[0:R, 0:n], onesb[0:R, 0:R], m["before"][:, n * i:n * i + n], start=False, stop=True))
                pe.wait_ge(S(q + "counted"), 3)
                p = use(f"ends{f}")
                filled(t.matmul(p[0:c.E, 0:1], ltri[0:c.E, 1, 0:c.E], ncolb[0:c.E, :], start=True, stop=True))
                pe.wait_ge(S(q + "counted"), 4)
                p = use(f"expert{f}")
                filled(t.matmul(p[0:1, 0:TAB], onesb[0:c.E, 0:1], m["pick"][0:c.E, 0:TAB // 2].bitcast(BF16), start=True, stop=True))
                hot_slot, hot_tile, _ = hot_views(f)
                p = use(f"holder{f}")
                groups = c.K * B
                for g in range(groups):
                    pe.wait_ge(S(q + "hot_slot"), g + 1)
                    pe.wait_ge(S(q + "hot_slot_act"), g + 1)
                    pe.wait_ge(S(q + "hot_tile"), g + 1)
                    for j in range(J):
                        last = t.matmul(p[:, 0:TAB], hot_slot[:, g % 2, j], hot_tile[:, g % 2, j],
                                        start=g + j == 0, stop=g == groups - 1 and j == J - 1)
                    if g < groups - 1:
                        last.then_inc(S(q + "hots_used"), 1)
                filled(last)
                gates = m["gates"].rearrange("p (e t) -> p e t", t=NT)
                for b in range(B):
                    p = use(f"cT{f}", b)
                    for j in range(J):
                        last = t.transpose(p[0:c.E, R * j:R * j + R], gates[:, :, J * b + j], ident[0:R, 0:R])
                    filled(last)
                    wait_evac(pe, f"cT{f}", b)
                    p = use(f"bias{f}", b)
                    for j in range(J):
                        last = t.matmul(p[0:R, D * j:D * j + D], cT[0:c.E, R * j:R * j + R], b2[0:c.E, f, :], start=True, stop=True)
                    filled(last)
                wait_evac(pe, f"bias{f}", B - 1)
                if f == 0:
                    attention_weights()
                expert_tensor(pe, c)
                pe.wait_ge(S(q + "res_ready"), c.tiles + 2)
                pe.wait_ge(S(q + "rT_ready"), c.tiles + 4)
                pe.wait_ge(S(q + "hid_dve"), c.tiles + 3)
                pe.wait_ge(S(q + "hid_act"), c.tiles + 3)
                if f == 0:
                    attention_products()


_OUTS = [((8, 500, 128), 'float32')]


def kernel(**inputs):
    import numpy as _np
    import concourse.bacc as _bacc
    from concourse import mybir as _mybir
    from concourse.bass_utils import run_bass_kernel_spmd as _run

    nc = _bacc.Bacc("TRN2", target_bir_lowering=False, num_devices=1)
    arrays, args = {}, {}
    for name in inputs:
        arr = _np.ascontiguousarray(inputs[name])
        arrays[f"in_{name}_dram"] = arr
        args[name] = nc.dram_tensor(f"in_{name}_dram", arr.shape, _mybir.dt.from_np(arr.dtype), kind="ExternalInput").ap()
    shape, dtype = _OUTS[0]
    out = nc.dram_tensor("out_0_dram", shape, _mybir.dt.from_np(_np.dtype(dtype)), kind="ExternalOutput").ap()
    tower_kernel(nc, args, out)
    r = _run(nc, [arrays], core_ids=[0])
    return r.results[0]["out_0_dram"]
```
